# Optimizing a Trainium2 kernel written in Bass

```python
import numpy as np
import jax
import jax.numpy as jnp

def _softmax(x, axis=-1):
    return jax.nn.softmax(x, axis=axis)

def _gelu(x):
    return jax.nn.gelu(x, approximate=True)

def _silu(x):
    return jax.nn.silu(x)

def _sigmoid(x):
    return jax.nn.sigmoid(x)

def _layernorm(x, axis=-1, eps=1e-05):
    m = jnp.mean(x, axis=axis, keepdims=True)
    v = jnp.var(x, axis=axis, keepdims=True)
    return (x - m) / jnp.sqrt(v + eps)

def _scatter_add(tgt, idx, src, axis=0):
    return tgt.at[idx].add(src)

def _segment_sum(src, seg, n):
    return jax.ops.segment_sum(src, seg, n)
kernel_name = 'mk_adaln_d2_jaxref_r8_570005'

def setup_inputs(seed: int=0):
    np.random.seed(seed)
    _w = jnp.asarray

    def _L0_attn_setup():
        import jax, jax.numpy as jnp
        import numpy as np
        B, N, D, DHAT, H = (2, 256, 128, 64, 16)
        F = DHAT // H
        G = D // H

        def _phi(x):
            return jax.nn.elu(x) + 1.0

        def _linear_attention(Q, K, V):
            kv = jnp.cumsum(jnp.einsum('bhtf,bhtg->bhtfg', K, V), axis=2)
            Z = 1.0 / (jnp.einsum('bhtf,bhtf->bht', Q, jnp.cumsum(K, axis=2)) + 1e-06)
            out = jnp.einsum('bhtf,bhtfg->bhtg', Q, kv) * Z[..., None]
            return out
        key = jax.random.key(seed)
        ks = jax.random.split(key, 9)

        def lin_w(k, din, dout):
            return jax.random.normal(k, (din, dout), jnp.float32) / np.sqrt(din).astype(np.float32)
        return {'x': jax.random.normal(ks[0], (B, N, D), jnp.float32), 'wq': lin_w(ks[1], D, DHAT), 'bq': jnp.zeros((DHAT,), jnp.float32), 'wk': lin_w(ks[2], D, DHAT), 'bk': jnp.zeros((DHAT,), jnp.float32), 'wv': lin_w(ks[3], D, D), 'bv': jnp.zeros((D,), jnp.float32), 'wo': lin_w(ks[4], D, D), 'bo': jnp.zeros((D,), jnp.float32)}
    _L0_attn_in = _L0_attn_setup()

    def _L0_ffn_setup():
        import jax, jax.numpy as jnp
        import numpy as np
        B, S, D, F, E, K = (4, 256, 128, 256, 8, 2)
        key = jax.random.key(seed)
        ks = jax.random.split(key, 9)
        sc = 0.02
        return {'hidden_states': jax.random.normal(ks[0], (B, S, D), jnp.float32), 'router_w': jax.random.normal(ks[1], (E, D), jnp.float32) * sc, 'w_gate': jax.random.normal(ks[2], (E, D, F), jnp.float32) * sc, 'w_up': jax.random.normal(ks[3], (E, D, F), jnp.float32) * sc, 'w_down': jax.random.normal(ks[4], (E, F, D), jnp.float32) * sc, 'sw_gate': jax.random.normal(ks[5], (D, F), jnp.float32) * sc, 'sw_up': jax.random.normal(ks[6], (D, F), jnp.float32) * sc, 'sw_down': jax.random.normal(ks[7], (F, D), jnp.float32) * sc, 'gate_w': jax.random.normal(ks[8], (1, D), jnp.float32) * sc}
    _L0_ffn_in = _L0_ffn_setup()
    _L0_c = _w((lambda *s: np.random.randn(*s).astype(np.float32) * 0.05)(4, 128))
    _L0_wmod = _w((lambda *s: np.random.randn(*s).astype(np.float32) * 0.05)(128, 6 * 128) * 128 ** (-0.5))

    def _L1_attn_setup():
        import jax, jax.numpy as jnp
        import numpy as np
        N_HEAD = 16
        FUTURE_DIM = 4

        def _layernorm(x, g, b, eps=1e-05):
            mu = jnp.mean(x, axis=-1, keepdims=True)
            var = jnp.mean(jnp.square(x - mu), axis=-1, keepdims=True)
            return (x - mu) * jax.lax.rsqrt(var + eps) * g + b

        def _future_attn_head(h, W_qkvf, W_conv, W_proj):
            B, T, D = h.shape
            H, hs, F = (N_HEAD, D // N_HEAD, FUTURE_DIM)
            NEG = jnp.float32(-jnp.inf)
            qkvf = h @ W_qkvf.T
            q, k, v, f = jnp.split(qkvf, 4, axis=-1)
            to_h = lambda t: t.reshape(B, T, H, hs).transpose(0, 2, 1, 3)
            q, k, v, f = (to_h(q), to_h(k), to_h(v), to_h(f))
            attn = jnp.einsum('bhtd,bhsd->bhts', q, k) * hs ** (-0.5)
            rows = jnp.arange(T)[:, None]
            causal_mask = jnp.arange(T)[None, :] <= rows
            causal_attn = jnp.where(causal_mask, attn, 0.0)
            padded_causal = jnp.pad(causal_attn, ((0, 0), (0, 0), (0, 0), (0, F)))
            up_future = jnp.einsum('bhtc,cdf->btfhd', f, W_conv).reshape(B, T, F, D)
            k_future = jnp.einsum('btfc,dc->btfd', up_future, W_qkvf[D:2 * D])
            k_future = k_future.reshape(B, T, F, H, hs).transpose(0, 3, 1, 2, 4)
            future_attention = jnp.einsum('bhtd,bhtfd->bhtf', q, k_future)
            cols_f = rows + 1 + jnp.arange(F)[None, :]
            full_attn = padded_causal.at[:, :, rows, cols_f].set(future_attention)
            full_mask = jnp.arange(T + F)[None, :] <= rows + F
            full_attn = jnp.where(full_mask, full_attn, NEG)
            sm = jax.nn.softmax(full_attn, axis=-1)
            sm_causal = jnp.where(causal_mask, sm[..., :T], 0.0)
            unpadded_future = sm[:, :, rows, cols_f]
            v_future = jnp.einsum('btfc,dc->btfd', up_future, W_qkvf[2 * D:3 * D])
            v_future = v_future.reshape(B, T, F, H, hs).transpose(0, 3, 1, 2, 4)
            future_x = jnp.einsum('bhtf,bhtfd->bhtd', unpadded_future, v_future)
            causal_x = jnp.einsum('bhts,bhsd->bhtd', sm_causal, v)
            new_x = (causal_x + future_x).transpose(0, 2, 1, 3).reshape(B, T, D)
            return new_x @ W_proj.T
        key = jax.random.key(seed)
        ks = jax.random.split(key, 7)
        B, T, D, H, F = (2, 128, 128, N_HEAD, FUTURE_DIM)
        hs = D // H
        s = 0.02
        return {'x': jax.random.normal(ks[0], (B, T, D), jnp.float32), 'W_qkvf': jax.random.normal(ks[1], (4 * D, D), jnp.float32) * s, 'W_conv': jax.random.normal(ks[2], (hs, hs, F), jnp.float32) * s, 'W_proj': jax.random.normal(ks[3], (D, D), jnp.float32) * s, 'W_ff1': jax.random.normal(ks[4], (D, 4 * D), jnp.float32) * s, 'W_ff2': jax.random.normal(ks[5], (4 * D, D), jnp.float32) * s, 'ln1_g': jnp.ones((D,), jnp.float32), 'ln1_b': jnp.zeros((D,), jnp.float32), 'ln2_g': jnp.ones((D,), jnp.float32), 'ln2_b': jnp.zeros((D,), jnp.float32)}
    _L1_attn_in = _L1_attn_setup()

    def _L1_ffn_setup():
        import jax, jax.numpy as jnp
        import numpy as np
        D_MODEL = 128
        D1, D2 = (32, 32)
        F1, F2 = (64, 64)
        E = 64
        TOP_K = 2

        def kmoe(x_flat, W_router, A, B, scale, bias, d_in1, d_in2, d_out1, d_out2, top_k):
            logits = x_flat @ W_router.T
            vals, idx = jax.lax.top_k(logits, top_k)
            probs = jax.nn.softmax(vals, axis=-1)
            xs = x_flat.reshape(-1, d_in1, d_in2)
            Ag = A[idx]
            Bg = B[idx]
            Y = jnp.einsum('nkoi,nij,nkpj->nkop', Ag, xs, Bg)
            out = jnp.einsum('nkop,nk->nop', Y, probs).reshape(-1, d_out1 * d_out2)
            return out * scale + bias
        key = jax.random.key(seed)
        ks = jax.random.split(key, 12)
        s = 0.02
        return {'x': jax.random.normal(ks[0], (4, 256, D_MODEL), dtype=jnp.float32), 'W_up': jax.random.normal(ks[1], (E, D1 * D2), dtype=jnp.float32) * s, 'A_up': jax.random.normal(ks[2], (E, F1, D1), dtype=jnp.float32) * s, 'B_up': jax.random.normal(ks[3], (E, F2, D2), dtype=jnp.float32) * s, 'scale_up': jnp.ones((1,), dtype=jnp.float32), 'bias_up': jnp.zeros((F1 * F2,), dtype=jnp.float32), 'W_down': jax.random.normal(ks[4], (E, F1 * F2), dtype=jnp.float32) * s, 'A_down': jax.random.normal(ks[5], (E, D1, F1), dtype=jnp.float32) * s, 'B_down': jax.random.normal(ks[6], (E, D2, F2), dtype=jnp.float32) * s, 'scale_down': jnp.ones((1,), dtype=jnp.float32), 'bias_down': jnp.zeros((D1 * D2,), dtype=jnp.float32)}
    _L1_ffn_in = _L1_ffn_setup()
    _L1_c = _w((lambda *s: np.random.randn(*s).astype(np.float32) * 0.05)(4, 128))
    _L1_wmod = _w((lambda *s: np.random.randn(*s).astype(np.float32) * 0.05)(128, 6 * 128) * 128 ** (-0.5))
    _d = {'L0_attn_x': _L0_attn_in['x'], 'L0_attn_wq': _L0_attn_in['wq'], 'L0_attn_bq': _L0_attn_in['bq'], 'L0_attn_wk': _L0_attn_in['wk'], 'L0_attn_bk': _L0_attn_in['bk'], 'L0_attn_wv': _L0_attn_in['wv'], 'L0_attn_bv': _L0_attn_in['bv'], 'L0_attn_wo': _L0_attn_in['wo'], 'L0_attn_bo': _L0_attn_in['bo'], 'L0_ffn_router_w': _L0_ffn_in['router_w'], 'L0_ffn_w_gate': _L0_ffn_in['w_gate'], 'L0_ffn_w_up': _L0_ffn_in['w_up'], 'L0_ffn_w_down': _L0_ffn_in['w_down'], 'L0_ffn_sw_gate': _L0_ffn_in['sw_gate'], 'L0_ffn_sw_up': _L0_ffn_in['sw_up'], 'L0_ffn_sw_down': _L0_ffn_in['sw_down'], 'L0_ffn_gate_w': _L0_ffn_in['gate_w'], 'L0_c': _L0_c, 'L0_wmod': _L0_wmod, 'L1_attn_W_qkvf': _L1_attn_in['W_qkvf'], 'L1_attn_W_conv': _L1_attn_in['W_conv'], 'L1_attn_W_proj': _L1_attn_in['W_proj'], 'L1_attn_W_ff1': _L1_attn_in['W_ff1'], 'L1_attn_W_ff2': _L1_attn_in['W_ff2'], 'L1_attn_ln1_g': _L1_attn_in['ln1_g'], 'L1_attn_ln1_b': _L1_attn_in['ln1_b'], 'L1_attn_ln2_g': _L1_attn_in['ln2_g'], 'L1_attn_ln2_b': _L1_attn_in['ln2_b'], 'L1_ffn_W_up': _L1_ffn_in['W_up'], 'L1_ffn_A_up': _L1_ffn_in['A_up'], 'L1_ffn_B_up': _L1_ffn_in['B_up'], 'L1_ffn_scale_up': _L1_ffn_in['scale_up'], 'L1_ffn_bias_up': _L1_ffn_in['bias_up'], 'L1_ffn_W_down': _L1_ffn_in['W_down'], 'L1_ffn_A_down': _L1_ffn_in['A_down'], 'L1_ffn_B_down': _L1_ffn_in['B_down'], 'L1_ffn_scale_down': _L1_ffn_in['scale_down'], 'L1_ffn_bias_down': _L1_ffn_in['bias_down'], 'L1_c': _L1_c, 'L1_wmod': _L1_wmod}
    _x0 = _d['L0_attn_x']
    _d['L0_attn_x'] = jax.random.normal(jax.random.fold_in(jax.random.key(seed), 1), (4, 1024, 128), dtype=_x0.dtype)
    del _x0
    return _d

def reference(L0_attn_x, L0_attn_wq, L0_attn_bq, L0_attn_wk, L0_attn_bk, L0_attn_wv, L0_attn_bv, L0_attn_wo, L0_attn_bo, L0_ffn_router_w, L0_ffn_w_gate, L0_ffn_w_up, L0_ffn_w_down, L0_ffn_sw_gate, L0_ffn_sw_up, L0_ffn_sw_down, L0_ffn_gate_w, L0_c, L0_wmod, L1_attn_W_qkvf, L1_attn_W_conv, L1_attn_W_proj, L1_attn_W_ff1, L1_attn_W_ff2, L1_attn_ln1_g, L1_attn_ln1_b, L1_attn_ln2_g, L1_attn_ln2_b, L1_ffn_W_up, L1_ffn_A_up, L1_ffn_B_up, L1_ffn_scale_up, L1_ffn_bias_up, L1_ffn_W_down, L1_ffn_A_down, L1_ffn_B_down, L1_ffn_scale_down, L1_ffn_bias_down, L1_c, L1_wmod):

    def _L0_attn_ref(x, wq, bq, wk, bk, wv, bv, wo, bo):
        import jax, jax.numpy as jnp
        import numpy as np
        B, N, D, DHAT, H = (2, 256, 128, 64, 16)
        F = DHAT // H
        G = D // H

        def _phi(x):
            return jax.nn.elu(x) + 1.0

        def _linear_attention(Q, K, V):
            kv = jnp.cumsum(jnp.einsum('bhtf,bhtg->bhtfg', K, V), axis=2)
            Z = 1.0 / (jnp.einsum('bhtf,bhtf->bht', Q, jnp.cumsum(K, axis=2)) + 1e-06)
            out = jnp.einsum('bhtf,bhtfg->bhtg', Q, kv) * Z[..., None]
            return out
        Bx, Nx, Dx = x.shape
        Q = (x @ wq + bq).reshape(Bx, Nx, H, F).transpose(0, 2, 1, 3)
        K = (x @ wk + bk).reshape(Bx, Nx, H, F).transpose(0, 2, 1, 3)
        V = (x @ wv + bv).reshape(Bx, Nx, H, G).transpose(0, 2, 1, 3)
        Q, K = (_phi(Q), _phi(K))
        out = _linear_attention(Q, K, V)
        out = out.transpose(0, 2, 1, 3).reshape(Bx, Nx, Dx)
        return out @ wo + bo

    def _L0_ffn_ref(hidden_states, router_w, w_gate, w_up, w_down, sw_gate, sw_up, sw_down, gate_w):
        import jax, jax.numpy as jnp
        import numpy as np
        B, S, D, F, E, K = (4, 256, 128, 256, 8, 2)
        bsz, seq_len, d = hidden_states.shape
        x = hidden_states.reshape(-1, d)
        T = x.shape[0]
        n_exp = router_w.shape[0]
        logits = x @ router_w.T
        probs = jax.nn.softmax(logits, axis=-1)
        rw, sel = jax.lax.top_k(probs, K)
        cw = jnp.zeros((T, n_exp), x.dtype).at[jnp.arange(T)[:, None], sel].set(rw)
        g = jnp.einsum('td,edf->etf', x, w_gate)
        u = jnp.einsum('td,edf->etf', x, w_up)
        h = jax.nn.silu(g) * u
        y = jnp.einsum('etf,efd->etd', h, w_down)
        moe_out = jnp.einsum('te,etd->td', cw, y)
        shared = jax.nn.silu(x @ sw_gate) * (x @ sw_up) @ sw_down
        gate = jax.nn.sigmoid(x @ gate_w.T)
        out = moe_out + gate * shared
        return out.reshape(bsz, seq_len, d)

    def _L1_attn_ref(x, W_qkvf, W_conv, W_proj, W_ff1, W_ff2, ln1_g, ln1_b, ln2_g, ln2_b):
        import jax, jax.numpy as jnp
        import numpy as np
        N_HEAD = 16
        FUTURE_DIM = 4

        def _layernorm(x, g, b, eps=1e-05):
            mu = jnp.mean(x, axis=-1, keepdims=True)
            var = jnp.mean(jnp.square(x - mu), axis=-1, keepdims=True)
            return (x - mu) * jax.lax.rsqrt(var + eps) * g + b

        def _future_attn_head(h, W_qkvf, W_conv, W_proj):
            B, T, D = h.shape
            H, hs, F = (N_HEAD, D // N_HEAD, FUTURE_DIM)
            NEG = jnp.float32(-jnp.inf)
            qkvf = h @ W_qkvf.T
            q, k, v, f = jnp.split(qkvf, 4, axis=-1)
            to_h = lambda t: t.reshape(B, T, H, hs).transpose(0, 2, 1, 3)
            q, k, v, f = (to_h(q), to_h(k), to_h(v), to_h(f))
            attn = jnp.einsum('bhtd,bhsd->bhts', q, k) * hs ** (-0.5)
            rows = jnp.arange(T)[:, None]
            causal_mask = jnp.arange(T)[None, :] <= rows
            causal_attn = jnp.where(causal_mask, attn, 0.0)
            padded_causal = jnp.pad(causal_attn, ((0, 0), (0, 0), (0, 0), (0, F)))
            up_future = jnp.einsum('bhtc,cdf->btfhd', f, W_conv).reshape(B, T, F, D)
            k_future = jnp.einsum('btfc,dc->btfd', up_future, W_qkvf[D:2 * D])
            k_future = k_future.reshape(B, T, F, H, hs).transpose(0, 3, 1, 2, 4)
            future_attention = jnp.einsum('bhtd,bhtfd->bhtf', q, k_future)
            cols_f = rows + 1 + jnp.arange(F)[None, :]
            full_attn = padded_causal.at[:, :, rows, cols_f].set(future_attention)
            full_mask = jnp.arange(T + F)[None, :] <= rows + F
            full_attn = jnp.where(full_mask, full_attn, NEG)
            sm = jax.nn.softmax(full_attn, axis=-1)
            sm_causal = jnp.where(causal_mask, sm[..., :T], 0.0)
            unpadded_future = sm[:, :, rows, cols_f]
            v_future = jnp.einsum('btfc,dc->btfd', up_future, W_qkvf[2 * D:3 * D])
            v_future = v_future.reshape(B, T, F, H, hs).transpose(0, 3, 1, 2, 4)
            future_x = jnp.einsum('bhtf,bhtfd->bhtd', unpadded_future, v_future)
            causal_x = jnp.einsum('bhts,bhsd->bhtd', sm_causal, v)
            new_x = (causal_x + future_x).transpose(0, 2, 1, 3).reshape(B, T, D)
            return new_x @ W_proj.T
        x = x + _future_attn_head(_layernorm(x, ln1_g, ln1_b), W_qkvf, W_conv, W_proj)
        h = _layernorm(x, ln2_g, ln2_b)
        x = x + jax.nn.gelu(h @ W_ff1, approximate=False) @ W_ff2
        return x

    def _L1_ffn_ref(x, W_up, A_up, B_up, scale_up, bias_up, W_down, A_down, B_down, scale_down, bias_down):
        import jax, jax.numpy as jnp
        import numpy as np
        D_MODEL = 128
        D1, D2 = (32, 32)
        F1, F2 = (64, 64)
        E = 64
        TOP_K = 2

        def kmoe(x_flat, W_router, A, B, scale, bias, d_in1, d_in2, d_out1, d_out2, top_k):
            logits = x_flat @ W_router.T
            vals, idx = jax.lax.top_k(logits, top_k)
            probs = jax.nn.softmax(vals, axis=-1)
            xs = x_flat.reshape(-1, d_in1, d_in2)
            Ag = A[idx]
            Bg = B[idx]
            Y = jnp.einsum('nkoi,nij,nkpj->nkop', Ag, xs, Bg)
            out = jnp.einsum('nkop,nk->nop', Y, probs).reshape(-1, d_out1 * d_out2)
            return out * scale + bias
        orig_shape = x.shape
        x_flat = x.reshape(-1, D1 * D2)
        h = kmoe(x_flat, W_up, A_up, B_up, scale_up, bias_up, D1, D2, F1, F2, TOP_K)
        h = jax.nn.gelu(h, approximate=False)
        y = kmoe(h, W_down, A_down, B_down, scale_down, bias_down, F1, F2, D1, D2, TOP_K)
        return y.reshape(*orig_shape[:-1], D_MODEL)
    x = L0_attn_x
    mod = (_silu(L0_c) @ L0_wmod).reshape(L0_c.shape[0], 6, 1, -1)
    sa, ca, ga, sb, cb, gb = (mod[:, 0], mod[:, 1], mod[:, 2], mod[:, 3], mod[:, 4], mod[:, 5])
    ga = (2 * (ga >= 0) - 1) * jnp.maximum(jnp.abs(ga), 0.25)
    gb = (2 * (gb >= 0) - 1) * jnp.maximum(jnp.abs(gb), 0.25)
    h = _layernorm(x, axis=-1) * (1 + ca) + sa
    x = x + ga * _L0_attn_ref(h, L0_attn_wq, L0_attn_bq, L0_attn_wk, L0_attn_bk, L0_attn_wv, L0_attn_bv, L0_attn_wo, L0_attn_bo)
    h = _layernorm(x, axis=-1) * (1 + cb) + sb
    x = x + gb * _L0_ffn_ref(h, L0_ffn_router_w, L0_ffn_w_gate, L0_ffn_w_up, L0_ffn_w_down, L0_ffn_sw_gate, L0_ffn_sw_up, L0_ffn_sw_down, L0_ffn_gate_w)
    mod = (_silu(L1_c) @ L1_wmod).reshape(L1_c.shape[0], 6, 1, -1)
    sa, ca, ga, sb, cb, gb = (mod[:, 0], mod[:, 1], mod[:, 2], mod[:, 3], mod[:, 4], mod[:, 5])
    ga = (2 * (ga >= 0) - 1) * jnp.maximum(jnp.abs(ga), 0.25)
    gb = (2 * (gb >= 0) - 1) * jnp.maximum(jnp.abs(gb), 0.25)
    h = _layernorm(x, axis=-1) * (1 + ca) + sa
    x = x + ga * _L1_attn_ref(h, L1_attn_W_qkvf, L1_attn_W_conv, L1_attn_W_proj, L1_attn_W_ff1, L1_attn_W_ff2, L1_attn_ln1_g, L1_attn_ln1_b, L1_attn_ln2_g, L1_attn_ln2_b)
    h = _layernorm(x, axis=-1) * (1 + cb) + sb
    x = x + gb * _L1_ffn_ref(h, L1_ffn_W_up, L1_ffn_A_up, L1_ffn_B_up, L1_ffn_scale_up, L1_ffn_bias_up, L1_ffn_W_down, L1_ffn_A_down, L1_ffn_B_down, L1_ffn_scale_down, L1_ffn_bias_down)
    return x

_drawn_inputs = setup_inputs


def setup_inputs(seed=0):
    import zlib

    import numpy as np

    out = dict(_drawn_inputs(seed))
    spreads = {'L0_attn_bq': (0.0, 2.0),
     'L0_attn_bk': (0.0, 2.0),
     'L0_attn_bv': (0.0, 0.346),
     'L0_attn_bo': (0.0, 0.322),
     'L1_attn_ln1_g': (1.0, 0.6),
     'L1_attn_ln1_b': (0.0, 0.8),
     'L1_attn_ln2_g': (1.0, 0.6),
     'L1_attn_ln2_b': (0.0, 0.8),
     'L1_ffn_bias_up': (0.0, 0.8),
     'L1_ffn_bias_down': (0.0, 0.336)}
    factors = {'L0_attn_wq': 8.0,
     'L0_attn_wk': 5.181,
     'L0_ffn_router_w': 8.0,
     'L0_ffn_w_gate': 8.0,
     'L0_ffn_w_up': 8.0,
     'L0_ffn_w_down': 8.0,
     'L0_ffn_sw_gate': 8.0,
     'L0_ffn_sw_up': 8.0,
     'L0_ffn_sw_down': 8.0,
     'L0_ffn_gate_w': 8.0,
     'L1_attn_W_qkvf': 8.0,
     'L1_attn_W_conv': 8.0,
     'L1_attn_W_proj': 8.0,
     'L1_attn_W_ff1': 4.165,
     'L1_attn_W_ff2': 4.125,
     'L1_ffn_W_up': 8.0,
     'L1_ffn_A_up': 8.0,
     'L1_ffn_B_up': 8.0,
     'L1_ffn_W_down': 8.0,
     'L1_ffn_A_down': 8.0,
     'L1_ffn_B_down': 8.0}
    for name, (base, spread) in spreads.items():
        noise = np.random.default_rng([zlib.crc32(name.encode()), seed]).standard_normal(out[name].shape)
        drawn = base * np.exp(spread * noise) if base else spread * noise
        out[name] = jnp.asarray(drawn.astype(out[name].dtype))
    for name, factor in factors.items():
        out[name] = (out[name] * factor).astype(out[name].dtype)
    return out
```

```python
from contextlib import ExitStack

import numpy as np
import concourse.bass as bass
from concourse import mybir

F32 = mybir.dt.float32
BF16 = mybir.dt.bfloat16
U32 = mybir.dt.uint32
ALU = mybir.AluOpType
ACT = mybir.ActivationFunctionType
X_AXIS = mybir.AxisListType.X

P = 128
D = 128
B, T = 4, 1024
NC = T // P
CH = B * NC
W = B * P
EPS = 1e-5
SHIFT_A, SCALE_A, GATE_A, SHIFT_B, SCALE_B, GATE_B = range(6)

def done(i, per=1, k=0):
    return i * per + k + 2


def before(i, per=1, k=0):
    return i * per + k + 1


def stored(i, per=16):
    return i * per + per


class Mem:

    def __init__(self, nc, ctx):
        self.nc, self.ctx, self.sems = nc, ctx, []

    def sb(self, name, shape, dt=F32):
        return self.ctx.enter_context(self.nc.sbuf_tensor(name, shape, dt))

    def ps(self, name, shape, dt=F32):
        return self.ctx.enter_context(self.nc.psum_tensor(name, shape, dt))

    def sem(self, name):
        handle = self.nc.alloc_semaphore(name=name)
        self.sems.append(handle)
        return handle

    def stage(self, f, *args):
        kept, self.sems = self.sems, []
        f(self.nc, self, *args)
        self.nc.clear_and_free_semaphores(self.sems)
        self.nc.all_engine_barrier()
        self.sems = kept


def at(ap, i):
    return ap[:, :, bass.ds(i, 1), :].rearrange("p a o d -> p a (o d)")


def bcast(ap, shape):
    return ap.broadcast_to(shape)


def setup(nc, m, c, dram):
    loaded, cond_loaded = m.sem("loaded"), m.sem("cond_loaded")
    silu_done, bc_done, masks = m.sem("silu_done"), m.sem("bc_done"), m.sem("masks")
    cols_mm, cols_out = m.sem("cols_mm"), m.sem("cols_out")
    rows_mm, rows_out, fix = m.sem("rows_mm"), m.sem("rows_out"), m.sem("fix")
    loads = [
        (c.WQKV[:, 0:64], dram["L0_attn_wq"]), (c.WQKV[:, 64:128], dram["L0_attn_wk"]),
        (c.WQKV[:, 128:256], dram["L0_attn_wv"]), (c.WO[:, :], dram["L0_attn_wo"]),
        (c.BQKV[:, 0:64], dram["L0_attn_bq"].partition_broadcast(P)),
        (c.BQKV[:, 64:128], dram["L0_attn_bk"].partition_broadcast(P)),
        (c.BQKV[:, 128:256], dram["L0_attn_bv"].partition_broadcast(P)),
        (c.BO[:, :], dram["L0_attn_bo"].partition_broadcast(P)),
        (c.X[:, :, :], dram["L0_attn_x"].rearrange("b (n p) d -> p (b n) d", p=P)),
    ]
    cond = [
        (c.COND[:, 0, :], dram["L0_c"]),
        (c.COND[:, 1, :], dram["L1_c"]),
        (c.WMOD[:, 0, :], dram["L0_wmod"]), (c.WMOD[:, 1, :], dram["L1_wmod"]),
    ]
    ROWS = [(l, b) for l in range(2) for b in range(B)]
    with nc.Block() as block:

        @block.sync
        def _(sp):
            for dst, src in cond:
                sp.dma_start(dst, src).then_inc(cond_loaded, 16)
            for dst, src in loads:
                sp.dma_start(dst, src).then_inc(loaded, 16)
            sp.wait_ge(loaded, 16 * len(loads))

        @block.gpsimd
        def _(pool):
            nc.gpsimd.memset(c.IDENT[:, :], 0.0).then_inc(masks, 1)
            nc.gpsimd.memset(c.ONES[:, :], 1.0).then_inc(masks, 1)
            nc.gpsimd.memset(c.HALF[:, :], -0.5)
            nc.gpsimd.memset(c.EPS[:, :], EPS)
            nc.gpsimd.iota(c.IOTA[:, :], [[1, 8]], base=0, channel_multiplier=0,
                           allow_small_or_imprecise_dtypes=True)
            nc.gpsimd.memset(c.ZERO[:, :], 0.0).then_inc(masks, 1)
            pool.wait_ge(masks, 3)
            nc.gpsimd.affine_select(out=c.IDENT[:, :], in_=c.IDENT[:, :], compare_op=ALU.not_equal,
                                    fill=1.0, base=0, pattern=[[-1, P]], channel_multiplier=1)
            nc.gpsimd.affine_select(out=c.IDENTB[:, :], in_=c.ZERO[:, :], compare_op=ALU.not_equal,
                                    fill=1.0, base=0, pattern=[[-1, P]], channel_multiplier=1)
            nc.gpsimd.affine_select(out=c.UPTO[:, :], in_=c.ONES[:, :], compare_op=ALU.is_ge,
                                    fill=0.0, base=0, pattern=[[1, P]], channel_multiplier=-1)
            nc.gpsimd.affine_select(out=c.LATER[:, :], in_=c.ZERO[:, :], compare_op=ALU.is_ge,
                                    fill=-1e30, base=0, pattern=[[-1, P]],
                                    channel_multiplier=1).then_inc(masks, 1)

        @block.scalar
        def _(act):
            act.wait_ge(cond_loaded, 16 * len(cond))
            nc.scalar.activation(c.COND[:, :, :], c.COND[:, :, :], ACT.Silu).then_inc(silu_done, 1)
            for n, (l, b) in enumerate(ROWS):
                act.wait_ge(rows_mm, n + 1)
                k = 2 * (n % 2)
                nc.scalar.copy(c.MROW[:, l, b, 0:4, :],
                               c.PS[:, k, :].rearrange("p (j d) -> p j d", d=D))
                nc.scalar.copy(c.MROW[:, l, b, 4:6, :],
                               c.PS[:, k + 1, 0:256].rearrange("p (j d) -> p j d", d=D)
                               ).then_inc(rows_out, 1)

        @block.vector
        def _(dve):
            dve.wait_ge(silu_done, 1)
            for n, (l, b) in enumerate(ROWS):
                nc.vector.tensor_copy(c.CB[:, n, :], bcast(c.COND[:, l, b:b + 1], [P, P])
                                      ).then_inc(bc_done, 1)
            dve.wait_ge(cols_mm, 1)
            nc.vector.tensor_copy(c.MCOL[:, :, :, :], c.PS[:, 4, 0:48].rearrange(
                "p (l j b) -> p l j b", l=2, j=6)).then_inc(cols_out, 1)
            dve.wait_ge(cols_out, 1)
            for j in (SCALE_A, SCALE_B):
                nc.vector.tensor_scalar_add(c.MCOL[:, :, j, :], c.MCOL[:, :, j, :], 1.0)
            dve.wait_ge(rows_out, len(ROWS))
            for j in (SCALE_A, SCALE_B):
                nc.vector.tensor_scalar_add(c.MROW[:, :, :, j, :], c.MROW[:, :, :, j, :], 1.0)
            k = 0
            for j in (GATE_A, GATE_B):
                g = c.MROW[:, :, :, j, :].rearrange("p l b d -> p (l b) d")
                nc.vector.tensor_scalar(c.CB[:, :, :], g, 0.0, 2.0, ALU.is_ge, ALU.mult).then_inc(fix, 1)
                nc.vector.tensor_scalar(c.CB2[:, :, :], g, -1.0, None, ALU.mult).then_inc(fix, 1)
                dve.wait_ge(fix, k + 2)
                nc.vector.tensor_scalar_add(c.CB[:, :, :], c.CB[:, :, :], -1.0).then_inc(fix, 1)
                nc.vector.tensor_tensor(c.CB2[:, :, :], c.CB2[:, :, :], g, ALU.max).then_inc(fix, 1)
                dve.wait_ge(fix, k + 4)
                nc.vector.scalar_tensor_tensor(g, c.CB2[:, :, :], 0.25, c.CB[:, :, :], ALU.max,
                                               ALU.mult).then_inc(fix, 1)
                dve.wait_ge(fix, k + 5)
                k += 5

        @block.tensor
        def _(pe):
            pe.wait_ge(silu_done, 1)
            for l in range(2):
                for j in range(6):
                    o = (l * 6 + j) * B
                    last = nc.tensor.matmul(c.PS[:, 4, o:o + B], c.WMOD[:, l, j * D:(j + 1) * D],
                                            c.COND[:, l, :], start=True, stop=True)
            last.then_inc(cols_mm, 1)
            for n, (l, b) in enumerate(ROWS):
                pe.wait_ge(bc_done, n + 1)
                if n >= 2:
                    pe.wait_ge(rows_out, n - 1)
                k = 2 * (n % 2)
                nc.tensor.matmul(c.PS[:, k, :], c.CB[:, n, :], c.WMOD[:, l, 0:512], start=True, stop=True)
                nc.tensor.matmul(c.PS[:, k + 1, 0:256], c.CB[:, n, :], c.WMOD[:, l, 512:768],
                                 start=True, stop=True).then_inc(rows_mm, 1)


def ln_stats(nc, dve, c, s, src, i):
    for b in range(B):
        ins = nc.vector.bn_stats(c.ST[:, b, :], src(b))
    ins.then_inc(s.stats, 1)
    dve.wait_ge(s.stats, done(i))
    dve.sem_inc(c.passed, 1)
    for b in range(B):
        ins = nc.vector.bn_aggr(c.MV[:, b, :], c.ST[:, b, :])
    ins.then_inc(s.moments, 1)


def ln_rstd(nc, pool, c, s, i):
    pool.wait_ge(s.moments, done(i))
    nc.gpsimd.tensor_tensor(c.VE[:, :], c.MV[:, :, 1], c.EPS[:, :], ALU.add).then_inc(s.var_eps, 1)
    pool.wait_ge(s.var_eps, done(i))
    nc.gpsimd.tensor_tensor(c.RSTD[:, :], c.VE[:, :], c.HALF[:, :], ALU.pow).then_inc(s.rstd, 1)


def ln_apply(nc, dve, c, s, src, dst, i):
    dve.wait_ge(s.rstd, done(i))
    for b in range(B):
        ins = nc.vector.tensor_scalar(dst(b), src(b), c.MV[:, b, 0:1], c.RSTD[:, b:b + 1],
                                      ALU.subtract, ALU.mult)
    ins.then_inc(s.normed, 1)


class LnSems:
    def __init__(self, m, tag):
        self.stats, self.moments = m.sem(tag + "_stats"), m.sem(tag + "_moments")
        self.var_eps, self.rstd = m.sem(tag + "_var_eps"), m.sem(tag + "_rstd")
        self.normed = m.sem(tag + "_normed")

    def dve(self):
        return [self.stats, self.moments, self.normed]

    def pool(self):
        return [self.var_eps, self.rstd]


def credit(engine, sems):
    for s in sems:
        engine.sem_inc(s, 1)


def linear_attention(nc, m, c):
    H, F, G = 16, 4, 8
    KV = H * F * G
    ln = LnSems(m, "la")
    turned, h_ready, qkv_mm, qkv_out = (m.sem("la_" + n) for n in ("turned", "h_ready", "qkv_mm", "qkv_out"))
    neg_done, exp_done, phi_done = (m.sem("la_" + n) for n in ("neg", "exp", "phi"))
    kv_dve, kv_pool, cum_mm, sum_done = (m.sem("la_" + n) for n in ("kv_dve", "kv_pool", "cum_mm", "sum"))
    prod_done, red_done, den_done, rec_done, o_done = (
        m.sem("la_" + n) for n in ("prod", "red", "den", "rec", "o"))
    o_turned, o_out, proj_mm, y_done, gated, res_done = (
        m.sem("la_" + n) for n in ("o_turned", "o_out", "proj", "y", "gated", "res"))
    X4 = c.X[:, :, :].rearrange("p (b n) d -> p b n d", b=B)
    PS = c.PS[:, :, :].rearrange("p k n -> p (k n)")

    def kv_product(engine, b):
        k = c.PHI[:, b, 64:128].rearrange("p (h f) -> p h f", f=F).unsqueeze(3)
        v = c.QKV[:, b, 128:256].rearrange("p (h g) -> p h g", g=G).unsqueeze(2)
        return engine.tensor_tensor(c.KVP[:, b, :].rearrange("p (h f g) -> p h f g", h=H, f=F),
                                    bcast(k, [P, H, F, G]), bcast(v, [P, H, F, G]), ALU.mult)

    with nc.Block() as block:

        @block.vector
        def _(dve):
            credit(dve, ln.dve() + [qkv_out, neg_done, phi_done, kv_dve, prod_done, red_done,
                                    den_done, rec_done, o_done, y_done])
            with dve.Fori(0, NC) as i:
                xi = at(X4, i)
                ln_stats(nc, dve, c, ln, lambda b: xi[:, b, :], i)
                ln_apply(nc, dve, c, ln, lambda b: xi[:, b, :], lambda b: c.XN[:, b, :], i)
                dve.wait_ge(qkv_mm, done(i))
                nc.vector.tensor_tensor(c.QKV[:, :, :], PS[:, 512:1536].rearrange("p (b n) -> p b n", b=B),
                                        bcast(c.BQKV[:, :].unsqueeze(1), [P, B, 256]), ALU.add
                                        ).then_inc(qkv_out, 1)
                dve.wait_ge(qkv_out, done(i))
                nc.vector.tensor_scalar(c.NEG[:, :, :], c.QKV[:, :, 0:128], 0.0, None, ALU.min
                                        ).then_inc(neg_done, 1)
                dve.wait_ge(exp_done, done(i))
                nc.vector.scalar_tensor_tensor(c.PHI[:, :, :], c.QKV[:, :, 0:128], 0.0, c.NEG[:, :, :],
                                               ALU.max, ALU.add).then_inc(phi_done, 1)
                dve.wait_ge(phi_done, done(i))
                for b in range(2):
                    last = kv_product(nc.vector, b)
                last.then_inc(kv_dve, 1)
                dve.wait_ge(cum_mm, done(i))
                for b in range(B):
                    q = c.PHI[:, b, 0:64].rearrange("p (h f) -> p h f", f=F).unsqueeze(3)
                    nc.vector.tensor_tensor(
                        c.PROD[:, b, :].rearrange("p (h f g) -> p h f g", h=H, f=F),
                        c.PS[:, 4 + b, :].rearrange("p (h f g) -> p h f g", h=H, f=F),
                        bcast(q, [P, H, F, G]), ALU.mult)
                nc.vector.tensor_tensor(c.KPROD[:, :, :], c.PS[:, 3, 0:256].rearrange("p (b n) -> p b n", b=B),
                                        c.PHI[:, :, 0:64], ALU.mult).then_inc(prod_done, 1)
                dve.wait_ge(prod_done, done(i))
                nc.vector.tensor_reduce(c.DEN[:, :], c.KPROD[:, :, :].rearrange("p b (h f) -> p (b h) f", f=F),
                                        X_AXIS, ALU.add)
                for b in range(B):
                    last = nc.vector.tensor_reduce(
                        c.NUM[:, b, :], c.PROD[:, b, :].rearrange("p (h f g) -> p h g f", h=H, f=F),
                        X_AXIS, ALU.add)
                last.then_inc(red_done, 1)
                dve.wait_ge(red_done, done(i))
                nc.vector.tensor_scalar_add(c.DEN[:, :], c.DEN[:, :], 1e-6).then_inc(den_done, 1)
                dve.wait_ge(den_done, done(i))
                nc.vector.reciprocal(c.REC[:, :], c.DEN[:, :]).then_inc(rec_done, 1)
                dve.wait_ge(rec_done, done(i))
                nc.vector.tensor_tensor(c.O[:, :, :].rearrange("p b (h g) -> p (b h) g", g=G),
                                        c.NUM[:, :, :].rearrange("p b (h g) -> p (b h) g", g=G),
                                        bcast(c.REC[:, :].unsqueeze(2), [P, B * H, G]), ALU.mult
                                        ).then_inc(o_done, 1)
                dve.wait_ge(proj_mm, done(i))
                nc.vector.tensor_tensor(c.Y[:, :, :], c.PS[:, 2, :].rearrange("p (b d) -> p b d", b=B),
                                        bcast(c.BO[:, :].unsqueeze(1), [P, B, D]), ALU.add
                                        ).then_inc(y_done, 1)

        @block.gpsimd
        def _(pool):
            credit(pool, ln.pool() + [kv_pool, gated, res_done])
            nc.gpsimd.memset(c.KVSUM[:, :, :], 0.0)
            nc.gpsimd.memset(c.KSUM[:, :, :], 0.0).then_inc(sum_done, 2)
            with pool.Fori(0, NC) as i:
                ln_rstd(nc, pool, c, ln, i)
                pool.wait_ge(phi_done, done(i))
                for b in range(2, B):
                    last = kv_product(nc.gpsimd, b)
                last.then_inc(kv_pool, 1)
                pool.wait_ge(kv_pool, done(i))
                pool.wait_ge(kv_dve, done(i))
                pool.wait_ge(cum_mm, done(i))
                nc.gpsimd.tensor_tensor(c.KVSUM[:, :, :], c.KVSUM[:, :, :], c.KVP[:, :, :], ALU.add)
                nc.gpsimd.tensor_tensor(c.KSUM[:, :, :], c.KSUM[:, :, :], c.PHI[:, :, 64:128], ALU.add
                                        ).then_inc(sum_done, 1)
                pool.wait_ge(y_done, done(i))
                nc.gpsimd.tensor_tensor(c.Y[:, :, :], c.Y[:, :, :], c.MROW[:, 0, :, GATE_A, :], ALU.mult
                                        ).then_inc(gated, 1)
                pool.wait_ge(gated, done(i))
                xi = at(X4, i)
                nc.gpsimd.tensor_tensor(xi, xi, c.Y[:, :, :], ALU.add).then_inc(res_done, 1)

        @block.scalar
        def _(act):
            credit(act, [h_ready, exp_done, o_out])
            with act.Fori(0, NC) as i:
                act.wait_ge(turned, done(i))
                for b in range(B):
                    last = nc.scalar.activation(c.HT[:, b, :], c.PS[:, 0, b * P:(b + 1) * P], ACT.Identity,
                                                scale=c.MCOL[:, 0, SCALE_A, b:b + 1],
                                                bias=c.MCOL[:, 0, SHIFT_A, b:b + 1])
                last.then_inc(h_ready, 1)
                act.wait_ge(neg_done, done(i))
                nc.scalar.activation(c.NEG[:, :, :], c.NEG[:, :, :], ACT.Exp).then_inc(exp_done, 1)
                act.wait_ge(o_turned, done(i))
                nc.scalar.copy(c.OT[:, :, :], c.PS[:, 1, :].rearrange("p (b t) -> p b t", b=B)
                               ).then_inc(o_out, 1)

        @block.tensor
        def _(pe):
            credit(pe, [turned, qkv_mm, cum_mm, o_turned, proj_mm])
            with pe.Fori(0, NC) as i:
                pe.wait_ge(ln.normed, done(i))
                for b in range(B):
                    last = nc.tensor.transpose(c.PS[:, 0, b * P:(b + 1) * P], c.XN[:, b, :], c.IDENT[:, :])
                last.then_inc(turned, 1)
                pe.wait_ge(h_ready, done(i))
                for b in range(B):
                    last = nc.tensor.matmul(PS[:, 512 + 256 * b:768 + 256 * b], c.HT[:, b, :], c.WQKV[:, :],
                                            start=True, stop=True)
                last.then_inc(qkv_mm, 1)
                pe.wait_ge(phi_done, done(i))
                pe.wait_ge(sum_done, done(i))
                kp = c.PS[:, 3, 0:256]
                nc.tensor.matmul(kp, c.UPTO[:, :], c.PHI[:, :, 64:128], start=True, stop=False)
                nc.tensor.matmul(kp, c.ONES[:, :], c.KSUM[:, :, :], start=False, stop=True)
                pe.wait_ge(kv_dve, done(i))
                pe.wait_ge(kv_pool, done(i))
                for b in range(B):
                    nc.tensor.matmul(c.PS[:, 4 + b, :], c.UPTO[:, :], c.KVP[:, b, :], start=True, stop=False)
                    last = nc.tensor.matmul(c.PS[:, 4 + b, :], c.ONES[:, :], c.KVSUM[:, b, :],
                                            start=False, stop=True)
                last.then_inc(cum_mm, 1)
                pe.wait_ge(o_done, done(i))
                for b in range(B):
                    last = nc.tensor.transpose(c.PS[:, 1, b * P:(b + 1) * P], c.O[:, b, :], c.IDENT[:, :])
                last.then_inc(o_turned, 1)
                pe.wait_ge(o_out, done(i))
                for b in range(B):
                    last = nc.tensor.matmul(c.PS[:, 2, b * P:(b + 1) * P], c.OT[:, b, :], c.WO[:, :],
                                            start=True, stop=True)
                last.then_inc(proj_mm, 1)


NE0, F0 = 8, 256


def load_experts(nc, m, c, dram):
    w = m.sem("experts_loaded")
    return w, [
        (c.WR[:, 0:8], dram["L0_ffn_router_w"]), (c.WR[:, 8:9], dram["L0_ffn_gate_w"]),
        (c.WG[:, 0:NE0, :], dram["L0_ffn_w_gate"].rearrange("e d f -> d e f")),
        (c.WU[:, 0:NE0, :], dram["L0_ffn_w_up"].rearrange("e d f -> d e f")),
        (c.WD[:, 0:NE0, :, :], dram["L0_ffn_w_down"].rearrange("e (k p) d -> p e k d", p=P)),
        (c.WG[:, NE0, :], dram["L0_ffn_sw_gate"]), (c.WU[:, NE0, :], dram["L0_ffn_sw_up"]),
        (c.WD[:, NE0, :, :], dram["L0_ffn_sw_down"].rearrange("(k p) d -> p k d", p=P)),
    ]


def experts(nc, m, c, dram):
    NE = NE0 + 1
    ln = LnSems(m, "ex")
    turned, h_ready, logit_mm, logit_out = (m.sem("ex_" + n) for n in ("turned", "h_ready", "logit_mm", "logit_out"))
    top_done, idx_done, idx_f, shifted, exp_done = (
        m.sem("ex_" + n) for n in ("top", "idx", "idx_f", "shifted", "exp"))
    hot, sum_done, rec_done, cw_done = (m.sem("ex_" + n) for n in ("hot", "sum", "rec", "cw"))
    gate_mm, up_mm, silu_done, mul_done, down_mm, acc_done = (
        m.sem("ex_" + n) for n in ("gate_mm", "up_mm", "silu", "mul", "down_mm", "acc"))
    y_done, res_done = m.sem("ex_y"), m.sem("ex_res")
    X4 = c.X[:, :, :].rearrange("p (b n) d -> p b n d", b=B)
    HT = c.HT[:, :, :].rearrange("p b t -> p (b t)")
    loaded, loads = load_experts(nc, m, c, dram)

    with nc.Block() as block:

        @block.sync
        def _(sp):
            for dst, src in loads:
                sp.dma_start(dst, src).then_inc(loaded, 16)

        @block.vector
        def _(dve):
            credit(dve, ln.dve() + [logit_out, top_done, idx_done, idx_f, shifted, hot, sum_done,
                                    rec_done, cw_done, mul_done, acc_done, y_done])
            with dve.Fori(0, NC) as i:
                xi = at(X4, i)
                ln_stats(nc, dve, c, ln, lambda b: xi[:, b, :], i)
                ln_apply(nc, dve, c, ln, lambda b: xi[:, b, :], lambda b: c.XN[:, b, :], i)
                dve.wait_ge(logit_mm, done(i))
                nc.vector.tensor_copy(c.LG[:, :, :], c.PS[:, 7, 0:64].rearrange("p (b e) -> p b e", b=B)[:, :, 0:9]
                                      ).then_inc(logit_out, 1)
                dve.wait_ge(logit_out, done(i))
                dve.sem_inc(c.passed, 1)
                for b in range(B):
                    last = nc.vector.max(c.TOP[:, b, :], c.LG[:, b, 0:8])
                last.then_inc(top_done, 1)
                dve.wait_ge(top_done, done(i))
                nc.vector.tensor_tensor(c.EX[:, :, 0:8], c.LG[:, :, 0:8], bcast(c.TOP[:, :, 0:1], [P, B, 8]),
                                        ALU.subtract)
                nc.vector.tensor_scalar(c.EX[:, :, 8:9], c.LG[:, :, 8:9], -1.0, None, ALU.mult
                                        ).then_inc(shifted, 1)
                for b in range(B):
                    last = nc.vector.max_index(c.TIX[:, b, :], c.TOP[:, b, :], c.LG[:, b, 0:8])
                last.then_inc(idx_done, 1)
                dve.wait_ge(idx_done, done(i))
                nc.vector.tensor_copy(c.TIF[:, :, :], c.TIX[:, :, 0:2]).then_inc(idx_f, 1)
                dve.wait_ge(idx_f, done(i))
                for k in range(2):
                    last = nc.vector.tensor_tensor(c.HOT[:, k, :, :], bcast(c.IOTA[:, :].unsqueeze(1), [P, B, 8]),
                                                   bcast(c.TIF[:, :, k:k + 1], [P, B, 8]), ALU.is_equal)
                last.then_inc(hot, 1)
                dve.wait_ge(hot, done(i))
                dve.wait_ge(exp_done, done(i))
                nc.vector.tensor_reduce(c.SUM[:, :, 0:1], c.EX[:, :, 0:8], X_AXIS, ALU.add)
                nc.vector.tensor_scalar_add(c.SUM[:, :, 1:2], c.EX[:, :, 8:9], 1.0)
                nc.vector.tensor_tensor(c.HOT[:, 0, :, :], c.HOT[:, 0, :, :], c.HOT[:, 1, :, :], ALU.add
                                        ).then_inc(sum_done, 1)
                dve.wait_ge(sum_done, done(i))
                nc.vector.reciprocal(c.RS[:, :, :], c.SUM[:, :, :])
                nc.vector.tensor_tensor(c.HOT[:, 0, :, :], c.HOT[:, 0, :, :], c.EX[:, :, 0:8], ALU.mult
                                        ).then_inc(rec_done, 1)
                dve.wait_ge(rec_done, done(i))
                nc.vector.tensor_tensor(c.CW[:, :, 0:8], c.HOT[:, 0, :, :], bcast(c.RS[:, :, 0:1], [P, B, 8]),
                                        ALU.mult)
                nc.vector.tensor_copy(c.CW[:, :, 8:9], c.RS[:, :, 1:2]).then_inc(cw_done, 1)

                def accumulate(e):
                    dve.wait_ge(down_mm, done(i, NE, e))
                    if e == 0:
                        dve.wait_ge(cw_done, done(i))
                    else:
                        dve.wait_ge(acc_done, done(i, NE, e - 1))
                    for b in range(B):
                        y = c.PS[:, 6, b * P:(b + 1) * P]
                        if e == 0:
                            last = nc.vector.tensor_scalar(c.Y[:, b, :], y, c.CW[:, b, e:e + 1], None, ALU.mult)
                        else:
                            last = nc.vector.scalar_tensor_tensor(c.Y[:, b, :], y, c.CW[:, b, e:e + 1],
                                                                  c.Y[:, b, :], ALU.mult, ALU.add)
                    last.then_inc(acc_done, 1)

                for e in range(NE):
                    dve.wait_ge(silu_done, done(i, NE, e))
                    dve.wait_ge(up_mm, done(i, NE, e))
                    nc.vector.tensor_tensor(c.HH[:, e % 2, :, :], c.PS[:, 4:6, :], c.SG[:, e % 2, :, :],
                                            ALU.mult).then_inc(mul_done, 1)
                    if e >= 1:
                        accumulate(e - 1)
                accumulate(NE - 1)
                dve.wait_ge(acc_done, done(i, NE, NE - 1))
                nc.vector.tensor_tensor(c.Y[:, :, :], c.Y[:, :, :], c.MROW[:, 0, :, GATE_B, :], ALU.mult
                                        ).then_inc(y_done, 1)
                dve.wait_ge(y_done, done(i))
                nc.vector.tensor_tensor(xi, xi, c.Y[:, :, :], ALU.add)

        @block.gpsimd
        def _(pool):
            credit(pool, ln.pool())
            with pool.Fori(0, NC) as i:
                ln_rstd(nc, pool, c, ln, i)

        @block.scalar
        def _(act):
            credit(act, [h_ready, exp_done, silu_done])
            with act.Fori(0, NC) as i:
                act.wait_ge(turned, done(i))
                for b in range(B):
                    last = nc.scalar.activation(c.HT[:, b, :], c.PS[:, 6, b * P:(b + 1) * P], ACT.Identity,
                                                scale=c.MCOL[:, 0, SCALE_B, b:b + 1],
                                                bias=c.MCOL[:, 0, SHIFT_B, b:b + 1])
                last.then_inc(h_ready, 1)
                act.wait_ge(shifted, done(i))
                nc.scalar.activation(c.EX[:, :, :], c.EX[:, :, :], ACT.Exp).then_inc(exp_done, 1)
                for e in range(NE):
                    act.wait_ge(gate_mm, done(i, NE, e))
                    k = 2 * (e % 2)
                    if e >= 2:
                        act.wait_ge(mul_done, done(i, NE, e - 2))
                    nc.scalar.activation(c.SG[:, e % 2, :, :], c.PS[:, k:k + 2, :], ACT.Silu
                                         ).then_inc(silu_done, 1)

        @block.tensor
        def _(pe):
            credit(pe, [turned, logit_mm, gate_mm, up_mm, down_mm])
            pe.wait_ge(loaded, 16 * len(loads))
            with pe.Fori(0, NC) as i:
                pe.wait_ge(ln.normed, done(i))
                for b in range(B):
                    last = nc.tensor.transpose(c.PS[:, 6, b * P:(b + 1) * P], c.XN[:, b, :], c.IDENT[:, :])
                last.then_inc(turned, 1)
                pe.wait_ge(h_ready, done(i))
                for b in range(B):
                    last = nc.tensor.matmul(c.PS[:, 7, 16 * b:16 * b + 9], c.HT[:, b, :], c.WR[:, :],
                                            start=True, stop=True)
                last.then_inc(logit_mm, 1)

                def down(e):
                    pe.wait_ge(mul_done, done(i, NE, e))
                    if e:
                        pe.wait_ge(acc_done, done(i, NE, e - 1))
                    for b in range(B):
                        for k in range(2):
                            last = nc.tensor.matmul(c.PS[:, 6, b * P:(b + 1) * P],
                                                    c.HH[:, e % 2, k, b * P:(b + 1) * P], c.WD[:, e, k, :],
                                                    start=(k == 0), stop=(k == 1))
                    last.then_inc(down_mm, 1)

                for e in range(NE):
                    if e >= 2:
                        pe.wait_ge(silu_done, done(i, NE, e - 2))
                    for k in range(2):
                        last = nc.tensor.matmul(c.PS[:, 2 * (e % 2) + k, :], c.WG[:, e, k * P:(k + 1) * P], HT,
                                                start=True, stop=True)
                    last.then_inc(gate_mm, 1)
                    if e >= 1:
                        pe.wait_ge(mul_done, done(i, NE, e - 1))
                    for k in range(2):
                        last = nc.tensor.matmul(c.PS[:, 4 + k, :], c.WU[:, e, k * P:(k + 1) * P], HT,
                                                start=True, stop=True)
                    last.then_inc(up_mm, 1)
                    if e >= 1:
                        down(e - 1)
                down(NE - 1)


H1, HS, NF = 16, 8, 4
GH = 4
NG = H1 // GH
ROW_Q = (0, 0, 1, 1, 0, 2)
ROW_K = (0, 1, 0, 1, 2, 0)
NT = len(ROW_Q)
NS = 3
KM = 96
KA = KM + NS


def attention_inputs(nc, m, c, dram, scratch):
    lx, lh = LnSems(m, "ax"), LnSems(m, "ah")
    loaded, mask_done, bd_done = m.sem("ai_loaded"), m.sem("ai_mask"), m.sem("ai_bd")
    g_mm, g_out, big_mm, big_out = (m.sem("ai_" + n) for n in ("g_mm", "g_out", "big_mm", "big_out"))
    scaled, h_done, h_stored = m.sem("ai_scaled"), m.sem("ai_h"), m.sem("ai_h_stored")
    turned, z_ready, qk_mm, qk_out = (m.sem("ai_" + n) for n in ("turned", "z", "qk_mm", "qk_out"))
    rest1, part2, part3, parts_stored = (m.sem("ai_" + n) for n in ("rest1", "part2", "part3", "parts_stored"))
    tok_mm, qv_out, vf_out, vf_stored = (m.sem("ai_" + n) for n in ("tok_mm", "qv_out", "vf_out", "vf_stored"))
    prod_done, logit_done, v_kept, fmax_done = (m.sem("ai_" + n) for n in ("prod", "logit", "v_kept", "fmax"))
    X4 = c.X[:, :, :].rearrange("p (b n) d -> p b n d", b=B)
    V4 = c.VT[:, :, :].rearrange("p (b n) d -> p b n d", b=B)
    F4 = c.FUT[:, :, :].rearrange("p (b n) d -> p b n d", b=B)
    M4 = c.FMAX[:, :, :].rearrange("p (b n) d -> p b n d", b=B)
    ZT = c.HT[:, :, :].rearrange("p b t -> p (b t)")
    BANKS = ((3, 4, 5), (6, 7, 0))
    conv = dram["L1_attn_W_conv"]
    loads = [(c.WT[:, :], dram["L1_attn_W_qkvf_T"]), (c.WF[:, :], dram["L1_attn_W_qkvf"][3 * D:4 * D, :]),
             (c.LNG[:, 0:1], dram["L1_attn_ln1_g"].rearrange("(d o) -> d o", o=1)),
             (c.LNG[:, 1:2], dram["L1_attn_ln1_b"].rearrange("(d o) -> d o", o=1)),
             (c.LNG[:, 2:3], dram["L1_attn_ln2_g"].rearrange("(d o) -> d o", o=1)),
             (c.LNG[:, 3:4], dram["L1_attn_ln2_b"].rearrange("(d o) -> d o", o=1))]
    loads += [(c.CV[HS * h:HS * h + HS, :, :], conv) for h in range(H1)]

    with nc.Block() as block:

        @block.sync
        def _(sp):
            for dst, src in loads:
                sp.dma_start(dst, src).then_inc(loaded, 16)
            for s in (h_stored, parts_stored, vf_stored):
                sp.sem_inc(s, 16)
            with sp.Fori(0, NC) as i:
                sp.wait_ge(h_done, done(i))
                sp.dma_start(scratch.h[:, bass.ds(i, 1), :, :].rearrange("b o p d -> p b (o d)"), c.H[:, :, :]
                             ).then_inc(h_stored, 16)
                sp.wait_ge(part3, done(i))
                sp.dma_start(scratch.qk[:, :, bass.ds(i * P, P)], c.PARTS[:, :, :]).then_inc(parts_stored, 16)
                sp.wait_ge(vf_out, done(i, B, B - 1))
                sp.dma_start(scratch.vf[:, bass.ds(i, 1), :, :].rearrange("b o p n -> p b (o n)"), c.VF[:, :, :]
                             ).then_inc(vf_stored, 16)
            sp.wait_ge(h_stored, 16 * NC + 16)
            sp.wait_ge(parts_stored, 16 * NC + 16)
            sp.wait_ge(vf_stored, 16 * NC + 16)

        @block.vector
        def _(dve):
            credit(dve, lx.dve() + lh.dve() + [scaled, h_done, rest1, prod_done, logit_done, fmax_done])
            dve.wait_ge(loaded, 16 * len(loads))
            dve.wait_ge(mask_done, 3)
            for f in range(NF):
                last = nc.vector.tensor_tensor(
                    c.BD[:, f, :].rearrange("p (h c) -> p h c", c=HS),
                    bcast(c.CV[:, f, :].unsqueeze(1), [P, H1, HS]),
                    c.BLOCKS[:, :].rearrange("p (h c) -> p h c", c=HS), ALU.mult)
            last.then_inc(bd_done, 1)
            dve.wait_ge(g_mm, 1)
            nc.vector.tensor_copy(c.GK[:, :, :], c.PS[:, 0:2, :].rearrange("p k (f n) -> p (k f) n", n=256)
                                  ).then_inc(g_out, 1)
            dve.wait_ge(big_mm, 1)
            nc.vector.tensor_copy(c.BIG[:, :, :], c.PS[:, 2:4, :].rearrange("p k (f n) -> p (k f) n", n=256)
                                  ).then_inc(big_out, 1)
            with dve.Fori(0, NC) as i:
                xi = at(X4, i)
                ln_stats(nc, dve, c, lx, lambda b: xi[:, b, :], i)
                ln_apply(nc, dve, c, lx, lambda b: xi[:, b, :], lambda b: c.XN[:, b, :], i)
                dve.wait_ge(lx.normed, done(i))
                nc.vector.tensor_tensor(c.Y[:, :, :], c.XN[:, :, :], c.MROW[:, 1, :, SCALE_A, :], ALU.mult
                                        ).then_inc(scaled, 1)
                dve.wait_ge(scaled, done(i))
                dve.wait_ge(h_stored, stored(i))
                nc.vector.tensor_tensor(c.H[:, :, :], c.Y[:, :, :], c.MROW[:, 1, :, SHIFT_A, :], ALU.add
                                        ).then_inc(h_done, 1)
                dve.wait_ge(h_done, done(i))
                ln_stats(nc, dve, c, lh, lambda b: c.H[:, b, :], i)
                ln_apply(nc, dve, c, lh, lambda b: c.H[:, b, :], lambda b: c.O[:, b, :], i)
                dve.wait_ge(qk_out, done(i))
                nc.vector.tensor_tensor(c.QKF[:, :, :], c.QKF[:, :, :], c.PARTS[:, 0:8, :], ALU.subtract
                                        ).then_inc(rest1, 1)
                for b in range(B):
                    dve.wait_ge(tok_mm, done(i, B, b))
                    dve.wait_ge(qv_out, done(i, B, b))
                    q = c.QV[:, b, 0:D].unsqueeze(1)
                    nc.vector.tensor_tensor(c.FP[:, b, :, :], c.PS[:, BANKS[b % 2][1], :].rearrange(
                        "p (f n) -> p f n", f=NF), bcast(q, [P, NF, D]), ALU.mult).then_inc(prod_done, 1)
                dve.wait_ge(prod_done, done(i, B, B - 1))
                fi = at(F4, i)
                for b in range(B):
                    last = nc.vector.tensor_reduce(fi[:, b, :], c.FP[:, b, :, :].rearrange(
                        "p f (h d) -> p (f h) d", d=HS), X_AXIS, ALU.add)
                last.then_inc(logit_done, 1)
                dve.wait_ge(logit_done, done(i))
                mi = at(M4, i)
                for b in range(B):
                    last = nc.vector.tensor_reduce(mi[:, b, :], fi[:, b, :].rearrange("p (f h) -> p h f", f=NF),
                                                   X_AXIS, ALU.max)
                last.then_inc(fmax_done, 1)

        @block.gpsimd
        def _(pool):
            credit(pool, lx.pool() + lh.pool() + [part2, part3, v_kept])
            nc.gpsimd.memset(c.BLOCKS[:, :], 1.0).then_inc(mask_done, 1)
            blocks = c.BLOCKS[:, :].rearrange("p (h c) -> p h c", c=HS)
            for n, (base, step, mult) in enumerate(((0, -HS, 1), (HS - 1, HS, -1))):
                pool.wait_ge(mask_done, n + 1)
                nc.gpsimd.affine_select(out=blocks, in_=blocks, compare_op=ALU.is_ge, fill=0.0, base=base,
                                        pattern=[[step, H1], [0, HS]], channel_multiplier=mult
                                        ).then_inc(mask_done, 1)
            with pool.Fori(0, NC) as i:
                ln_rstd(nc, pool, c, lx, i)
                ln_rstd(nc, pool, c, lh, i)
                pool.wait_ge(rest1, done(i))
                pool.sem_inc(c.passed, 1)
                nc.gpsimd.tensor_copy(c.PARTS[:, 8:16, :], c.QKF[:, :, :]).then_inc(part2, 1)
                pool.wait_ge(part2, done(i))
                nc.gpsimd.tensor_tensor(c.PARTS[:, 16:24, :], c.QKF[:, :, :], c.PARTS[:, 8:16, :], ALU.subtract
                                        ).then_inc(part3, 1)
                pool.wait_ge(qv_out, done(i, B, B - 1))
                pool.sem_inc(c.passed, 1)
                nc.gpsimd.tensor_copy(at(V4, i), c.QV[:, :, D:2 * D]).then_inc(v_kept, 1)

        @block.scalar
        def _(act):
            credit(act, [z_ready, qk_out, qv_out, vf_out])
            act.wait_ge(loaded, 16 * len(loads))
            with act.Fori(0, NC) as i:
                act.wait_ge(turned, done(i))
                nc.scalar.activation(ZT, c.PS[:, 0, :], ACT.Identity, scale=c.LNG[:, 0:1], bias=c.LNG[:, 1:2]
                                     ).then_inc(z_ready, 1)
                act.wait_ge(qk_mm, done(i))
                act.wait_ge(parts_stored, stored(i))
                for n, scale in enumerate((HS ** -0.5, 1.0)):
                    flat = c.QKF[:, 4 * n:4 * n + 4, :].rearrange("p b t -> p (b t)")
                    part = c.PARTS[:, 4 * n:4 * n + 4, :].rearrange("p b t -> p (b t)")
                    nc.scalar.mul(flat, c.PS[:, 1 + n, :], scale)
                    last = nc.scalar.mul(part, c.PS[:, 1 + n, :], scale)
                last.then_inc(qk_out, 1)
                act.wait_ge(vf_stored, stored(i))
                act.wait_ge(v_kept, before(i))
                for b in range(B):
                    act.wait_ge(tok_mm, done(i, B, b))
                    bank = BANKS[b % 2]
                    nc.scalar.copy(c.QV[:, b, :], c.PS[:, bank[0], 0:2 * D]).then_inc(qv_out, 1)
                    nc.scalar.copy(c.VF[:, b, :], c.PS[:, bank[2], :]).then_inc(vf_out, 1)

        @block.tensor
        def _(pe):
            credit(pe, [turned, qk_mm, tok_mm])
            pe.wait_ge(bd_done, 1)
            for f in range(NF):
                last = nc.tensor.matmul(c.PS[:, f // 2, 256 * (f % 2):256 * (f % 2) + 256], c.BD[:, f, :],
                                        c.WT[:, D:3 * D], start=True, stop=True)
            last.then_inc(g_mm, 1)
            pe.wait_ge(g_out, 1)
            for f in range(NF):
                last = nc.tensor.matmul(c.PS[:, 2 + f // 2, 256 * (f % 2):256 * (f % 2) + 256], c.WF[:, :],
                                        c.GK[:, f, :], start=True, stop=True)
            last.then_inc(big_mm, 1)
            pe.wait_ge(big_out, 1)
            with pe.Fori(0, NC) as i:
                pe.wait_ge(lh.normed, done(i))
                pe.wait_ge(vf_out, before(i, B, 0))
                for b in range(B):
                    last = nc.tensor.transpose(c.PS[:, 0, b * P:(b + 1) * P], c.O[:, b, :], c.IDENT[:, :])
                last.then_inc(turned, 1)
                pe.wait_ge(z_ready, done(i))
                for n in range(2):
                    last = nc.tensor.matmul(c.PS[:, 1 + n, :], c.WT[:, n * D:(n + 1) * D], ZT, start=True, stop=True)
                last.then_inc(qk_mm, 1)
                for b in range(B):
                    bank = BANKS[b % 2]
                    if b >= 2:
                        pe.wait_ge(vf_out, done(i, B, b - 2))
                        pe.wait_ge(prod_done, done(i, B, b - 2))
                    else:
                        pe.wait_ge(prod_done, before(i, B, 0))
                    zb = c.HT[:, b, :]
                    nc.tensor.matmul(c.PS[:, bank[0], 0:D], zb, c.WT[:, 0:D], start=True, stop=True)
                    nc.tensor.matmul(c.PS[:, bank[0], D:2 * D], zb, c.WT[:, 2 * D:3 * D], start=True, stop=True)
                    nc.tensor.matmul(c.PS[:, bank[1], :], zb, c.BIG[:, :, 0:D], start=True, stop=True)
                    nc.tensor.matmul(c.PS[:, bank[2], :], zb, c.BIG[:, :, D:2 * D], start=True, stop=True
                                     ).then_inc(tok_mm, 1)


HALVES, HB = 2, 4
UNITS = [(half, s) for half in range(HALVES) for s in range(HB * (half + 1))]
MAX_UNITS = [(t, half, h) for t in range(NC) for half in range(t // HB + 1) for h in range(GH)]


def attention(nc, m, c, scratch):
    NU, NM = len(UNITS), len(MAX_UNITS)
    tiles_set, v_laid = m.sem("at_tiles_set"), m.sem("at_v_laid")
    qk_loaded = [m.sem(f"at_qk_loaded{g}") for g in range(NG)]
    max_mm, max_taken, top_done, shift_done = (m.sem("at_" + n) for n in ("max_mm", "max_taken", "top", "shift"))
    shift_t, neg_done, n1, r1, n2, r2 = (m.sem("at_" + n) for n in ("shift_t", "neg", "n1", "r1", "n2", "r2"))
    shift_rows = m.sem("at_shift_rows")
    score_mm, exp_done, masked, value_mm = (m.sem("at_" + n) for n in ("score_mm", "exp", "masked", "value_mm"))
    of_out, of_t, nd_out = m.sem("at_of_out"), m.sem("at_of_t"), m.sem("at_nd_out")
    C4 = lambda t, b: t[:, bass.ds(b * NC, NC), :]
    LOADS = 2 * NT
    serial = lambda b, g, u, p=0: ((b * NG + g) * NU + u) * 2 + p
    scored = lambda n: n + 1 + NG * NU * 2
    exped = lambda n: n + 3
    valued = lambda b, g, u: (b * NG + g) * NU + u + 1 + 2 * NU

    def width(half, s):
        first = max(s - HB * half, 0)
        return (HB - first) * P, (HB * half + first) * P

    with nc.Block() as block:

        @block.sync
        def _(sp):
            sp.wait_ge(tiles_set, 4)

            def load(b, g):
                sp.wait_ge(score_mm, (b * NG + g + 1) * (2 * NU))
                for tile, qk, rows in ((c.QS, 0, ROW_Q), (c.KS, 1, ROW_K)):
                    for r, part in enumerate(rows):
                        src = scratch.qk[GH * g * HS:GH * (g + 1) * HS,
                                         bass.ds(b + (part * 2 + qk) * B, 1), :].rearrange(
                            "(h d) o t -> d h (o t)", d=HS)
                        sp.dma_start(tile[r * HS:(r + 1) * HS, g, :, :], src).then_inc(qk_loaded[g], 16)

            def shift(b, g):
                sp.wait_ge(r2, done(b, NG, g))
                for n in range(NS):
                    dst = c.QS[KM + n:KM + n + 1, g, :, :].rearrange("o h t -> o (h t)")
                    sp.dma_start(dst, c.NEGM[:, g % 2, n, :]).then_inc(shift_rows, 16)

            with sp.Fori(0, B) as b:
                load(b, 0)
                load(b, 1)
                shift(b, 0)
                load(b, 2)
                shift(b, 1)
                load(b, 3)
                shift(b, 2)
                shift(b, 3)
            sp.wait_ge(shift_rows, 16 * NS * B * NG)

        @block.vector
        def _(dve):
            nc.vector.memset(c.KS[KM:P, :, :, :], 1.0).then_inc(tiles_set, 1)
            nc.vector.memset(c.QS[:, :, :, :], 0.0).then_inc(tiles_set, 1)
            nc.vector.memset(c.MP[:, :, :, :], -1e30).then_inc(max_taken, 2)
            credit(dve, [top_done, shift_done, neg_done, n1, r1, n2, r2])

            def group(b, g):
                for u, (t, half, h) in enumerate(MAX_UNITS):
                    w = min(512, (t + 1) * P - 512 * half)
                    dve.wait_ge(max_mm, (b * NG + g) * NM + u + 1)
                    nc.vector.reduce_max(c.MP[:, t, half, h:h + 1], c.PS[:, 4 + u % 2, 0:w], X_AXIS
                                         ).then_inc(max_taken, 1)
                dve.wait_ge(max_taken, (b * NG + g + 1) * NM + 2)
                nc.vector.tensor_tensor(c.MX[:, :, :], c.MP[:, :, 0, :], c.MP[:, :, 1, :], ALU.max
                                        ).then_inc(top_done, 1)
                dve.wait_ge(top_done, done(b, NG, g))
                for dst in (C4(c.SHIFT, b)[:, :, GH * g:GH * g + GH], c.MG[:, :, :].rearrange("p h n -> p n h")):
                    last = nc.vector.tensor_tensor(dst, c.MX[:, :, :], C4(c.FMAX, b)[:, :, GH * g:GH * g + GH],
                                                   ALU.max)
                last.then_inc(shift_done, 1)
                dve.wait_ge(shift_t, done(b, NG, g))
                nc.vector.tensor_scalar(c.SH[:, 0, :], c.PS[0:NC * GH, 7, 0:P], -1.0, None, ALU.mult
                                        ).then_inc(neg_done, 1)
                dve.wait_ge(neg_done, done(b, NG, g))
                parts = c.NEGM[:, g % 2, :, :]
                nc.vector.tensor_copy(parts[:, 0, :], c.SH[:, 0, :]).then_inc(n1, 1)
                dve.wait_ge(n1, done(b, NG, g))
                nc.vector.tensor_tensor(c.SH[:, 1, :], c.SH[:, 0, :], parts[:, 0, :], ALU.subtract).then_inc(r1, 1)
                dve.wait_ge(r1, done(b, NG, g))
                nc.vector.tensor_copy(parts[:, 1, :], c.SH[:, 1, :]).then_inc(n2, 1)
                dve.wait_ge(n2, done(b, NG, g))
                nc.vector.tensor_tensor(parts[:, 2, :], c.SH[:, 1, :], parts[:, 1, :], ALU.subtract).then_inc(r2, 1)

            with dve.Fori(0, B) as b:
                for g in range(NG):
                    group(b, g)

        @block.gpsimd
        def _(pool):
            nc.gpsimd.memset(c.KS[0:KM, :, :, :], 0.0).then_inc(tiles_set, 1)
            nc.gpsimd.memset(c.VG[:, :, :, :, :], 0.0).then_inc(tiles_set, 1)
            pool.wait_ge(tiles_set, 4)
            nc.gpsimd.memset(c.VG[:, :, :, :, HS:HS + 1], 1.0)
            credit(pool, [v_laid, masked])
            with pool.Fori(0, B) as b:
                for g in range(NG):
                    pool.wait_ge(value_mm, (b * NG + g + 1) * NU)
                    v = C4(c.VT, b)[:, :, GH * HS * g:GH * HS * (g + 1)].rearrange("p n (h d) -> p n h d", d=HS)
                    pool.sem_inc(c.passed, 1)
                    for h in range(GH):
                        last = nc.gpsimd.tensor_copy(c.VG[:, g % 2, :, h, 0:HS], v[:, :, h, :])
                    last.then_inc(v_laid, 1)
                    for u, (half, s) in enumerate(UNITS):
                        if s < HB * half:
                            continue
                        for p in range(2):
                            pool.wait_ge(exp_done, exped(serial(b, g, u, p)))
                            pool.sem_inc(c.passed, 1)
                            diagonal = c.PT[:, u % 2, p, :, 0:P]
                            nc.gpsimd.affine_select(out=diagonal, in_=diagonal, compare_op=ALU.is_ge, fill=0.0,
                                                    base=0, pattern=[[0, 2], [1, P]], channel_multiplier=-1
                                                    ).then_inc(masked, 1)

        @block.scalar
        def _(act):
            credit(act, [exp_done, exp_done, of_out, nd_out])

            def sums_out(b, g, half):
                n = (b * NG + g) * 2 + half
                act.wait_ge(value_mm, valued(b, g, (3, 11)[half]))
                act.wait_ge(of_t, n + 1)
                nc.scalar.copy(c.OF[:, :], c.PS[:, 6, :]).then_inc(of_out, 1)

            def sums_kept(b, g, half):
                act.wait_ge(of_t, (b * NG + g) * 2 + half + 2)
                nd = c.ND[:, bass.ds(b * NC + HB * half, HB), GH * g:GH * g + GH, :]
                src = c.PS[:, 7, :].rearrange("p (n h r) -> p n h r", n=HB, h=GH)
                for h in range(GH):
                    last = nc.scalar.copy(nd[:, :, h, :], src[:, :, h, 0:HS + 1])
                last.then_inc(nd_out, 1)

            with act.Fori(0, B) as b:
                for g in range(NG):
                    for u, (half, s) in enumerate(UNITS):
                        w, _ = width(half, s)
                        for p in range(2):
                            act.wait_ge(score_mm, scored(serial(b, g, u, p)))
                            act.wait_ge(value_mm, valued(b, g, u - 2))
                            nc.scalar.activation(c.PT[:, u % 2, p, :, 0:w], c.PS[:, 2 * p:2 * p + 2, 0:w],
                                                 ACT.Exp).then_inc(exp_done, 1)
                        if u == 4:
                            sums_out(b, g, 0)
                        if u == 6:
                            sums_kept(b, g, 0)
                    sums_out(b, g, 1)
                    sums_kept(b, g, 1)

        @block.tensor
        def _(pe):
            credit(pe, [shift_t, of_t])
            pe.sem_inc(score_mm, NG * NU * 2)
            pe.sem_inc(value_mm, 2 * NU)

            def maxima(b, g, units):
                for u in units:
                    t, half, h = MAX_UNITS[u]
                    w = min(512, (t + 1) * P - 512 * half)
                    if u == 0:
                        pe.wait_ge(qk_loaded[g], b * (16 * LOADS) + 16 * LOADS)
                    pe.wait_ge(max_taken, (b * NG + g) * NM + u + 1)
                    diagonal = half == t // HB
                    last = nc.tensor.matmul(c.PS[:, 4 + u % 2, 0:w], c.QS[0:KM, g, h, t * P:(t + 1) * P],
                                            c.KS[0:KM, g, h, 512 * half:512 * half + w],
                                            start=True, stop=not diagonal)
                    if diagonal:
                        last = nc.tensor.matmul(c.PS[:, 4 + u % 2, w - P:w], c.IDENTB[:, :], c.LATER[:, :],
                                                start=False, stop=True)
                    last.then_inc(max_mm, 1)

            def turn_shift(b, g):
                pe.wait_ge(shift_done, done(b, NG, g))
                pe.wait_ge(nd_out, (b * NG + g) * 2 + 1)
                nc.tensor.transpose(c.PS[0:NC * GH, 7, 0:P], c.MG[:, :, :].rearrange("p h n -> p (h n)"),
                                    c.IDENT[:, :]).then_inc(shift_t, 1)

            def values(b, g, u):
                half, s = UNITS[u]
                w, first = width(half, s)
                gn = b * NG + g
                pe.wait_ge(exp_done, exped(serial(b, g, u, 1)))
                if s >= HB * half:
                    seen = sum(1 for q in UNITS[:u + 1] if q[1] >= HB * q[0])
                    pe.wait_ge(masked, gn * (2 * NC) + (2 * seen + 1))
                if u == 0:
                    pe.wait_ge(v_laid, done(b, NG, g))
                if s == 0:
                    pe.wait_ge(of_out, gn * 2 + (half + 1))
                o = first - 512 * half
                for h in range(GH):
                    last = nc.tensor.matmul(c.PS[32 * h:32 * h + 32, 6, o:o + w], c.VG[:, g % 2, s, h, :],
                                            c.PT[:, u % 2, h // 2, h % 2, 0:w],
                                            start=(s == 0), stop=(s == HB * (half + 1) - 1))
                last.then_inc(value_mm, 1)

            def turn_sums(b, g, half):
                gn = b * NG + g
                pe.wait_ge(of_out, gn * 2 + (half + 2))
                pe.wait_ge(neg_done, done(b, NG, g))
                pe.wait_ge(nd_out, gn * 2 + (half + 1))
                for n in range(HB):
                    last = nc.tensor.transpose(c.PS[:, 7, n * P:(n + 1) * P], c.OF[:, n * P:(n + 1) * P],
                                               c.IDENT[:, :])
                last.then_inc(of_t, 1)

            with pe.Fori(0, B) as b:
                maxima(b, 0, range(NM))
                turn_shift(b, 0)
                for g in range(NG):
                    pe.wait_ge(shift_rows, (b * NG + g + 1) * (16 * NS))
                    for u, (half, s) in enumerate(UNITS):
                        w, first = width(half, s)
                        for p in range(2):
                            pe.wait_ge(exp_done, exped(serial(b, g, u - 1, p)))
                            for k in range(2):
                                h = 2 * p + k
                                last = nc.tensor.matmul(c.PS[:, h, 0:w], c.KS[0:KA, g, h, s * P:(s + 1) * P],
                                                        c.QS[0:KA, g, h, first:first + w], start=True, stop=True)
                            last.then_inc(score_mm, 1)
                            if g + 1 < NG:
                                at_once = NM // (2 * NU)
                                k = (2 * u + p) * at_once
                                maxima(b, g + 1, range(k, k + at_once))
                        if u:
                            values(b, g, u - 1)
                        if u == 5:
                            turn_sums(b, g, 0)
                    values(b, g, NU - 1)
                    turn_sums(b, g, 1)
                    if g + 1 < NG:
                        turn_shift(b, g + 1)


F1 = 4 * D
NB1 = F1 // P


def attention_output(nc, m, c, dram, scratch):
    ln = LnSems(m, "ao")
    loaded, in_loaded = m.sem("ao_loaded"), m.sem("ao_in_loaded")
    less, exp_done, prod_done, num_done, den_done, rec_done, o_done, both_done = (
        m.sem("ao_" + n) for n in ("less", "exp", "prod", "num", "den", "rec", "o", "both"))
    o_t, o_out, proj_mm, x1_done, turned, z_ready = (
        m.sem("ao_" + n) for n in ("o_t", "o_out", "proj", "x1", "turned", "z"))
    up_mm, gelu_done, down_mm, y_done, gated, res_done = (
        m.sem("ao_" + n) for n in ("up", "gelu", "down", "y", "gated", "res"))
    X4 = c.X[:, :, :].rearrange("p (b n) d -> p b n d", b=B)
    F4 = c.FUT[:, :, :].rearrange("p (b n) d -> p b n d", b=B)
    M4 = c.SHIFT[:, :, :].rearrange("p (b n) d -> p b n d", b=B)
    N4 = c.ND[:, :, :, :].rearrange("p (b n) h r -> p b n (h r)", b=B)
    ZT = c.HT[:, :, :].rearrange("p b t -> p (b t)")
    loads = [(c.WP[:, :], dram["L1_attn_W_proj_T"]), (c.W1[:, :], dram["L1_attn_W_ff1"]),
             (c.W2[:, :, :], dram["L1_attn_W_ff2"].rearrange("(k p) d -> p k d", p=P))]

    with nc.Block() as block:

        @block.sync
        def _(sp):
            for dst, src in loads:
                sp.dma_start(dst, src).then_inc(loaded, 16)
            with sp.Fori(0, NC) as i:
                sp.wait_ge(x1_done, before(i))
                sp.dma_start(c.VF[:, :, :], scratch.vf[:, bass.ds(i, 1), :, :].rearrange("b o p n -> p b (o n)")
                             ).then_inc(in_loaded, 16)
                sp.dma_start(c.H[:, :, :], scratch.h[:, bass.ds(i, 1), :, :].rearrange("b o p d -> p b (o d)")
                             ).then_inc(in_loaded, 16)

        @block.vector
        def _(dve):
            credit(dve, ln.dve() + [less, prod_done, num_done, den_done, both_done, rec_done, o_done, x1_done,
                                    y_done, gated, res_done])
            with dve.Fori(0, NC) as i:
                fi, mi, ni, xi = at(F4, i), at(M4, i), at(N4, i), at(X4, i)
                for b in range(B):
                    last = nc.vector.tensor_tensor(
                        c.PF[:, b, :].rearrange("p (f h) -> p f h", f=NF), fi[:, b, :].rearrange("p (f h) -> p f h", f=NF),
                        bcast(mi[:, b, :].unsqueeze(1), [P, NF, H1]), ALU.subtract)
                last.then_inc(less, 1)
                dve.wait_ge(exp_done, done(i))
                dve.wait_ge(in_loaded, i * 32 + 32)
                for b in range(B):
                    last = nc.vector.tensor_tensor(
                        c.FP[:, b, :, :].rearrange("p f (h d) -> p (f h) d", d=HS),
                        c.VF[:, b, :].rearrange("p (n d) -> p n d", d=HS),
                        bcast(c.PF[:, b, :].unsqueeze(2), [P, NF * H1, HS]), ALU.mult)
                last.then_inc(prod_done, 1)
                dve.wait_ge(prod_done, done(i))
                for b in range(B):
                    nc.vector.tensor_reduce(c.O[:, b, :], c.FP[:, b, :, :].rearrange("p f n -> p n f"), X_AXIS, ALU.add)
                    last = nc.vector.tensor_reduce(c.DEN[:, b, :], c.PF[:, b, :].rearrange("p (f h) -> p h f", f=NF),
                                                   X_AXIS, ALU.add)
                last.then_inc(num_done, 1)
                dve.wait_ge(num_done, done(i))
                n9 = ni.rearrange("p b (h r) -> p b h r", r=HS + 1)
                for b in range(B):
                    nc.vector.tensor_tensor(c.DEN[:, b, :], c.DEN[:, b, :], n9[:, b, :, HS], ALU.add)
                    last = nc.vector.tensor_tensor(c.O[:, b, :].rearrange("p (h d) -> p h d", d=HS),
                                                   c.O[:, b, :].rearrange("p (h d) -> p h d", d=HS),
                                                   n9[:, b, :, 0:HS], ALU.add)
                last.then_inc(both_done, 1)
                dve.wait_ge(both_done, done(i))
                nc.vector.reciprocal(c.DEN[:, :, :], c.DEN[:, :, :]).then_inc(rec_done, 1)
                dve.wait_ge(rec_done, done(i))
                nc.vector.tensor_tensor(c.O[:, :, :].rearrange("p b (h d) -> p (b h) d", d=HS),
                                        c.O[:, :, :].rearrange("p b (h d) -> p (b h) d", d=HS),
                                        bcast(c.DEN[:, :, :].rearrange("p b h -> p (b h)").unsqueeze(2),
                                              [P, B * H1, HS]), ALU.mult).then_inc(o_done, 1)
                dve.wait_ge(proj_mm, done(i))
                nc.vector.tensor_tensor(c.X1[:, :, :], c.PS[:, 2, :].rearrange("p (b d) -> p b d", b=B),
                                        c.H[:, :, :], ALU.add).then_inc(x1_done, 1)
                dve.wait_ge(x1_done, done(i))
                ln_stats(nc, dve, c, ln, lambda b: c.X1[:, b, :], i)
                ln_apply(nc, dve, c, ln, lambda b: c.X1[:, b, :], lambda b: c.XN[:, b, :], i)
                dve.wait_ge(down_mm, done(i))
                nc.vector.tensor_tensor(c.Y[:, :, :], c.PS[:, 3, :].rearrange("p (b d) -> p b d", b=B),
                                        c.X1[:, :, :], ALU.add).then_inc(y_done, 1)
                dve.wait_ge(y_done, done(i))
                nc.vector.tensor_tensor(c.Y[:, :, :], c.Y[:, :, :], c.MROW[:, 1, :, GATE_A, :], ALU.mult
                                        ).then_inc(gated, 1)
                dve.wait_ge(gated, done(i))
                nc.vector.tensor_tensor(xi, xi, c.Y[:, :, :], ALU.add).then_inc(res_done, 1)

        @block.gpsimd
        def _(pool):
            credit(pool, ln.pool())
            with pool.Fori(0, NC) as i:
                ln_rstd(nc, pool, c, ln, i)

        @block.scalar
        def _(act):
            credit(act, [exp_done, o_out, z_ready, gelu_done])
            with act.Fori(0, NC) as i:
                act.wait_ge(less, done(i))
                nc.scalar.activation(c.PF[:, :, :], c.PF[:, :, :], ACT.Exp).then_inc(exp_done, 1)
                act.wait_ge(o_t, done(i))
                nc.scalar.copy(c.OT[:, :, :], c.PS[:, 1, :].rearrange("p (b t) -> p b t", b=B)).then_inc(o_out, 1)
                act.wait_ge(turned, done(i))
                nc.scalar.activation(ZT, c.PS[:, 0, :], ACT.Identity, scale=c.LNG[:, 2:3], bias=c.LNG[:, 3:4]
                                     ).then_inc(z_ready, 1)
                act.wait_ge(up_mm, done(i))
                nc.scalar.activation(c.GE[:, :, :], c.PS[:, 4:8, :], ACT.Gelu).then_inc(gelu_done, 1)

        @block.tensor
        def _(pe):
            credit(pe, [o_t, proj_mm, turned, up_mm, down_mm])
            pe.wait_ge(loaded, 16 * len(loads))
            with pe.Fori(0, NC) as i:
                pe.wait_ge(o_done, done(i))
                for b in range(B):
                    last = nc.tensor.transpose(c.PS[:, 1, b * P:(b + 1) * P], c.O[:, b, :], c.IDENT[:, :])
                last.then_inc(o_t, 1)
                pe.wait_ge(o_out, done(i))
                for b in range(B):
                    last = nc.tensor.matmul(c.PS[:, 2, b * P:(b + 1) * P], c.OT[:, b, :], c.WP[:, :],
                                            start=True, stop=True)
                last.then_inc(proj_mm, 1)
                pe.wait_ge(ln.normed, done(i))
                for b in range(B):
                    last = nc.tensor.transpose(c.PS[:, 0, b * P:(b + 1) * P], c.XN[:, b, :], c.IDENT[:, :])
                last.then_inc(turned, 1)
                pe.wait_ge(z_ready, done(i))
                for k in range(NB1):
                    last = nc.tensor.matmul(c.PS[:, 4 + k, :], c.W1[:, k * P:(k + 1) * P], ZT, start=True, stop=True)
                last.then_inc(up_mm, 1)
                pe.wait_ge(gelu_done, done(i))
                for b in range(B):
                    for k in range(NB1):
                        last = nc.tensor.matmul(c.PS[:, 3, b * P:(b + 1) * P], c.GE[:, k, b * P:(b + 1) * P],
                                                c.W2[:, k, :], start=(k == 0), stop=(k == NB1 - 1))
                last.then_inc(down_mm, 1)


E1 = 64
PAIRS = B * T // 8 // 2
SB, BP = 128, 8
NSB, NBP = PAIRS // SB, SB // BP
GR = NSB * 2


def experts_input(nc, m, c, scratch):
    ln = LnSems(m, "ki")
    turned, h_ready, x_stored = m.sem("ki_turned"), m.sem("ki_h"), m.sem("ki_x_stored")
    X4 = c.X[:, :, :].rearrange("p (b n) d -> p b n d", b=B)
    H4 = c.HTA[:, :].rearrange("p (b n t) -> p b n t", b=B, n=NC)
    with nc.Block() as block:

        @block.sync
        def _(sp):
            sp.dma_start(scratch.x, c.X[:, :, :]).then_inc(x_stored, 16)
            sp.wait_ge(h_ready, NC + 1)
            sp.dma_start(scratch.ht, c.HTA[:, :]).then_inc(x_stored, 16)
            sp.wait_ge(x_stored, 32)

        @block.vector
        def _(dve):
            credit(dve, ln.dve())
            with dve.Fori(0, NC) as i:
                xi = at(X4, i)
                ln_stats(nc, dve, c, ln, lambda b: xi[:, b, :], i)
                dve.wait_ge(turned, before(i))
                ln_apply(nc, dve, c, ln, lambda b: xi[:, b, :], lambda b: c.XN[:, b, :], i)

        @block.gpsimd
        def _(pool):
            credit(pool, ln.pool())
            with pool.Fori(0, NC) as i:
                ln_rstd(nc, pool, c, ln, i)

        @block.scalar
        def _(act):
            credit(act, [h_ready])
            with act.Fori(0, NC) as i:
                act.wait_ge(turned, done(i))
                hi = at(H4, i)
                for b in range(B):
                    last = nc.scalar.activation(hi[:, b, :], c.PS[:, 0, b * P:(b + 1) * P], ACT.Identity,
                                                scale=c.MCOL[:, 1, SCALE_B, b:b + 1],
                                                bias=c.MCOL[:, 1, SHIFT_B, b:b + 1])
                last.then_inc(h_ready, 1)

        @block.tensor
        def _(pe):
            credit(pe, [turned])
            with pe.Fori(0, NC) as i:
                pe.wait_ge(ln.normed, done(i))
                pe.wait_ge(h_ready, before(i))
                for b in range(B):
                    last = nc.tensor.transpose(c.PS[:, 0, b * P:(b + 1) * P], c.XN[:, b, :], c.IDENT[:, :])
                last.then_inc(turned, 1)


def route(nc, m, c, tag, logits_mm):
    names = ("logit_mm", "logit_out", "top", "idx", "idx_f", "diff", "exp", "sum", "rec", "second", "hot",
             "weighed", "turned")
    s = {n: m.sem(tag + "_" + n) for n in names}
    with nc.Block() as block:

        @block.vector
        def _(dve):
            dve.wait_ge(s["logit_mm"], 1)
            nc.vector.tensor_copy(c.LG1[:, :, :], c.PS[:, 0, 0:GR * E1].rearrange("p (g e) -> p g e", g=GR)
                                  ).then_inc(s["logit_out"], 1)
            dve.wait_ge(s["logit_out"], 1)
            for g in range(GR):
                last = nc.vector.max(c.TOP1[:, g, :], c.LG1[:, g, :])
            last.then_inc(s["top"], 1)
            dve.wait_ge(s["top"], 1)
            nc.vector.tensor_tensor(c.PR[:, :, 1:2], c.TOP1[:, :, 1:2], c.TOP1[:, :, 0:1], ALU.subtract
                                    ).then_inc(s["diff"], 1)
            for g in range(GR):
                last = nc.vector.max_index(c.TIX1[:, g, :], c.TOP1[:, g, :], c.LG1[:, g, :])
            last.then_inc(s["idx"], 1)
            dve.wait_ge(s["idx"], 1)
            nc.vector.tensor_copy(c.TIF1[:, :, :], c.TIX1[:, :, 0:2]).then_inc(s["idx_f"], 1)
            dve.wait_ge(s["idx_f"], 1)
            for k in range(2):
                for twin in range(2):
                    last = nc.vector.tensor_tensor(c.OH[:, k, :, twin, :],
                                                   bcast(c.IOTA1[:, :].unsqueeze(1), [P, GR, E1]),
                                                   bcast(c.TIF1[:, :, k:k + 1], [P, GR, E1]), ALU.is_equal)
            last.then_inc(s["hot"], 1)
            dve.wait_ge(s["exp"], 1)
            nc.vector.tensor_scalar_add(c.PR[:, :, 2:3], c.PR[:, :, 1:2], 1.0).then_inc(s["sum"], 1)
            dve.wait_ge(s["sum"], 1)
            nc.vector.reciprocal(c.PR[:, :, 0:1], c.PR[:, :, 2:3]).then_inc(s["rec"], 1)
            dve.wait_ge(s["rec"], 1)
            nc.vector.tensor_tensor(c.PR[:, :, 1:2], c.PR[:, :, 1:2], c.PR[:, :, 0:1], ALU.mult
                                    ).then_inc(s["second"], 1)
            dve.wait_ge(s["second"], 1)
            dve.wait_ge(s["hot"], 1)
            for k in range(2):
                last = nc.vector.tensor_tensor(c.OHW[:, k, :, :], c.OH[:, k, :, 0, :],
                                               bcast(c.PR[:, :, k:k + 1], [P, GR, E1]), ALU.mult)
            last.then_inc(s["weighed"], 1)
            dve.wait_ge(s["turned"], 1)
            nc.vector.tensor_copy(c.OHT[:, :, :], c.PS[:, 4:6, :])
            nc.vector.tensor_copy(c.OHTW[:, :, :], c.PS[0:E1, 6:8, :])

        @block.scalar
        def _(act):
            act.wait_ge(s["diff"], 1)
            nc.scalar.activation(c.PR[:, :, 1:2], c.PR[:, :, 1:2], ACT.Exp).then_inc(s["exp"], 1)

        @block.tensor
        def _(pe):
            logits_mm(pe).then_inc(s["logit_mm"], 1)
            pe.wait_ge(s["weighed"], 1)
            for k in range(2):
                for g in range(GR):
                    nc.tensor.transpose(c.PS[:, 4 + k, g * P:(g + 1) * P],
                                        c.OH[:, k, g, :, :].rearrange("p t e -> p (t e)"), c.IDENT[:, :])
                    last = nc.tensor.transpose(c.PS[0:E1, 6 + k, g * P:(g + 1) * P], c.OHW[:, k, g, :],
                                               c.IDENT[:, :])
            last.then_inc(s["turned"], 1)


def up_logits(nc, c):
    H = c.HTA[:, :].rearrange("p (n r k) -> p n r k", r=2, k=8)
    for sb in range(NSB):
        for r in range(2):
            o = (sb * 2 + r) * E1
            for k in range(8):
                last = nc.tensor.matmul(c.PS[:, 0, o:o + E1], H[:, sb * SB:(sb + 1) * SB, r, k], c.WUR[:, k, :],
                                        start=(k == 0), stop=(k == 7))
    return last


def down_turned(nc, c):
    for sb in range(NSB):
        last = nc.tensor.transpose(c.PS[:, 0, sb * P:(sb + 1) * P], c.LT[:, sb * SB:(sb + 1) * SB], c.IDENT[:, :])
    return last


def table_loads(c, dram, layer):
    flat = lambda name: dram[name].rearrange("e o i -> e (o i)")
    return [(table_rows(c, n)[E1 * twin:E1 * twin + E1, :], flat(f"L1_ffn_{n}_{layer}"))
            for n in "AB" for twin in range(2)]


def table_rows(c, name):
    k = 16 * "AB".index(name)
    return c.BG[:, k:k + 16, :].rearrange("p k n -> p (k n)")


def split_tables(nc, dve, c, split):
    pairs = [(table_rows(c, "A"), c.TWO[:, 0, :], c.LOW[:, 0, :]), (table_rows(c, "B"), c.TWO[:, 1, :], c.LOW[:, 1, :])]
    for rows, two, low in pairs:
        last = nc.vector.tensor_copy(two, rows)
    last.then_inc(split, 1)
    dve.wait_ge(split, 1)
    for rows, two, low in pairs:
        last = nc.vector.tensor_tensor(rows, rows, two, ALU.subtract)
    last.then_inc(split, 1)
    dve.wait_ge(split, 2)
    for rows, two, low in pairs:
        nc.vector.tensor_copy(two[E1:P, :], rows[E1:P, :])
        last = nc.vector.tensor_copy(low[0:E1, :], rows[0:E1, :])
    last.then_inc(split, 1)
    dve.wait_ge(split, 3)
    for rows, two, low in pairs:
        nc.vector.tensor_tensor(low[0:E1, :], rows[0:E1, :], low[0:E1, :], ALU.subtract)


def kronecker_loads(nc, m, c, dram, scratch):
    loaded, tables, split = m.sem("ke_loaded"), m.sem("ke_tables"), m.sem("ke_split")
    first = table_loads(c, dram, "up")
    loads = [(c.WUR[:, :, :], dram["L1_ffn_W_up"]),
             (c.SCL[:, 0:1], dram["L1_ffn_scale_up"].partition_broadcast(P)),
             (c.SCL[:, 1:2], dram["L1_ffn_scale_down"].partition_broadcast(P)),
             (c.BUP[0:64, :], dram["L1_ffn_bias_up"]), (c.BUP[64:128, :], dram["L1_ffn_bias_up"]),
             (c.BDN[:, :], dram["L1_ffn_bias_down"]), (c.HTA[:, :], scratch.ht)]
    with nc.Block() as block:

        @block.sync
        def _(sp):
            for dst, src in first:
                sp.dma_start(dst, src).then_inc(tables, 16)
            for dst, src in loads:
                sp.dma_start(dst, src).then_inc(loaded, 16)
            sp.wait_ge(loaded, 16 * len(loads))

        @block.vector
        def _(dve):
            nc.vector.memset(c.LOW[E1:P, :, :], 0.0)
            dve.wait_ge(tables, 16 * len(first))
            split_tables(nc, dve, c, split)

        @block.gpsimd
        def _(pool):
            nc.gpsimd.iota(c.IOTA1[:, :], [[1, E1]], base=0, channel_multiplier=0,
                           allow_small_or_imprecise_dtypes=True)
            nc.gpsimd.memset(c.XD[:, :, :, :], 0.0)
            nc.gpsimd.memset(c.T2[:, :, :, :], 0.0)


def kronecker(nc, m, c, up):
    tag = "ku" if up else "kd"
    names = ("oh_laid", "w_mm", "w_out", "gath_mm", "gath_dve", "gath_act", "x_dve", "x_pool", "one_mm", "t_out",
             "two_mm", "y_out")
    s = {n: m.sem(tag + "_" + n) for n in names}
    WIDE = 64
    NBANK = WIDE // 4
    G = 2 * NBANK
    HALF_B = NBP // 2 - 1
    HD = c.HD[:, :, :]
    made = lambda q: q + 3
    freed = lambda q: q + 1

    def gather(pe, n):
        table = (n + 1) % 2
        for k in range(4):
            col = (n // 2) * 4 + k
            o = c.PS[:, n % 4, k * P:(k + 1) * P]
            for part, start in ((c.TWO, True), (c.LOW, False)):
                for r in range(2):
                    cols = slice(r * SB, (r + 1) * SB)
                    if up:
                        for e in range(2):
                            q = 32 * (2 * r + e)
                            last = nc.tensor.matmul(o[q:q + 32, :], part[:, table, col * 32:col * 32 + 32],
                                                    c.OHB[:, e, cols], start=start, stop=not start)
                    else:
                        e, w = col // 32, col % 32
                        last = nc.tensor.matmul(o[64 * r:64 * r + 64, :], part[:, table, w * 64:w * 64 + 64],
                                                c.OHB[:, e, cols], start=start, stop=not start)
        return last

    def spread_weights():
        for r in range(2):
            for e in range(2):
                w = c.OHBW[:, e, r * SB:(r + 1) * SB]
                if up:
                    q = 32 * (2 * r + e)
                    last = nc.tensor.matmul(c.PS[q:q + 32, 7, 0:SB], c.ONES[0:E1, 0:32], w, start=True, stop=True)
                else:
                    last = nc.tensor.matmul(c.PS[64 * r:64 * r + 64, 7, e * SB:(e + 1) * SB], c.ONES[0:E1, 0:64],
                                            w, start=True, stop=True)
        return last

    def lay_up(engine, q, par, blocks):
        H = c.HTA[:, :].rearrange("p (n r k) -> p n r k", r=2, k=8)[:, bass.ds(q * BP, BP), :, :]
        for r, e in blocks:
            z = 32 * (2 * r + e)
            dst = c.XD[z:z + 32, par, :, z:z + 32].rearrange("p n (k f) -> p n k f", f=4)
            for f in range(4):
                last = engine.tensor_copy(dst[:, :, :, f], H[32 * f:32 * f + 32, :, r, :])
        return last

    def lay_down(engine, q, par, r):
        z = 64 * r
        return engine.tensor_copy(c.XD[z:z + 64, par, :, z:z + 64], HD[z:z + 64, bass.ds(q * BP, BP), :])

    with nc.Block() as block:

        @block.vector
        def _(dve):
            credit(dve, [s["oh_laid"], s["w_out"], s["gath_dve"], s["gath_dve"], s["x_dve"], s["y_out"], s["y_out"]])

            def lay(q, par):
                dve.wait_ge(s["one_mm"], freed(q))
                last = lay_up(nc.vector, q, par, ((0, 0), (0, 1), (1, 0))) if up else lay_down(nc.vector, q, par, 0)
                last.then_inc(s["x_dve"], 1)

            def product_out(q, par):
                dve.wait_ge(s["two_mm"], made(q))
                if up:
                    nc.vector.scalar_tensor_tensor(
                        HD[:, bass.ds(q * BP, BP), :], c.PS[:, 6 + par, :].rearrange("p (n o) -> p n o", n=BP),
                        c.SCL[:, 0:1], bcast(c.BUP[:, :].unsqueeze(1), [P, BP, 64]), ALU.mult, ALU.add
                    ).then_inc(s["y_out"], 1)
                else:
                    src = c.PS[:, 6 + par, 0:BP * 32].rearrange("p (n k f) -> p n k f", n=BP, f=4)
                    Y = c.YT[:, :].rearrange("p (n r k) -> p n r k", r=2, k=8)[:, bass.ds(q * BP, BP), :, :]
                    for r in range(2):
                        for f in range(4):
                            last = nc.vector.tensor_scalar(
                                Y[32 * f:32 * f + 32, :, r, :], src[32 * r:32 * r + 32, :, :, f],
                                c.SCL[32 * r:32 * r + 32, 1:2], None, ALU.mult)
                    last.then_inc(s["y_out"], 1)

            with dve.Fori(0, NSB) as sb:
                part = lambda t: t[:, :, :].rearrange("e k (b n) -> e k b n", b=NSB)[
                    :, :, bass.ds(sb, 1), :].rearrange("e k o n -> e k (o n)")
                nc.vector.tensor_copy(c.OHBW[:, :, :], part(c.OHTW))
                nc.vector.tensor_copy(c.OHB[:, :, :], part(c.OHT)).then_inc(s["oh_laid"], 1)
                for k in range(2):
                    lay(sb * NBP + k, k)
                dve.wait_ge(s["w_mm"], sb + 1)
                nc.vector.tensor_copy(c.WGT[:, :, :], c.PS[:, 7, 0:2 * SB].rearrange("p (e n) -> p e n", e=2)
                                      if not up else bcast(c.PS[:, 7, 0:SB].unsqueeze(1), [P, 2, SB])
                                      ).then_inc(s["w_out"], 1)
                dve.wait_ge(s["w_out"], done(sb))
                for n in range(0, G, 2):
                    k = (n // 2) * 4
                    e = k // 32
                    dve.wait_ge(s["gath_mm"], sb * G + n + 1)
                    nc.vector.tensor_tensor(c.BG[:, k:k + 4, :], c.PS[:, n % 4, :].rearrange("p (k n) -> p k n", k=4),
                                            bcast(c.WGT[:, e:e + 1, :], [P, 4, SB]), ALU.mult
                                            ).then_inc(s["gath_dve"], 1)
                with dve.Fori(0, HALF_B) as it:
                    for par in range(2):
                        q = sb * NBP + it * 2 + par
                        lay(q + 2, par)
                        product_out(q, par)
                for par in range(2):
                    product_out(sb * NBP + (NBP - 2 + par), par)

        @block.gpsimd
        def _(pool):
            credit(pool, [s["x_pool"]])
            with pool.Fori(0, NSB * NBP // 2) as it:
                for par in range(2):
                    q = it * 2 + par
                    pool.wait_ge(s["one_mm"], freed(q))
                    pool.sem_inc(c.passed, 1)
                    last = lay_up(nc.gpsimd, q, par, ((1, 1),)) if up else lay_down(nc.gpsimd, q, par, 1)
                    last.then_inc(s["x_pool"], 1)

        @block.scalar
        def _(act):
            credit(act, [s["gath_act"], s["gath_act"], s["t_out"], s["t_out"]])
            with act.Fori(0, NSB) as sb:
                for n in range(1, G, 2):
                    k = (n // 2) * 4
                    act.wait_ge(s["gath_mm"], sb * G + n + 1)
                    nc.scalar.copy(c.AG[:, k:k + 4, :], c.PS[:, n % 4, :].rearrange("p (k n) -> p k n", k=4)
                                   ).then_inc(s["gath_act"], 1)
                with act.Fori(0, NBP // 2) as it:
                    for par in range(2):
                        q = sb * NBP + it * 2 + par
                        act.wait_ge(s["one_mm"], made(q))
                        act.wait_ge(s["two_mm"], freed(q))
                        for r in range(2):
                            z = 64 * r
                            src = c.PS[z:z + 64, 4 + par, :]
                            if up:
                                last = nc.scalar.copy(c.T2[z:z + 64, par, :, z:z + 64],
                                                      src.rearrange("p (n k) -> p n k", n=BP))
                            else:
                                dst = c.T2[z:z + 64, par, :, :].rearrange("p n (e r k) -> p n e r k", e=2, r=2)
                                last = nc.scalar.copy(dst[:, :, :, r, :],
                                                      src.rearrange("p (n e k) -> p n e k", n=BP, e=2))
                        last.then_inc(s["t_out"], 1)
                if up:
                    act.wait_ge(s["y_out"], sb * NBP + (NBP + 2))
                    h = HD[:, bass.ds(sb * SB, SB), :]
                    nc.scalar.activation(h, h, ACT.Gelu)

        @block.tensor
        def _(pe):
            credit(pe, [s["one_mm"], s["one_mm"], s["two_mm"], s["two_mm"]])

            def column(t, place, a, b):
                return t[:, a:b, bass.ds(place, 1)].rearrange("p k o -> p (k o)")

            def one(sb, it, par):
                q = sb * NBP + it
                pe.wait_ge(s["x_dve"], done(q))
                pe.wait_ge(s["x_pool"], done(q))
                pe.wait_ge(s["t_out"], freed(q))
                pe.sem_inc(c.passed, 1)
                for j in range(BP):
                    last = nc.tensor.matmul(c.PS[:, 4 + par, j * 64:j * 64 + 64], c.XD[:, par, j, :],
                                            column(c.BG, it * BP + j, 0, 64), start=True, stop=True)
                last.then_inc(s["one_mm"], 1)

            def two(sb, it, par):
                q = sb * NBP + it
                pe.wait_ge(s["t_out"], made(q))
                pe.wait_ge(s["y_out"], freed(q))
                pe.sem_inc(c.passed, 1)
                for j in range(BP):
                    if up:
                        last = nc.tensor.matmul(c.PS[:, 6 + par, j * 64:j * 64 + 64], c.T2[:, par, j, :],
                                                column(c.AG, it * BP + j, 0, 64), start=True, stop=True)
                    else:
                        for e in range(2):
                            last = nc.tensor.matmul(c.PS[0:64, 6 + par, j * 32:j * 32 + 32],
                                                    c.T2[:, par, j, e * 64:e * 64 + 64],
                                                    column(c.AG, it * BP + j, 32 * e, 32 * e + 32),
                                                    start=(e == 0), stop=(e == 1))
                last.then_inc(s["two_mm"], 1)

            with pe.Fori(0, NSB) as sb:
                pe.wait_ge(s["oh_laid"], done(sb))
                pe.sem_inc(c.passed, 1)
                spread_weights().then_inc(s["w_mm"], 1)
                for n in range(G):
                    free = s["gath_act"] if n % 2 else s["gath_dve"]
                    pe.wait_ge(free, sb * NBANK + (n // 2 + 1))
                    pe.sem_inc(c.passed, 1)
                    gather(pe, n).then_inc(s["gath_mm"], 1)
                pe.wait_ge(s["gath_dve"], sb * NBANK + (NBANK + 2))
                pe.wait_ge(s["gath_act"], sb * NBANK + (NBANK + 2))
                pe.sem_inc(c.passed, 1)
                one(sb, 0, 0)
                with pe.Fori(0, HALF_B) as it:
                    for par in range(2):
                        one(sb, it * 2 + (par + 1), 1 - par)
                        two(sb, it * 2 + par, par)
                one(sb, NBP - 1, 1)
                two(sb, NBP - 2, 0)
                two(sb, NBP - 1, 1)


def down_logits(nc, m, c, dram):
    zeroed, loaded, mm = m.sem("dl_zeroed"), m.sem("dl_loaded"), m.sem("dl_mm")
    tables, split = m.sem("dl_tables"), m.sem("dl_split")
    tables_of_down = table_loads(c, dram, "down")
    with nc.Block() as block:

        @block.gpsimd
        def _(pool):
            nc.gpsimd.memset(c.AG[:, :, :], 0.0).then_inc(zeroed, 1)
            nc.gpsimd.memset(c.T2[:, :, :, :], 0.0)

        @block.sync
        def _(sp):
            for dst, src in tables_of_down:
                sp.dma_start(dst, src).then_inc(tables, 16)
            sp.wait_ge(zeroed, 1)
            for r in range(2):
                sp.dma_start(c.AG[64 * r:64 * r + 64, :, 64 * r:64 * r + 64], dram["L1_ffn_W_down"]
                             ).then_inc(loaded, 16)
            sp.wait_ge(loaded, 32)

        @block.vector
        def _(dve):
            dve.wait_ge(tables, 16 * len(tables_of_down))
            split_tables(nc, dve, c, split)

        @block.tensor
        def _(pe):
            pe.wait_ge(loaded, 32)
            for o in range(64):
                last = nc.tensor.matmul(c.PS[:, 1, 0:PAIRS], c.AG[:, o, :], c.HD[:, :, o],
                                        start=(o == 0), stop=(o == 63))
            last.then_inc(mm, 1)

        @block.scalar
        def _(act):
            act.wait_ge(mm, 1)
            nc.scalar.copy(c.LT[:, :], c.PS[:, 1, 0:PAIRS])


def experts_output(nc, m, c, scratch, out):
    x_loaded, biased, turned, gated, x_done, stored_ = (
        m.sem("ko_" + n) for n in ("x_loaded", "biased", "turned", "gated", "x_done", "stored"))
    Y4 = c.YT[:, :].rearrange("p (b n t) -> p b n t", b=B, n=NC)
    chunk = lambda t, i: t[:, :, bass.ds(i, 1), :].rearrange("p b o d -> p b (o d)")
    S4 = scratch.x.rearrange("p (b n) d -> p b n d", b=B)
    OUT = out.rearrange("b (n p) d -> p b n d", p=P)
    with nc.Block() as block:

        @block.sync
        def _(sp):
            sp.sem_inc(stored_, 16)
            with sp.Fori(0, NC) as i:
                sp.wait_ge(stored_, stored(i))
                sp.dma_start(c.XC[:, :, :], chunk(S4, i)).then_inc(x_loaded, 16)
                sp.wait_ge(x_done, done(i))
                sp.dma_start(chunk(OUT, i), c.XC[:, :, :]).then_inc(stored_, 16)
            sp.wait_ge(stored_, 16 * NC + 16)

        @block.vector
        def _(dve):
            credit(dve, [biased, gated, x_done])
            with dve.Fori(0, NC) as i:
                dve.wait_ge(turned, before(i))
                for b in range(B):
                    last = nc.vector.tensor_tensor(
                        c.YB[:, b, :].rearrange("p (m k) -> p m k", k=8),
                        chunk(Y4, i)[:, b, :].rearrange("p (m k) -> p m k", k=8),
                        bcast(c.BDN[:, :].unsqueeze(1), [P, P // 8, 8]), ALU.add)
                last.then_inc(biased, 1)
                dve.wait_ge(turned, done(i))
                nc.vector.tensor_tensor(c.Y[:, :, :], c.PS[:, 0, :].rearrange("p (b d) -> p b d", b=B),
                                        c.GATE[:, :, :], ALU.mult).then_inc(gated, 1)
                dve.wait_ge(gated, done(i))
                dve.wait_ge(x_loaded, i * 16 + 16)
                nc.vector.tensor_tensor(c.XC[:, :, :], c.XC[:, :, :], c.Y[:, :, :], ALU.add).then_inc(x_done, 1)

        @block.tensor
        def _(pe):
            credit(pe, [turned])
            with pe.Fori(0, NC) as i:
                pe.wait_ge(biased, done(i))
                pe.wait_ge(gated, before(i))
                for b in range(B):
                    last = nc.tensor.transpose(c.PS[:, 0, b * P:(b + 1) * P], c.YB[:, b, :], c.IDENT[:, :])
                last.then_inc(turned, 1)


class Tiles:
    pass


def allocate(m):
    c = Tiles()
    c.PS = m.ps("PS", [P, 8, 512])
    c.IDENT, c.ONES, c.UPTO = m.sb("IDENT", [P, P]), m.sb("ONES", [P, P]), m.sb("UPTO", [P, P])
    c.ZERO, c.LATER = m.sb("ZERO", [P, P], BF16), m.sb("LATER", [P, P], BF16)
    c.IDENTB = m.sb("IDENTB", [P, P], BF16)
    c.HALF, c.IOTA, c.EPS = m.sb("HALF", [P, B]), m.sb("IOTA", [P, 8]), m.sb("EPS", [P, B])
    c.COND, c.MCOL = m.sb("COND", [P, 2, B]), m.sb("MCOL", [P, 2, 6, B])
    c.ST, c.MV = m.sb("ST", [P, B, 6]), m.sb("MV", [P, B, 2])
    c.VE, c.RSTD = m.sb("VE", [P, B]), m.sb("RSTD", [P, B])
    c.Y, c.GATE = m.sb("Y", [P, B, D]), m.sb("GATE", [P, B, D])
    return c


class Scope:

    def __init__(self, nc, sem):
        self.nc, self.sem, self.stack = nc, sem, ExitStack()

    def __enter__(self):
        self.stack.__enter__()
        return self

    def __exit__(self, *e):
        return self.stack.__exit__(*e)

    def sb(self, name, shape, dt=F32):
        return self.stack.enter_context(self.nc.sbuf_tensor(name, shape, dt))


def keep_gate(nc, m, c):
    with nc.Block() as block:

        @block.vector
        def _(dve):
            nc.vector.tensor_copy(c.GATE[:, :, :], c.MROW[:, 1, :, GATE_B, :])


def build(nc, dram, out):
    with ExitStack() as ctx:
        m = Mem(nc, ctx)
        c = allocate(m)
        c.passed = m.sem("passed")
        scratch = Tiles()
        scratch.h = nc.dram_tensor("h1", (B, NC, P, D), F32, kind="Internal").ap()
        scratch.qk = nc.dram_tensor("qk_parts", (P, 3 * 2 * B, T), BF16, kind="Internal").ap()
        scratch.vf = nc.dram_tensor("future_v", (B, NC, P, NF * D), F32, kind="Internal").ap()
        scratch.ht = nc.dram_tensor("ht_mid", (P, B * T), F32, kind="Internal").ap()
        scratch.x = nc.dram_tensor("x_mid", (P, CH, D), F32, kind="Internal").ap()
        with Scope(nc, m.sem) as a:
            c.X = a.sb("X", [P, CH, D])
            c.MROW = a.sb("MROW", [P, 2, B, 6, D])
            c.XN, c.HT = a.sb("XN", [P, B, D]), a.sb("HT", [P, B, P])
            c.O, c.OT = a.sb("O", [P, B, D]), a.sb("OT", [P, B, P])
            with Scope(nc, m.sem) as t:
                c.WQKV, c.WO, c.BQKV, c.BO = (t.sb("WQKV", [P, 256]), t.sb("WO", [P, D]),
                                              t.sb("BQKV", [P, 256]), t.sb("BO", [P, D]))
                c.WMOD, c.CB, c.CB2 = t.sb("WMOD", [P, 2, 768]), t.sb("CB", [P, 8, P]), t.sb("CB2", [P, 8, P])
                c.QKV, c.NEG, c.PHI = (t.sb("QKV", [P, B, 256]), t.sb("NEG", [P, B, 128]),
                                       t.sb("PHI", [P, B, 128]))
                c.KVP, c.KVSUM, c.PROD = (t.sb(n, [P, B, 512]) for n in ("KVP", "KVSUM", "PROD"))
                c.KSUM, c.KPROD = t.sb("KSUM", [P, B, 64]), t.sb("KPROD", [P, B, 64])
                c.DEN, c.REC, c.NUM = t.sb("DEN", [P, 64]), t.sb("REC", [P, 64]), t.sb("NUM", [P, B, D])
                m.stage(setup, c, dram)
                m.stage(keep_gate, c)
                m.stage(linear_attention, c)
            with Scope(nc, m.sem) as t:
                c.WR, c.WG, c.WU = t.sb("WR", [P, 9]), t.sb("WG", [P, NE0 + 1, F0]), t.sb("WU", [P, NE0 + 1, F0])
                c.WD = t.sb("WD", [P, NE0 + 1, 2, D])
                c.LG, c.EX, c.CW = t.sb("LG", [P, B, 9]), t.sb("EX", [P, B, 9]), t.sb("CW", [P, B, 9])
                c.TOP, c.TIX = t.sb("TOP", [P, B, 8]), t.sb("TIX", [P, B, 8], U32)
                c.TIF, c.HOT = t.sb("TIF", [P, B, 2]), t.sb("HOT", [P, 2, B, 8])
                c.SUM, c.RS = t.sb("SUM", [P, B, 2]), t.sb("RS", [P, B, 2])
                c.SG, c.HH = t.sb("SG", [P, 2, 2, 512]), t.sb("HH", [P, 2, 2, 512])
                m.stage(experts, c, dram)
            with Scope(nc, m.sem) as u:
                c.VT, c.FUT, c.FMAX = (u.sb("VT", [P, CH, D]), u.sb("FUT", [P, CH, NF * H1]),
                                       u.sb("FMAX", [P, CH, H1]))
                c.SHIFT, c.LNG = u.sb("SHIFT", [P, CH, H1]), u.sb("LNG", [P, 4])
                with Scope(nc, m.sem) as t:
                    c.WT, c.WF, c.CV = t.sb("WT", [P, 4 * D]), t.sb("WF", [P, D]), t.sb("CV", [P, NF, HS])
                    c.BD, c.BLOCKS = t.sb("BD", [P, NF, P]), t.sb("BLOCKS", [P, P])
                    c.GK, c.BIG = t.sb("GK", [P, NF, 2 * D]), t.sb("BIG", [P, NF, 2 * D])
                    c.H, c.QKF = t.sb("H", [P, B, D]), t.sb("QKF", [P, 2 * B, P])
                    c.PARTS = t.sb("PARTS", [P, 6 * B, P], BF16)
                    c.QV, c.VF, c.FP = (t.sb("QV", [P, B, 2 * D]), t.sb("VF", [P, B, NF * D]),
                                        t.sb("FP", [P, B, NF, D]))
                    m.stage(attention_inputs, c, dram, scratch)
                c.ND = u.sb("ND", [P, CH, H1, HS + 1])
                with Scope(nc, m.sem) as t:
                    c.QS, c.KS = t.sb("QS", [P, NG, GH, T], BF16), t.sb("KS", [P, NG, GH, T], BF16)
                    c.PT, c.VG = t.sb("PT", [P, 2, 2, 2, 512]), t.sb("VG", [P, 2, NC, GH, 32])
                    c.MP, c.MX, c.MG = (t.sb("MP", [P, NC, 2, GH]), t.sb("MX", [P, NC, GH]),
                                        t.sb("MG", [P, GH, NC]))
                    c.SH, c.NEGM = t.sb("SH", [NC * GH, 2, P]), t.sb("NEGM", [NC * GH, 2, NS, P], BF16)
                    c.OF = t.sb("OF", [P, 512])
                    m.stage(attention, c, scratch)
                with Scope(nc, m.sem) as t:
                    c.WP, c.W1, c.W2 = t.sb("WP", [P, D]), t.sb("W1", [P, F1]), t.sb("W2", [P, NB1, D])
                    c.H, c.VF, c.FP = (t.sb("H2", [P, B, D]), t.sb("VF2", [P, B, NF * D]),
                                       t.sb("FP2", [P, B, NF, D]))
                    c.PF, c.DEN, c.X1 = (t.sb("PF", [P, B, NF * H1]), t.sb("DEN2", [P, B, H1]),
                                         t.sb("X1", [P, B, D]))
                    c.GE = t.sb("GE", [P, NB1, 512])
                    m.stage(attention_output, c, dram, scratch)
            c.HTA0 = a.sb("HTA0", [P, B * T])
            c.HTA = c.HTA0
            m.stage(experts_input, c, scratch)
        with Scope(nc, m.sem) as a:
            c.HTA = a.sb("HTA", [P, B * T])
            c.YT = c.HTA
            c.BG, c.AG = a.sb("BG", [P, 64, SB]), a.sb("AG", [P, 64, SB])
            c.HD, c.XD = a.sb("HD", [P, PAIRS, 64]), a.sb("XD", [P, 2, BP, P])
            c.T2, c.WGT = a.sb("T2", [P, 2, BP, P]), a.sb("WGT", [P, 2, SB])
            c.TWO, c.LOW = a.sb("TWO", [P, 2, 2048], BF16), a.sb("LOW", [P, 2, 2048], BF16)
            c.OH, c.OHW = a.sb("OH", [P, 2, GR, 2, E1]), a.sb("OHW", [P, 2, GR, E1])
            c.OHT, c.OHTW = a.sb("OHT", [P, 2, 512], BF16), a.sb("OHTW", [E1, 2, 512])
            c.OHB, c.OHBW = a.sb("OHB", [P, 2, 2 * SB], BF16), a.sb("OHBW", [E1, 2, 2 * SB])
            c.WUR, c.LG1 = a.sb("WUR", [P, 8, E1]), a.sb("LG1", [P, GR, E1])
            c.TOP1, c.TIX1 = a.sb("TOP1", [P, GR, 8]), a.sb("TIX1", [P, GR, 8], U32)
            c.TIF1, c.PR, c.IOTA1 = a.sb("TIF1", [P, GR, 2]), a.sb("PR", [P, GR, 3]), a.sb("IOTA1", [P, E1])
            c.SCL, c.BUP, c.BDN = a.sb("SCL", [P, 2]), a.sb("BUP", [P, 64]), a.sb("BDN", [P, 8])
            c.LT = a.sb("LT", [P, PAIRS])
            c.XC, c.YB = c.BG[:, 0:B, :], c.BG[:, B:2 * B, :]
            m.stage(kronecker_loads, c, dram, scratch)
            m.stage(route, c, "ru", lambda pe: up_logits(nc, c))
            m.stage(kronecker, c, True)
            m.stage(down_logits, c, dram)
            m.stage(route, c, "rd", lambda pe: down_turned(nc, c))
            m.stage(kronecker, c, False)
            m.stage(experts_output, c, scratch, out)


_INS = ['L0_attn_x', 'L0_attn_wq', 'L0_attn_bq', 'L0_attn_wk', 'L0_attn_bk', 'L0_attn_wv', 'L0_attn_bv',
        'L0_attn_wo', 'L0_attn_bo', 'L0_wmod', 'L1_wmod',
        'L0_ffn_w_gate', 'L0_ffn_w_up', 'L0_ffn_w_down', 'L0_ffn_sw_gate', 'L0_ffn_sw_up', 'L0_ffn_sw_down',
        'L1_attn_W_qkvf', 'L1_attn_W_ff1', 'L1_attn_W_ff2', 'L1_attn_ln1_g', 'L1_attn_ln1_b',
        'L1_attn_ln2_g', 'L1_attn_ln2_b', 'L1_ffn_A_up', 'L1_ffn_B_up', 'L1_ffn_A_down', 'L1_ffn_B_down',
        'L1_ffn_scale_up', 'L1_ffn_scale_down']


def layout(inputs):
    arrays = {name: np.ascontiguousarray(inputs[name]) for name in _INS}
    for name in ("L0_c", "L1_c", "L0_ffn_router_w", "L0_ffn_gate_w"):
        arrays[name] = np.ascontiguousarray(np.transpose(inputs[name]))
    for name in ("L1_attn_W_qkvf", "L1_attn_W_proj"):
        arrays[name + "_T"] = np.ascontiguousarray(np.transpose(inputs[name]))
    arrays["L1_attn_W_conv"] = np.ascontiguousarray(np.transpose(inputs["L1_attn_W_conv"], (1, 2, 0)))
    move = lambda name, shape, axes: np.ascontiguousarray(
        np.transpose(np.reshape(np.asarray(inputs[name]), shape), axes))
    arrays["L1_ffn_W_up"] = move("L1_ffn_W_up", (64, 8, D), (2, 1, 0))
    arrays["L1_ffn_W_down"] = move("L1_ffn_W_down", (64, 64, 64), (2, 1, 0))
    arrays["L1_ffn_bias_up"] = move("L1_ffn_bias_up", (64, 64), (1, 0))
    arrays["L1_ffn_bias_down"] = move("L1_ffn_bias_down", (8, D), (1, 0))
    return arrays


def kernel(**inputs):
    import concourse.bacc as bacc
    from concourse.bass_utils import run_bass_kernel_spmd

    nc = bacc.Bacc("TRN2", target_bir_lowering=False, num_devices=1)
    arrays = layout(inputs)
    dram = {name: nc.dram_tensor(f"in_{name}", a.shape, mybir.dt.from_np(a.dtype), kind="ExternalInput").ap()
            for name, a in arrays.items()}
    out = nc.dram_tensor("out_x", (B, T, D), F32, kind="ExternalOutput").ap()
    build(nc, dram, out)
    r = run_bass_kernel_spmd(nc, [{f"in_{name}": a for name, a in arrays.items()}], core_ids=[0])
    return r.results[0]["out_x"]
```

```python
from contextlib import ExitStack

import numpy as np
import concourse.bass as bass
from concourse import mybir

F32 = mybir.dt.float32
BF16 = mybir.dt.bfloat16
U32 = mybir.dt.uint32
ALU = mybir.AluOpType
ACT = mybir.ActivationFunctionType
X_AXIS = mybir.AxisListType.X

P = 128
D = 128
B, T = 4, 1024
NC = T // P
CH = B * NC
W = B * P
EPS = 1e-5
SHIFT_A, SCALE_A, GATE_A, SHIFT_B, SCALE_B, GATE_B = range(6)

def done(i, per=1, k=0):
    return i * per + k + 2


def before(i, per=1, k=0):
    return i * per + k + 1


def stored(i, per=16):
    return i * per + per


class Mem:

    def __init__(self, nc, ctx):
        self.nc, self.ctx, self.sems = nc, ctx, []

    def sb(self, name, shape, dt=F32):
        return self.ctx.enter_context(self.nc.sbuf_tensor(name, shape, dt))

    def ps(self, name, shape, dt=F32):
        return self.ctx.enter_context(self.nc.psum_tensor(name, shape, dt))

    def sem(self, name):
        handle = self.nc.alloc_semaphore(name=name)
        self.sems.append(handle)
        return handle

    def stage(self, f, *args):
        kept, self.sems = self.sems, []
        f(self.nc, self, *args)
        self.nc.clear_and_free_semaphores(self.sems)
        self.nc.all_engine_barrier()
        self.sems = kept


def at(ap, i):
    return ap[:, :, bass.ds(i, 1), :].rearrange("p a o d -> p a (o d)")


def bcast(ap, shape):
    return ap.broadcast_to(shape)


def setup(nc, m, c, dram):
    loaded, cond_loaded = m.sem("loaded"), m.sem("cond_loaded")
    silu_done, bc_done, masks = m.sem("silu_done"), m.sem("bc_done"), m.sem("masks")
    cols_mm, cols_out = m.sem("cols_mm"), m.sem("cols_out")
    rows_mm, rows_out, fix = m.sem("rows_mm"), m.sem("rows_out"), m.sem("fix")
    loads = [
        (c.WQKV[:, 0:64], dram["L0_attn_wq"]), (c.WQKV[:, 64:128], dram["L0_attn_wk"]),
        (c.WQKV[:, 128:256], dram["L0_attn_wv"]), (c.WO[:, :], dram["L0_attn_wo"]),
        (c.BQKV[:, 0:64], dram["L0_attn_bq"].partition_broadcast(P)),
        (c.BQKV[:, 64:128], dram["L0_attn_bk"].partition_broadcast(P)),
        (c.BQKV[:, 128:256], dram["L0_attn_bv"].partition_broadcast(P)),
        (c.BO[:, :], dram["L0_attn_bo"].partition_broadcast(P)),
        (c.X[:, :, :], dram["L0_attn_x"].rearrange("b (n p) d -> p (b n) d", p=P)),
    ]
    cond = [
        (c.COND[:, 0, :], dram["L0_c"]),
        (c.COND[:, 1, :], dram["L1_c"]),
        (c.WMOD[:, 0, :], dram["L0_wmod"]), (c.WMOD[:, 1, :], dram["L1_wmod"]),
    ]
    ROWS = [(l, b) for l in range(2) for b in range(B)]
    with nc.Block() as block:

        @block.sync
        def _(sp):
            for dst, src in cond:
                sp.dma_start(dst, src).then_inc(cond_loaded, 16)
            for dst, src in loads:
                sp.dma_start(dst, src).then_inc(loaded, 16)
            sp.wait_ge(loaded, 16 * len(loads))

        @block.gpsimd
        def _(pool):
            nc.gpsimd.memset(c.IDENT[:, :], 0.0).then_inc(masks, 1)
            nc.gpsimd.memset(c.ONES[:, :], 1.0).then_inc(masks, 1)
            nc.gpsimd.memset(c.HALF[:, :], -0.5)
            nc.gpsimd.memset(c.EPS[:, :], EPS)
            nc.gpsimd.iota(c.IOTA[:, :], [[1, 8]], base=0, channel_multiplier=0,
                           allow_small_or_imprecise_dtypes=True)
            nc.gpsimd.memset(c.ZERO[:, :], 0.0).then_inc(masks, 1)
            pool.wait_ge(masks, 3)
            nc.gpsimd.affine_select(out=c.IDENT[:, :], in_=c.IDENT[:, :], compare_op=ALU.not_equal,
                                    fill=1.0, base=0, pattern=[[-1, P]], channel_multiplier=1)
            nc.gpsimd.affine_select(out=c.IDENTB[:, :], in_=c.ZERO[:, :], compare_op=ALU.not_equal,
                                    fill=1.0, base=0, pattern=[[-1, P]], channel_multiplier=1)
            nc.gpsimd.affine_select(out=c.UPTO[:, :], in_=c.ONES[:, :], compare_op=ALU.is_ge,
                                    fill=0.0, base=0, pattern=[[1, P]], channel_multiplier=-1)
            nc.gpsimd.affine_select(out=c.LATER[:, :], in_=c.ZERO[:, :], compare_op=ALU.is_ge,
                                    fill=-1e30, base=0, pattern=[[-1, P]],
                                    channel_multiplier=1).then_inc(masks, 1)

        @block.scalar
        def _(act):
            act.wait_ge(cond_loaded, 16 * len(cond))
            nc.scalar.activation(c.COND[:, :, :], c.COND[:, :, :], ACT.Silu).then_inc(silu_done, 1)
            for n, (l, b) in enumerate(ROWS):
                act.wait_ge(rows_mm, n + 1)
                k = 2 * (n % 2)
                nc.scalar.copy(c.MROW[:, l, b, 0:4, :],
                               c.PS[:, k, :].rearrange("p (j d) -> p j d", d=D))
                nc.scalar.copy(c.MROW[:, l, b, 4:6, :],
                               c.PS[:, k + 1, 0:256].rearrange("p (j d) -> p j d", d=D)
                               ).then_inc(rows_out, 1)

        @block.vector
        def _(dve):
            dve.wait_ge(silu_done, 1)
            for n, (l, b) in enumerate(ROWS):
                nc.vector.tensor_copy(c.CB[:, n, :], bcast(c.COND[:, l, b:b + 1], [P, P])
                                      ).then_inc(bc_done, 1)
            dve.wait_ge(cols_mm, 1)
            nc.vector.tensor_copy(c.MCOL[:, :, :, :], c.PS[:, 4, 0:48].rearrange(
                "p (l j b) -> p l j b", l=2, j=6)).then_inc(cols_out, 1)
            dve.wait_ge(cols_out, 1)
            for j in (SCALE_A, SCALE_B):
                nc.vector.tensor_scalar_add(c.MCOL[:, :, j, :], c.MCOL[:, :, j, :], 1.0)
            dve.wait_ge(rows_out, len(ROWS))
            for j in (SCALE_A, SCALE_B):
                nc.vector.tensor_scalar_add(c.MROW[:, :, :, j, :], c.MROW[:, :, :, j, :], 1.0)
            k = 0
            for j in (GATE_A, GATE_B):
                g = c.MROW[:, :, :, j, :].rearrange("p l b d -> p (l b) d")
                nc.vector.tensor_scalar(c.CB[:, :, :], g, 0.0, 2.0, ALU.is_ge, ALU.mult).then_inc(fix, 1)
                nc.vector.tensor_scalar(c.CB2[:, :, :], g, -1.0, None, ALU.mult).then_inc(fix, 1)
                dve.wait_ge(fix, k + 2)
                nc.vector.tensor_scalar_add(c.CB[:, :, :], c.CB[:, :, :], -1.0).then_inc(fix, 1)
                nc.vector.tensor_tensor(c.CB2[:, :, :], c.CB2[:, :, :], g, ALU.max).then_inc(fix, 1)
                dve.wait_ge(fix, k + 4)
                nc.vector.scalar_tensor_tensor(g, c.CB2[:, :, :], 0.25, c.CB[:, :, :], ALU.max,
                                               ALU.mult).then_inc(fix, 1)
                dve.wait_ge(fix, k + 5)
                k += 5

        @block.tensor
        def _(pe):
            pe.wait_ge(silu_done, 1)
            for l in range(2):
                for j in range(6):
                    o = (l * 6 + j) * B
                    last = nc.tensor.matmul(c.PS[:, 4, o:o + B], c.WMOD[:, l, j * D:(j + 1) * D],
                                            c.COND[:, l, :], start=True, stop=True)
            last.then_inc(cols_mm, 1)
            for n, (l, b) in enumerate(ROWS):
                pe.wait_ge(bc_done, n + 1)
                if n >= 2:
                    pe.wait_ge(rows_out, n - 1)
                k = 2 * (n % 2)
                nc.tensor.matmul(c.PS[:, k, :], c.CB[:, n, :], c.WMOD[:, l, 0:512], start=True, stop=True)
                nc.tensor.matmul(c.PS[:, k + 1, 0:256], c.CB[:, n, :], c.WMOD[:, l, 512:768],
                                 start=True, stop=True).then_inc(rows_mm, 1)


HALF_BATCHES = ((0, slice(0, 2), (0, 1)), (1, slice(2, 4), (2, 3)))


def ln_stats(nc, dve, c, s, src, i):
    for _, _, batches in HALF_BATCHES:
        for b in batches:
            ins = nc.vector.bn_stats(c.ST[:, b, :], src(b))
        ins.then_inc(s.stats, 1)
    for h, _, batches in HALF_BATCHES:
        dve.wait_ge(s.stats, done(i, 2, h))
        dve.sem_inc(c.passed, 1)
        for b in batches:
            ins = nc.vector.bn_aggr(c.MV[:, b, :], c.ST[:, b, :])
        ins.then_inc(s.moments, 1)


def ln_rstd(nc, pool, c, s, i):
    for h, half, _ in HALF_BATCHES:
        pool.wait_ge(s.moments, done(i, 2, h))
        nc.gpsimd.tensor_tensor(c.VE[:, half], c.MV[:, half, 1], c.EPS[:, half], ALU.add).then_inc(s.var_eps, 1)
        pool.wait_ge(s.var_eps, done(i, 2, h))
        nc.gpsimd.tensor_tensor(c.RSTD[:, half], c.VE[:, half], c.HALF[:, half], ALU.pow).then_inc(s.rstd, 1)


def ln_apply(nc, dve, c, s, src, dst, i):
    for h, _, batches in HALF_BATCHES:
        dve.wait_ge(s.rstd, done(i, 2, h))
        for b in batches:
            ins = nc.vector.tensor_scalar(dst(b), src(b), c.MV[:, b, 0:1], c.RSTD[:, b:b + 1],
                                          ALU.subtract, ALU.mult)
        ins.then_inc(s.normed, 1)


def turn_half(nc, c, bank, offset, src, batches):
    for n, b in enumerate(batches):
        ins = nc.tensor.transpose(c.PS[:, bank, offset + n * P:offset + (n + 1) * P], src[:, b, :], c.IDENT[:, :])
    return ins


def one_ahead(engine, front, back):
    front(0)
    with engine.Fori(0, NC - 1) as i:
        front(i + 1)
        back(i)
    back(NC - 1)


class LnSems:
    def __init__(self, m, tag):
        self.stats, self.moments = m.sem(tag + "_stats"), m.sem(tag + "_moments")
        self.var_eps, self.rstd = m.sem(tag + "_var_eps"), m.sem(tag + "_rstd")
        self.normed = m.sem(tag + "_normed")

    def dve(self):
        return [self.stats, self.moments, self.normed]

    def pool(self):
        return [self.var_eps, self.rstd]


def credit(engine, sems):
    for s in sems:
        engine.sem_inc(s, 1)


def linear_attention(nc, m, c):
    H, F, G = 16, 4, 8
    KV = H * F * G
    ln = LnSems(m, "la")
    turned, h_ready, qkv_mm, qkv_out = (m.sem("la_" + n) for n in ("turned", "h_ready", "qkv_mm", "qkv_out"))
    neg_done, exp_done, phi_done = (m.sem("la_" + n) for n in ("neg", "exp", "phi"))
    kv_dve, kv_pool, cum_mm, sum_done = (m.sem("la_" + n) for n in ("kv_dve", "kv_pool", "cum_mm", "sum"))
    prod_done, red_done, den_done, rec_done, o_done = (
        m.sem("la_" + n) for n in ("prod", "red", "den", "rec", "o"))
    o_turned, o_out, proj_mm, y_done, gated, res_done = (
        m.sem("la_" + n) for n in ("o_turned", "o_out", "proj", "y", "gated", "res"))
    X4 = c.X[:, :, :].rearrange("p (b n) d -> p b n d", b=B)
    two = lambda h, o, n: c.PS[:, h, o:o + 2 * n].rearrange("p (b n) -> p b n", b=2)

    def kv_product(engine, b):
        k = c.PHI[:, b, 64:128].rearrange("p (h f) -> p h f", f=F).unsqueeze(3)
        v = c.QKV[:, b, 128:256].rearrange("p (h g) -> p h g", g=G).unsqueeze(2)
        return engine.tensor_tensor(c.KVP[:, b, :].rearrange("p (h f g) -> p h f g", h=H, f=F),
                                    bcast(k, [P, H, F, G]), bcast(v, [P, H, F, G]), ALU.mult)

    with nc.Block() as block:

        @block.vector
        def _(dve):
            credit(dve, ln.dve() + [qkv_out, neg_done, phi_done, kv_dve, prod_done, red_done,
                                    den_done, rec_done, o_done, y_done])
            with dve.Fori(0, NC) as i:
                xi = at(X4, i)
                ln_stats(nc, dve, c, ln, lambda b: xi[:, b, :], i)
                ln_apply(nc, dve, c, ln, lambda b: xi[:, b, :], lambda b: c.XN[:, b, :], i)
                for h, half, batches in HALF_BATCHES:
                    dve.wait_ge(qkv_mm, done(i, 2, h))
                    nc.vector.tensor_tensor(c.QKV[:, half, :], two(2 * h + 1, 0, 256),
                                            bcast(c.BQKV[:, :].unsqueeze(1), [P, 2, 256]), ALU.add
                                            ).then_inc(qkv_out, 1)
                    dve.wait_ge(qkv_out, done(i, 2, h))
                    nc.vector.tensor_scalar(c.NEG[:, half, :], c.QKV[:, half, 0:128], 0.0, None, ALU.min
                                            ).then_inc(neg_done, 1)
                for h, half, batches in HALF_BATCHES:
                    dve.wait_ge(exp_done, done(i, 2, h))
                    nc.vector.scalar_tensor_tensor(c.PHI[:, half, :], c.QKV[:, half, 0:128], 0.0, c.NEG[:, half, :],
                                                   ALU.max, ALU.add).then_inc(phi_done, 1)
                    dve.wait_ge(phi_done, done(i, 2, h))
                    kv_product(nc.vector, batches[0]).then_inc(kv_dve, 1)
                for h, half, batches in HALF_BATCHES:
                    dve.wait_ge(cum_mm, done(i, 2, h))
                    for b in batches:
                        q = c.PHI[:, b, 0:64].rearrange("p (h f) -> p h f", f=F).unsqueeze(3)
                        nc.vector.tensor_tensor(
                            c.PROD[:, b, :].rearrange("p (h f g) -> p h f g", h=H, f=F),
                            c.PS[:, 4 + b, :].rearrange("p (h f g) -> p h f g", h=H, f=F),
                            bcast(q, [P, H, F, G]), ALU.mult)
                    nc.vector.tensor_tensor(c.KPROD[:, half, :], two(2 * h, 0, 64), c.PHI[:, half, 0:64], ALU.mult
                                            ).then_inc(prod_done, 1)
                    dve.wait_ge(prod_done, done(i, 2, h))
                    den = slice(h * 2 * H, (h + 1) * 2 * H)
                    nc.vector.tensor_reduce(c.DEN[:, den], c.KPROD[:, half, :].rearrange(
                        "p b (h f) -> p (b h) f", f=F), X_AXIS, ALU.add).then_inc(red_done, 1)
                    for b in batches:
                        last = nc.vector.tensor_reduce(
                            c.NUM[:, b, :], c.PROD[:, b, :].rearrange("p (h f g) -> p h g f", h=H, f=F),
                            X_AXIS, ALU.add)
                    last.then_inc(red_done, 1)
                    dve.wait_ge(red_done, done(i, 4, 2 * h))
                    nc.vector.tensor_scalar_add(c.DEN[:, den], c.DEN[:, den], 1e-6).then_inc(den_done, 1)
                    dve.wait_ge(den_done, done(i, 2, h))
                    nc.vector.reciprocal(c.REC[:, den], c.DEN[:, den]).then_inc(rec_done, 1)
                    dve.wait_ge(rec_done, done(i, 2, h))
                    dve.wait_ge(red_done, done(i, 4, 2 * h + 1))
                    nc.vector.tensor_tensor(c.O[:, half, :].rearrange("p b (h g) -> p (b h) g", g=G),
                                            c.NUM[:, half, :].rearrange("p b (h g) -> p (b h) g", g=G),
                                            bcast(c.REC[:, den].unsqueeze(2), [P, 2 * H, G]), ALU.mult
                                            ).then_inc(o_done, 1)
                for h, half, batches in HALF_BATCHES:
                    dve.wait_ge(proj_mm, done(i, 2, h))
                    nc.vector.tensor_tensor(c.Y[:, half, :], two(2 * h + 1, 0, D),
                                            bcast(c.BO[:, :].unsqueeze(1), [P, 2, D]), ALU.add
                                            ).then_inc(y_done, 1)

        @block.gpsimd
        def _(pool):
            credit(pool, ln.pool() + [kv_pool, gated, res_done])
            nc.gpsimd.memset(c.KVSUM[:, :, :], 0.0)
            nc.gpsimd.memset(c.KSUM[:, :, :], 0.0).then_inc(sum_done, 2)
            with pool.Fori(0, NC) as i:
                ln_rstd(nc, pool, c, ln, i)
                for h, half, batches in HALF_BATCHES:
                    pool.wait_ge(phi_done, done(i, 2, h))
                    kv_product(nc.gpsimd, batches[1]).then_inc(kv_pool, 1)
                for h, half, batches in HALF_BATCHES:
                    pool.wait_ge(kv_pool, done(i, 2, h))
                    pool.wait_ge(kv_dve, done(i, 2, h))
                    pool.wait_ge(cum_mm, done(i, 2, h))
                    nc.gpsimd.tensor_tensor(c.KVSUM[:, half, :], c.KVSUM[:, half, :], c.KVP[:, half, :], ALU.add)
                    nc.gpsimd.tensor_tensor(c.KSUM[:, half, :], c.KSUM[:, half, :], c.PHI[:, half, 64:128], ALU.add
                                            ).then_inc(sum_done, 1)
                xi = at(X4, i)
                for h, half, batches in HALF_BATCHES:
                    pool.wait_ge(y_done, done(i, 2, h))
                    nc.gpsimd.tensor_tensor(c.Y[:, half, :], c.Y[:, half, :], c.MROW[:, 0, half, GATE_A, :], ALU.mult
                                            ).then_inc(gated, 1)
                    pool.wait_ge(gated, done(i, 2, h))
                    nc.gpsimd.tensor_tensor(xi[:, half, :], xi[:, half, :], c.Y[:, half, :], ALU.add
                                            ).then_inc(res_done, 1)

        @block.scalar
        def _(act):
            credit(act, [h_ready, exp_done, o_out])
            with act.Fori(0, NC) as i:
                for h, half, batches in HALF_BATCHES:
                    act.wait_ge(turned, done(i, 2, h))
                    for n, b in enumerate(batches):
                        last = nc.scalar.activation(c.HT[:, b, :], c.PS[:, 2 * h, n * P:(n + 1) * P], ACT.Identity,
                                                    scale=c.MCOL[:, 0, SCALE_A, b:b + 1],
                                                    bias=c.MCOL[:, 0, SHIFT_A, b:b + 1])
                    last.then_inc(h_ready, 1)
                for h, half, batches in HALF_BATCHES:
                    act.wait_ge(neg_done, done(i, 2, h))
                    nc.scalar.activation(c.NEG[:, half, :], c.NEG[:, half, :], ACT.Exp).then_inc(exp_done, 1)
                for h, half, batches in HALF_BATCHES:
                    act.wait_ge(o_turned, done(i, 2, h))
                    nc.scalar.copy(c.OT[:, half, :], two(2 * h, 256, P)).then_inc(o_out, 1)

        @block.tensor
        def _(pe):
            credit(pe, [turned, qkv_mm, cum_mm, o_turned, proj_mm])
            with pe.Fori(0, NC) as i:
                for h, half, batches in HALF_BATCHES:
                    pe.wait_ge(ln.normed, done(i, 2, h))
                    turn_half(nc, c, 2 * h, 0, c.XN, batches).then_inc(turned, 1)
                for h, half, batches in HALF_BATCHES:
                    pe.wait_ge(h_ready, done(i, 2, h))
                    for n, b in enumerate(batches):
                        last = nc.tensor.matmul(c.PS[:, 2 * h + 1, 256 * n:256 * n + 256], c.HT[:, b, :],
                                                c.WQKV[:, :], start=True, stop=True)
                    last.then_inc(qkv_mm, 1)
                for h, half, batches in HALF_BATCHES:
                    pe.wait_ge(sum_done, i * 2 + (h + 1))
                    pe.wait_ge(phi_done, done(i, 2, h))
                    kp = c.PS[:, 2 * h, 0:128]
                    nc.tensor.matmul(kp, c.UPTO[:, :], c.PHI[:, half, 64:128], start=True, stop=False)
                    nc.tensor.matmul(kp, c.ONES[:, :], c.KSUM[:, half, :], start=False, stop=True)
                    pe.wait_ge(kv_dve, done(i, 2, h))
                    pe.wait_ge(kv_pool, done(i, 2, h))
                    for b in batches:
                        nc.tensor.matmul(c.PS[:, 4 + b, :], c.UPTO[:, :], c.KVP[:, b, :], start=True, stop=False)
                        last = nc.tensor.matmul(c.PS[:, 4 + b, :], c.ONES[:, :], c.KVSUM[:, b, :],
                                                start=False, stop=True)
                    last.then_inc(cum_mm, 1)
                for h, half, batches in HALF_BATCHES:
                    pe.wait_ge(o_done, done(i, 2, h))
                    turn_half(nc, c, 2 * h, 256, c.O, batches).then_inc(o_turned, 1)
                for h, half, batches in HALF_BATCHES:
                    pe.wait_ge(o_out, done(i, 2, h))
                    for n, b in enumerate(batches):
                        last = nc.tensor.matmul(c.PS[:, 2 * h + 1, n * P:(n + 1) * P], c.OT[:, b, :], c.WO[:, :],
                                                start=True, stop=True)
                    last.then_inc(proj_mm, 1)


NE0, F0 = 8, 256


def load_experts(nc, m, c, dram):
    w = m.sem("experts_loaded")
    return w, [
        (c.WR[:, 0:8], dram["L0_ffn_router_w"]), (c.WR[:, 8:9], dram["L0_ffn_gate_w"]),
        (c.WG[:, 0:NE0, :], dram["L0_ffn_w_gate"].rearrange("e d f -> d e f")),
        (c.WU[:, 0:NE0, :], dram["L0_ffn_w_up"].rearrange("e d f -> d e f")),
        (c.WD[:, 0:NE0, :, :], dram["L0_ffn_w_down"].rearrange("e (k p) d -> p e k d", p=P)),
        (c.WG[:, NE0, :], dram["L0_ffn_sw_gate"]), (c.WU[:, NE0, :], dram["L0_ffn_sw_up"]),
        (c.WD[:, NE0, :, :], dram["L0_ffn_sw_down"].rearrange("(k p) d -> p k d", p=P)),
    ]


def experts(nc, m, c, dram):
    NE = NE0 + 1
    ln = LnSems(m, "ex")
    turned, h_ready, logit_mm, logit_out = (m.sem("ex_" + n) for n in ("turned", "h_ready", "logit_mm", "logit_out"))
    top_done, idx_done, idx_f, shifted, exp_done = (
        m.sem("ex_" + n) for n in ("top", "idx", "idx_f", "shifted", "exp"))
    hot, sum_done, rec_done, cw_done = (m.sem("ex_" + n) for n in ("hot", "sum", "rec", "cw"))
    gate_mm, up_mm, silu_done, mul_done, down_mm, acc_done = (
        m.sem("ex_" + n) for n in ("gate_mm", "up_mm", "silu", "mul", "down_mm", "acc"))
    y_done, res_done = m.sem("ex_y"), m.sem("ex_res")
    X4 = c.X[:, :, :].rearrange("p (b n) d -> p b n d", b=B)
    HT = c.HT[:, :, :].rearrange("p b t -> p (b t)")
    loaded, loads = load_experts(nc, m, c, dram)

    with nc.Block() as block:

        @block.sync
        def _(sp):
            for dst, src in loads:
                sp.dma_start(dst, src).then_inc(loaded, 16)

        @block.vector
        def _(dve):
            credit(dve, ln.dve() + [logit_out, top_done, idx_done, idx_f, shifted, hot, sum_done,
                                    rec_done, cw_done, mul_done, acc_done, y_done])
            with dve.Fori(0, NC) as i:
                xi = at(X4, i)
                ln_stats(nc, dve, c, ln, lambda b: xi[:, b, :], i)
                ln_apply(nc, dve, c, ln, lambda b: xi[:, b, :], lambda b: c.XN[:, b, :], i)
                dve.wait_ge(logit_mm, done(i))
                nc.vector.tensor_copy(c.LG[:, :, :], c.PS[:, 7, 0:64].rearrange("p (b e) -> p b e", b=B)[:, :, 0:9]
                                      ).then_inc(logit_out, 1)
                dve.wait_ge(logit_out, done(i))
                dve.sem_inc(c.passed, 1)
                for b in range(B):
                    last = nc.vector.max(c.TOP[:, b, :], c.LG[:, b, 0:8])
                last.then_inc(top_done, 1)
                dve.wait_ge(top_done, done(i))
                nc.vector.tensor_tensor(c.EX[:, :, 0:8], c.LG[:, :, 0:8], bcast(c.TOP[:, :, 0:1], [P, B, 8]),
                                        ALU.subtract)
                nc.vector.tensor_scalar(c.EX[:, :, 8:9], c.LG[:, :, 8:9], -1.0, None, ALU.mult
                                        ).then_inc(shifted, 1)
                for b in range(B):
                    last = nc.vector.max_index(c.TIX[:, b, :], c.TOP[:, b, :], c.LG[:, b, 0:8])
                last.then_inc(idx_done, 1)
                dve.wait_ge(idx_done, done(i))
                nc.vector.tensor_copy(c.TIF[:, :, :], c.TIX[:, :, 0:2]).then_inc(idx_f, 1)
                dve.wait_ge(idx_f, done(i))
                for k in range(2):
                    last = nc.vector.tensor_tensor(c.HOT[:, k, :, :], bcast(c.IOTA[:, :].unsqueeze(1), [P, B, 8]),
                                                   bcast(c.TIF[:, :, k:k + 1], [P, B, 8]), ALU.is_equal)
                last.then_inc(hot, 1)
                dve.wait_ge(hot, done(i))
                dve.wait_ge(exp_done, done(i))
                nc.vector.tensor_reduce(c.SUM[:, :, 0:1], c.EX[:, :, 0:8], X_AXIS, ALU.add)
                nc.vector.tensor_scalar_add(c.SUM[:, :, 1:2], c.EX[:, :, 8:9], 1.0)
                nc.vector.tensor_tensor(c.HOT[:, 0, :, :], c.HOT[:, 0, :, :], c.HOT[:, 1, :, :], ALU.add
                                        ).then_inc(sum_done, 1)
                dve.wait_ge(sum_done, done(i))
                nc.vector.reciprocal(c.RS[:, :, :], c.SUM[:, :, :])
                nc.vector.tensor_tensor(c.HOT[:, 0, :, :], c.HOT[:, 0, :, :], c.EX[:, :, 0:8], ALU.mult
                                        ).then_inc(rec_done, 1)
                dve.wait_ge(rec_done, done(i))
                nc.vector.tensor_tensor(c.CW[:, :, 0:8], c.HOT[:, 0, :, :], bcast(c.RS[:, :, 0:1], [P, B, 8]),
                                        ALU.mult)
                nc.vector.tensor_copy(c.CW[:, :, 8:9], c.RS[:, :, 1:2]).then_inc(cw_done, 1)

                def accumulate(e):
                    dve.wait_ge(down_mm, done(i, NE, e))
                    if e == 0:
                        dve.wait_ge(cw_done, done(i))
                    else:
                        dve.wait_ge(acc_done, done(i, NE, e - 1))
                    for b in range(B):
                        y = c.PS[:, 6, b * P:(b + 1) * P]
                        if e == 0:
                            last = nc.vector.tensor_scalar(c.Y[:, b, :], y, c.CW[:, b, e:e + 1], None, ALU.mult)
                        else:
                            last = nc.vector.scalar_tensor_tensor(c.Y[:, b, :], y, c.CW[:, b, e:e + 1],
                                                                  c.Y[:, b, :], ALU.mult, ALU.add)
                    last.then_inc(acc_done, 1)

                for e in range(NE):
                    dve.wait_ge(silu_done, done(i, NE, e))
                    dve.wait_ge(up_mm, done(i, NE, e))
                    nc.vector.tensor_tensor(c.HH[:, e % 2, :, :], c.PS[:, 4:6, :], c.SG[:, e % 2, :, :],
                                            ALU.mult).then_inc(mul_done, 1)
                    if e >= 1:
                        accumulate(e - 1)
                accumulate(NE - 1)
                dve.wait_ge(acc_done, done(i, NE, NE - 1))
                nc.vector.tensor_tensor(c.Y[:, :, :], c.Y[:, :, :], c.MROW[:, 0, :, GATE_B, :], ALU.mult
                                        ).then_inc(y_done, 1)
                dve.wait_ge(y_done, done(i))
                nc.vector.tensor_tensor(xi, xi, c.Y[:, :, :], ALU.add)

        @block.gpsimd
        def _(pool):
            credit(pool, ln.pool())
            with pool.Fori(0, NC) as i:
                ln_rstd(nc, pool, c, ln, i)

        @block.scalar
        def _(act):
            credit(act, [h_ready, exp_done, silu_done])
            with act.Fori(0, NC) as i:
                act.wait_ge(turned, done(i))
                for b in range(B):
                    last = nc.scalar.activation(c.HT[:, b, :], c.PS[:, 6, b * P:(b + 1) * P], ACT.Identity,
                                                scale=c.MCOL[:, 0, SCALE_B, b:b + 1],
                                                bias=c.MCOL[:, 0, SHIFT_B, b:b + 1])
                last.then_inc(h_ready, 1)
                act.wait_ge(shifted, done(i))
                nc.scalar.activation(c.EX[:, :, :], c.EX[:, :, :], ACT.Exp).then_inc(exp_done, 1)
                for e in range(NE):
                    act.wait_ge(gate_mm, done(i, NE, e))
                    k = 2 * (e % 2)
                    if e >= 2:
                        act.wait_ge(mul_done, done(i, NE, e - 2))
                    nc.scalar.activation(c.SG[:, e % 2, :, :], c.PS[:, k:k + 2, :], ACT.Silu
                                         ).then_inc(silu_done, 1)

        @block.tensor
        def _(pe):
            credit(pe, [turned, logit_mm, gate_mm, up_mm, down_mm])
            pe.wait_ge(loaded, 16 * len(loads))
            with pe.Fori(0, NC) as i:
                pe.wait_ge(ln.normed, done(i, 2, 1))
                for b in range(B):
                    last = nc.tensor.transpose(c.PS[:, 6, b * P:(b + 1) * P], c.XN[:, b, :], c.IDENT[:, :])
                last.then_inc(turned, 1)
                pe.wait_ge(h_ready, done(i))
                for b in range(B):
                    last = nc.tensor.matmul(c.PS[:, 7, 16 * b:16 * b + 9], c.HT[:, b, :], c.WR[:, :],
                                            start=True, stop=True)
                last.then_inc(logit_mm, 1)

                def down(e):
                    pe.wait_ge(mul_done, done(i, NE, e))
                    if e:
                        pe.wait_ge(acc_done, done(i, NE, e - 1))
                    for b in range(B):
                        for k in range(2):
                            last = nc.tensor.matmul(c.PS[:, 6, b * P:(b + 1) * P],
                                                    c.HH[:, e % 2, k, b * P:(b + 1) * P], c.WD[:, e, k, :],
                                                    start=(k == 0), stop=(k == 1))
                    last.then_inc(down_mm, 1)

                for e in range(NE):
                    if e >= 2:
                        pe.wait_ge(silu_done, done(i, NE, e - 2))
                    for k in range(2):
                        last = nc.tensor.matmul(c.PS[:, 2 * (e % 2) + k, :], c.WG[:, e, k * P:(k + 1) * P], HT,
                                                start=True, stop=True)
                    last.then_inc(gate_mm, 1)
                    if e >= 1:
                        pe.wait_ge(mul_done, done(i, NE, e - 1))
                    for k in range(2):
                        last = nc.tensor.matmul(c.PS[:, 4 + k, :], c.WU[:, e, k * P:(k + 1) * P], HT,
                                                start=True, stop=True)
                    last.then_inc(up_mm, 1)
                    if e >= 1:
                        down(e - 1)
                down(NE - 1)


H1, HS, NF = 16, 8, 4
GH = 4
NG = H1 // GH
ROW_Q = (0, 0, 1, 1, 0, 2)
ROW_K = (0, 1, 0, 1, 2, 0)
NT = len(ROW_Q)
NS = 3
KM = 96
KA = KM + NS


def attention_inputs(nc, m, c, dram, scratch):
    lx, lh = LnSems(m, "ax"), LnSems(m, "ah")
    loaded, mask_done, bd_done = m.sem("ai_loaded"), m.sem("ai_mask"), m.sem("ai_bd")
    g_mm, g_out, big_mm, big_out = (m.sem("ai_" + n) for n in ("g_mm", "g_out", "big_mm", "big_out"))
    scaled, h_done, h_stored = m.sem("ai_scaled"), m.sem("ai_h"), m.sem("ai_h_stored")
    turned, z_ready, qk_mm, qk_out = (m.sem("ai_" + n) for n in ("turned", "z", "qk_mm", "qk_out"))
    rest1, part2, part3, parts_stored = (m.sem("ai_" + n) for n in ("rest1", "part2", "part3", "parts_stored"))
    tok_mm, qv_out, vf_out, vf_stored = (m.sem("ai_" + n) for n in ("tok_mm", "qv_out", "vf_out", "vf_stored"))
    prod_done, logit_done, v_kept, fmax_done = (m.sem("ai_" + n) for n in ("prod", "logit", "v_kept", "fmax"))
    X4 = c.X[:, :, :].rearrange("p (b n) d -> p b n d", b=B)
    V4 = c.VT[:, :, :].rearrange("p (b n) d -> p b n d", b=B)
    F4 = c.FUT[:, :, :].rearrange("p (b n) d -> p b n d", b=B)
    M4 = c.FMAX[:, :, :].rearrange("p (b n) d -> p b n d", b=B)
    ZT = c.HT[:, :, :].rearrange("p b t -> p (b t)")
    BANKS = ((3, 4, 5), (6, 7, 0))
    conv = dram["L1_attn_W_conv"]
    loads = [(c.WT[:, :], dram["L1_attn_W_qkvf_T"]), (c.WF[:, :], dram["L1_attn_W_qkvf"][3 * D:4 * D, :]),
             (c.LNG[:, 0:1], dram["L1_attn_ln1_g"].rearrange("(d o) -> d o", o=1)),
             (c.LNG[:, 1:2], dram["L1_attn_ln1_b"].rearrange("(d o) -> d o", o=1)),
             (c.LNG[:, 2:3], dram["L1_attn_ln2_g"].rearrange("(d o) -> d o", o=1)),
             (c.LNG[:, 3:4], dram["L1_attn_ln2_b"].rearrange("(d o) -> d o", o=1))]
    loads += [(c.CV[HS * h:HS * h + HS, :, :], conv) for h in range(H1)]

    with nc.Block() as block:

        @block.sync
        def _(sp):
            for dst, src in loads:
                sp.dma_start(dst, src).then_inc(loaded, 16)
            for s in (h_stored, parts_stored, vf_stored):
                sp.sem_inc(s, 16)

            def front(i):
                sp.wait_ge(h_done, done(i, 2, 1))
                sp.dma_start(scratch.h[:, bass.ds(i, 1), :, :].rearrange("b o p d -> p b (o d)"), c.H[:, :, :]
                             ).then_inc(h_stored, 16)

            def back(i):
                sp.wait_ge(part3, done(i))
                sp.dma_start(scratch.qk[:, :, bass.ds(i * P, P)], c.PARTS[:, :, :]).then_inc(parts_stored, 16)
                sp.wait_ge(vf_out, done(i, B, B - 1))
                sp.dma_start(scratch.vf[:, bass.ds(i, 1), :, :].rearrange("b o p n -> p b (o n)"), c.VF[:, :, :]
                             ).then_inc(vf_stored, 16)
            one_ahead(sp, front, back)
            sp.wait_ge(h_stored, 16 * NC + 16)
            sp.wait_ge(parts_stored, 16 * NC + 16)
            sp.wait_ge(vf_stored, 16 * NC + 16)

        @block.vector
        def _(dve):
            credit(dve, lx.dve() + lh.dve() + [scaled, h_done, rest1, prod_done, logit_done, fmax_done])
            dve.wait_ge(loaded, 16 * len(loads))
            dve.wait_ge(mask_done, 3)
            for f in range(NF):
                last = nc.vector.tensor_tensor(
                    c.BD[:, f, :].rearrange("p (h c) -> p h c", c=HS),
                    bcast(c.CV[:, f, :].unsqueeze(1), [P, H1, HS]),
                    c.BLOCKS[:, :].rearrange("p (h c) -> p h c", c=HS), ALU.mult)
            last.then_inc(bd_done, 1)
            dve.wait_ge(g_mm, 1)
            nc.vector.tensor_copy(c.GK[:, :, :], c.PS[:, 0:2, :].rearrange("p k (f n) -> p (k f) n", n=256)
                                  ).then_inc(g_out, 1)
            dve.wait_ge(big_mm, 1)
            nc.vector.tensor_copy(c.BIG[:, :, :], c.PS[:, 2:4, :].rearrange("p k (f n) -> p (k f) n", n=256)
                                  ).then_inc(big_out, 1)

            def front(i):
                xi = at(X4, i)
                ln_stats(nc, dve, c, lx, lambda b: xi[:, b, :], i)
                ln_apply(nc, dve, c, lx, lambda b: xi[:, b, :], lambda b: c.XN[:, b, :], i)
                for h, half, _ in HALF_BATCHES:
                    dve.wait_ge(lx.normed, done(i, 2, h))
                    nc.vector.tensor_tensor(c.Y[:, half, :], c.XN[:, half, :], c.MROW[:, 1, half, SCALE_A, :],
                                            ALU.mult).then_inc(scaled, 1)
                dve.wait_ge(h_stored, stored(i))
                for h, half, _ in HALF_BATCHES:
                    dve.wait_ge(scaled, done(i, 2, h))
                    nc.vector.tensor_tensor(c.H[:, half, :], c.Y[:, half, :], c.MROW[:, 1, half, SHIFT_A, :],
                                            ALU.add).then_inc(h_done, 1)
                dve.wait_ge(h_done, done(i, 2, 1))
                ln_stats(nc, dve, c, lh, lambda b: c.H[:, b, :], i)
                dve.wait_ge(turned, before(i, 2))
                ln_apply(nc, dve, c, lh, lambda b: c.H[:, b, :], lambda b: c.O[:, b, :], i)

            def back(i):
                dve.wait_ge(qk_out, done(i))
                nc.vector.tensor_tensor(c.QKF[:, :, :], c.QKF[:, :, :], c.PARTS[:, 0:8, :], ALU.subtract
                                        ).then_inc(rest1, 1)
                for b in range(B):
                    dve.wait_ge(tok_mm, done(i, B, b))
                    dve.wait_ge(qv_out, done(i, B, b))
                    q = c.QV[:, b, 0:D].unsqueeze(1)
                    nc.vector.tensor_tensor(c.FP[:, b, :, :], c.PS[:, BANKS[b % 2][1], :].rearrange(
                        "p (f n) -> p f n", f=NF), bcast(q, [P, NF, D]), ALU.mult).then_inc(prod_done, 1)
                dve.wait_ge(prod_done, done(i, B, B - 1))
                fi = at(F4, i)
                for b in range(B):
                    last = nc.vector.tensor_reduce(fi[:, b, :], c.FP[:, b, :, :].rearrange(
                        "p f (h d) -> p (f h) d", d=HS), X_AXIS, ALU.add)
                last.then_inc(logit_done, 1)
                dve.wait_ge(logit_done, done(i))
                mi = at(M4, i)
                for b in range(B):
                    last = nc.vector.tensor_reduce(mi[:, b, :], fi[:, b, :].rearrange("p (f h) -> p h f", f=NF),
                                                   X_AXIS, ALU.max)
                last.then_inc(fmax_done, 1)

            one_ahead(dve, front, back)

        @block.gpsimd
        def _(pool):
            credit(pool, lx.pool() + lh.pool() + [part2, part3, v_kept])
            nc.gpsimd.memset(c.BLOCKS[:, :], 1.0).then_inc(mask_done, 1)
            blocks = c.BLOCKS[:, :].rearrange("p (h c) -> p h c", c=HS)
            for n, (base, step, mult) in enumerate(((0, -HS, 1), (HS - 1, HS, -1))):
                pool.wait_ge(mask_done, n + 1)
                nc.gpsimd.affine_select(out=blocks, in_=blocks, compare_op=ALU.is_ge, fill=0.0, base=base,
                                        pattern=[[step, H1], [0, HS]], channel_multiplier=mult
                                        ).then_inc(mask_done, 1)

            def front(i):
                ln_rstd(nc, pool, c, lx, i)
                ln_rstd(nc, pool, c, lh, i)

            def back(i):
                pool.wait_ge(rest1, done(i))
                pool.sem_inc(c.passed, 1)
                nc.gpsimd.tensor_copy(c.PARTS[:, 8:16, :], c.QKF[:, :, :]).then_inc(part2, 1)
                pool.wait_ge(part2, done(i))
                nc.gpsimd.tensor_tensor(c.PARTS[:, 16:24, :], c.QKF[:, :, :], c.PARTS[:, 8:16, :], ALU.subtract
                                        ).then_inc(part3, 1)
                pool.wait_ge(qv_out, done(i, B, B - 1))
                pool.sem_inc(c.passed, 1)
                nc.gpsimd.tensor_copy(at(V4, i), c.QV[:, :, D:2 * D]).then_inc(v_kept, 1)

            one_ahead(pool, front, back)

        @block.scalar
        def _(act):
            credit(act, [z_ready, qk_out, qv_out, vf_out])
            act.wait_ge(loaded, 16 * len(loads))
            with act.Fori(0, NC) as i:
                for h, half, _ in HALF_BATCHES:
                    act.wait_ge(turned, done(i, 2, h))
                    nc.scalar.activation(ZT[:, h * 256:h * 256 + 256], c.PS[:, h, 0:256], ACT.Identity,
                                         scale=c.LNG[:, 0:1], bias=c.LNG[:, 1:2]).then_inc(z_ready, 1)
                act.wait_ge(qk_mm, done(i))
                act.wait_ge(parts_stored, stored(i))
                for n, scale in enumerate((HS ** -0.5, 1.0)):
                    flat = c.QKF[:, 4 * n:4 * n + 4, :].rearrange("p b t -> p (b t)")
                    part = c.PARTS[:, 4 * n:4 * n + 4, :].rearrange("p b t -> p (b t)")
                    nc.scalar.mul(flat, c.PS[:, 1 + n, :], scale)
                    last = nc.scalar.mul(part, c.PS[:, 1 + n, :], scale)
                last.then_inc(qk_out, 1)
                act.wait_ge(vf_stored, stored(i))
                act.wait_ge(v_kept, before(i))
                for b in range(B):
                    act.wait_ge(tok_mm, done(i, B, b))
                    bank = BANKS[b % 2]
                    nc.scalar.copy(c.QV[:, b, :], c.PS[:, bank[0], 0:2 * D]).then_inc(qv_out, 1)
                    nc.scalar.copy(c.VF[:, b, :], c.PS[:, bank[2], :]).then_inc(vf_out, 1)

        @block.tensor
        def _(pe):
            credit(pe, [turned, qk_mm, tok_mm])
            pe.wait_ge(bd_done, 1)
            for f in range(NF):
                last = nc.tensor.matmul(c.PS[:, f // 2, 256 * (f % 2):256 * (f % 2) + 256], c.BD[:, f, :],
                                        c.WT[:, D:3 * D], start=True, stop=True)
            last.then_inc(g_mm, 1)
            pe.wait_ge(g_out, 1)
            for f in range(NF):
                last = nc.tensor.matmul(c.PS[:, 2 + f // 2, 256 * (f % 2):256 * (f % 2) + 256], c.WF[:, :],
                                        c.GK[:, f, :], start=True, stop=True)
            last.then_inc(big_mm, 1)
            pe.wait_ge(big_out, 1)
            with pe.Fori(0, NC) as i:
                pe.wait_ge(vf_out, before(i, B, 0))
                pe.wait_ge(qk_out, before(i))
                for h, _, batches in HALF_BATCHES:
                    pe.wait_ge(lh.normed, done(i, 2, h))
                    turn_half(nc, c, h, 0, c.O, batches).then_inc(turned, 1)
                pe.wait_ge(z_ready, done(i, 2, 1))
                for n in range(2):
                    last = nc.tensor.matmul(c.PS[:, 1 + n, :], c.WT[:, n * D:(n + 1) * D], ZT, start=True, stop=True)
                last.then_inc(qk_mm, 1)
                for b in range(B):
                    bank = BANKS[b % 2]
                    if b >= 2:
                        pe.wait_ge(vf_out, done(i, B, b - 2))
                        pe.wait_ge(prod_done, done(i, B, b - 2))
                    else:
                        pe.wait_ge(prod_done, before(i, B, 0))
                    zb = c.HT[:, b, :]
                    nc.tensor.matmul(c.PS[:, bank[0], 0:D], zb, c.WT[:, 0:D], start=True, stop=True)
                    nc.tensor.matmul(c.PS[:, bank[0], D:2 * D], zb, c.WT[:, 2 * D:3 * D], start=True, stop=True)
                    nc.tensor.matmul(c.PS[:, bank[1], :], zb, c.BIG[:, :, 0:D], start=True, stop=True)
                    nc.tensor.matmul(c.PS[:, bank[2], :], zb, c.BIG[:, :, D:2 * D], start=True, stop=True
                                     ).then_inc(tok_mm, 1)


HALVES, HB = 2, 4
UNITS = [(half, s) for half in range(HALVES) for s in range(HB * (half + 1))]
MAX_UNITS = [(t, half, h) for t in range(NC) for half in range(t // HB + 1) for h in range(GH)]


def attention(nc, m, c, scratch):
    NU, NM = len(UNITS), len(MAX_UNITS)
    set_dve, set_pool, v_laid = m.sem("at_set_dve"), m.sem("at_set_pool"), m.sem("at_v_laid")
    qk_loaded = [m.sem(f"at_qk_loaded{g}") for g in range(NG)]
    max_mm, max_taken, top_done, shift_done = (m.sem("at_" + n) for n in ("max_mm", "max_taken", "top", "shift"))
    shift_t, neg_done, n1, r1, n2, r2 = (m.sem("at_" + n) for n in ("shift_t", "neg", "n1", "r1", "n2", "r2"))
    shift_rows = m.sem("at_shift_rows")
    score_mm, exp_done, masked, value_mm = (m.sem("at_" + n) for n in ("score_mm", "exp", "masked", "value_mm"))
    of_out, of_t, nd_out = m.sem("at_of_out"), m.sem("at_of_t"), m.sem("at_nd_out")
    C4 = lambda t, b: t[:, bass.ds(b * NC, NC), :]
    LOADS = 2 * NT
    AT_ONCE, LEAD = NM // (2 * NU), 12
    serial = lambda b, g, u, p=0: ((b * NG + g) * NU + u) * 2 + p
    scored = lambda n: n + 1 + NG * NU * 2
    exped = lambda n: n + 3
    valued = lambda b, g, u: (b * NG + g) * NU + u + 1 + 2 * NU

    def width(half, s):
        first = max(s - HB * half, 0)
        return (HB - first) * P, (HB * half + first) * P

    with nc.Block() as block:

        @block.sync
        def _(sp):
            def load(b, g):
                sp.wait_ge(score_mm, (b * NG + g + 1) * (2 * NU))
                for tile, qk, rows in ((c.QS, 0, ROW_Q), (c.KS, 1, ROW_K)):
                    for r, part in enumerate(rows):
                        src = scratch.qk[GH * g * HS:GH * (g + 1) * HS,
                                         bass.ds(b + (part * 2 + qk) * B, 1), :].rearrange(
                            "(h d) o t -> d h (o t)", d=HS)
                        sp.dma_start(tile[r * HS:(r + 1) * HS, g, :, :], src).then_inc(qk_loaded[g], 16)

            def shift(b, g):
                sp.wait_ge(r2, done(b, NG, g))
                for n in range(NS):
                    dst = c.QS[KM + n:KM + n + 1, g, :, :].rearrange("o h t -> o (h t)")
                    sp.dma_start(dst, c.NEGM[:, g % 2, n, :]).then_inc(shift_rows, 16)

            def batch(b, last):
                shift(b, 0)
                load(b, NG - 1)
                for g in range(1, NG):
                    shift(b, g)
                    if not last:
                        load(b + 1, g - 1)

            for g in range(NG - 1):
                sp.wait_ge(set_dve, 2 * g + 2)
                sp.wait_ge(set_pool, g + 1)
                load(0, g)
            sp.wait_ge(set_dve, 2 * NG)
            sp.wait_ge(set_pool, NG)
            with sp.Fori(0, B - 1) as b:
                batch(b, False)
            batch(B - 1, True)
            sp.wait_ge(shift_rows, 16 * NS * B * NG)

        @block.vector
        def _(dve):
            for g in range(NG):
                nc.vector.memset(c.KS[KM:P, g, :, :], 1.0).then_inc(set_dve, 1)
                nc.vector.memset(c.QS[:, g, :, :], 0.0).then_inc(set_dve, 1)
            nc.vector.memset(c.MP[:, :, :, :], -1e30).then_inc(max_taken, 2)
            credit(dve, [top_done, shift_done, neg_done, n1, r1, n2, r2])

            def group(b, g):
                for u, (t, half, h) in enumerate(MAX_UNITS):
                    w = min(512, (t + 1) * P - 512 * half)
                    dve.wait_ge(max_mm, (b * NG + g) * NM + u + 1)
                    nc.vector.reduce_max(c.MP[:, t, half, h:h + 1], c.PS[:, 4 + u % 2, 0:w], X_AXIS
                                         ).then_inc(max_taken, 1)
                dve.wait_ge(max_taken, (b * NG + g + 1) * NM + 2)
                nc.vector.tensor_tensor(c.MX[:, :, :], c.MP[:, :, 0, :], c.MP[:, :, 1, :], ALU.max
                                        ).then_inc(top_done, 1)
                dve.wait_ge(top_done, done(b, NG, g))
                for dst in (C4(c.SHIFT, b)[:, :, GH * g:GH * g + GH], c.MG[:, :, :].rearrange("p h n -> p n h")):
                    last = nc.vector.tensor_tensor(dst, c.MX[:, :, :], C4(c.FMAX, b)[:, :, GH * g:GH * g + GH],
                                                   ALU.max)
                last.then_inc(shift_done, 1)
                dve.wait_ge(shift_t, done(b, NG, g))
                nc.vector.tensor_scalar(c.SH[:, 0, :], c.PS[0:NC * GH, 7, 0:P], -1.0, None, ALU.mult
                                        ).then_inc(neg_done, 1)
                dve.wait_ge(neg_done, done(b, NG, g))
                parts = c.NEGM[:, g % 2, :, :]
                nc.vector.tensor_copy(parts[:, 0, :], c.SH[:, 0, :]).then_inc(n1, 1)
                dve.wait_ge(n1, done(b, NG, g))
                nc.vector.tensor_tensor(c.SH[:, 1, :], c.SH[:, 0, :], parts[:, 0, :], ALU.subtract).then_inc(r1, 1)
                dve.wait_ge(r1, done(b, NG, g))
                nc.vector.tensor_copy(parts[:, 1, :], c.SH[:, 1, :]).then_inc(n2, 1)
                dve.wait_ge(n2, done(b, NG, g))
                nc.vector.tensor_tensor(parts[:, 2, :], c.SH[:, 1, :], parts[:, 1, :], ALU.subtract).then_inc(r2, 1)

            with dve.Fori(0, B) as b:
                for g in range(NG):
                    group(b, g)

        @block.gpsimd
        def _(pool):
            for g in range(NG):
                nc.gpsimd.memset(c.KS[0:KM, g, :, :], 0.0).then_inc(set_pool, 1)
            nc.gpsimd.memset(c.VG[:, :, :, :, :], 0.0).then_inc(set_pool, 1)
            pool.wait_ge(set_pool, NG + 1)
            nc.gpsimd.memset(c.VG[:, :, :, :, HS:HS + 1], 1.0)
            credit(pool, [v_laid, masked])
            with pool.Fori(0, B) as b:
                for g in range(NG):
                    pool.wait_ge(value_mm, (b * NG + g + 1) * NU)
                    v = C4(c.VT, b)[:, :, GH * HS * g:GH * HS * (g + 1)].rearrange("p n (h d) -> p n h d", d=HS)
                    pool.sem_inc(c.passed, 1)
                    for h in range(GH):
                        last = nc.gpsimd.tensor_copy(c.VG[:, g % 2, :, h, 0:HS], v[:, :, h, :])
                    last.then_inc(v_laid, 1)
                    for u, (half, s) in enumerate(UNITS):
                        if s < HB * half:
                            continue
                        for p in range(2):
                            pool.wait_ge(exp_done, exped(serial(b, g, u, p)))
                            pool.sem_inc(c.passed, 1)
                            diagonal = c.PT[:, u % 2, p, :, 0:P]
                            nc.gpsimd.affine_select(out=diagonal, in_=diagonal, compare_op=ALU.is_ge, fill=0.0,
                                                    base=0, pattern=[[0, 2], [1, P]], channel_multiplier=-1
                                                    ).then_inc(masked, 1)

        @block.scalar
        def _(act):
            credit(act, [exp_done, exp_done, of_out, nd_out])

            def sums_out(b, g, half):
                n = (b * NG + g) * 2 + half
                act.wait_ge(value_mm, valued(b, g, (3, 11)[half]))
                act.wait_ge(of_t, n + 1)
                nc.scalar.copy(c.OF[:, :], c.PS[:, 6, :]).then_inc(of_out, 1)

            def sums_kept(b, g, half):
                act.wait_ge(of_t, (b * NG + g) * 2 + half + 2)
                nd = c.ND[:, bass.ds(b * NC + HB * half, HB), GH * g:GH * g + GH, :]
                src = c.PS[:, 7, :].rearrange("p (n h r) -> p n h r", n=HB, h=GH)
                for h in range(GH):
                    last = nc.scalar.copy(nd[:, :, h, :], src[:, :, h, 0:HS + 1])
                last.then_inc(nd_out, 1)

            with act.Fori(0, B) as b:
                for g in range(NG):
                    for u, (half, s) in enumerate(UNITS):
                        w, _ = width(half, s)
                        for p in range(2):
                            act.wait_ge(score_mm, scored(serial(b, g, u, p)))
                            act.wait_ge(value_mm, valued(b, g, u - 2))
                            nc.scalar.activation(c.PT[:, u % 2, p, :, 0:w], c.PS[:, 2 * p:2 * p + 2, 0:w],
                                                 ACT.Exp).then_inc(exp_done, 1)
                        if u == 4:
                            sums_out(b, g, 0)
                        if u == 6:
                            sums_kept(b, g, 0)
                    sums_out(b, g, 1)
                    sums_kept(b, g, 1)

        @block.tensor
        def _(pe):
            credit(pe, [shift_t, of_t])
            pe.sem_inc(score_mm, NG * NU * 2)
            pe.sem_inc(value_mm, 2 * NU)

            def maxima(b, g, units):
                slot = g % NG
                for u in units:
                    t, half, h = MAX_UNITS[u]
                    w = min(512, (t + 1) * P - 512 * half)
                    if u == 0:
                        pe.wait_ge(qk_loaded[slot], (b + g // NG) * (16 * LOADS) + 16 * LOADS)
                    pe.wait_ge(max_taken, (b * NG + g) * NM + u + 1)
                    diagonal = half == t // HB
                    last = nc.tensor.matmul(c.PS[:, 4 + u % 2, 0:w], c.QS[0:KM, slot, h, t * P:(t + 1) * P],
                                            c.KS[0:KM, slot, h, 512 * half:512 * half + w],
                                            start=True, stop=not diagonal)
                    if diagonal:
                        last = nc.tensor.matmul(c.PS[:, 4 + u % 2, w - P:w], c.IDENTB[:, :], c.LATER[:, :],
                                                start=False, stop=True)
                    last.then_inc(max_mm, 1)

            def turn_shift(b, g):
                pe.wait_ge(shift_done, done(b, NG, g))
                pe.wait_ge(nd_out, (b * NG + g) * 2)
                nc.tensor.transpose(c.PS[0:NC * GH, 7, 0:P], c.MG[:, :, :].rearrange("p h n -> p (h n)"),
                                    c.IDENT[:, :]).then_inc(shift_t, 1)

            def values(b, g, u):
                half, s = UNITS[u]
                w, first = width(half, s)
                gn = b * NG + g
                pe.wait_ge(exp_done, exped(serial(b, g, u, 1)))
                if s >= HB * half:
                    seen = sum(1 for q in UNITS[:u + 1] if q[1] >= HB * q[0])
                    pe.wait_ge(masked, gn * (2 * NC) + (2 * seen + 1))
                if u == 0:
                    pe.wait_ge(v_laid, done(b, NG, g))
                if s == 0:
                    pe.wait_ge(of_out, gn * 2 + (half + 1))
                o = first - 512 * half
                for h in range(GH):
                    last = nc.tensor.matmul(c.PS[32 * h:32 * h + 32, 6, o:o + w], c.VG[:, g % 2, s, h, :],
                                            c.PT[:, u % 2, h // 2, h % 2, 0:w],
                                            start=(s == 0), stop=(s == HB * (half + 1) - 1))
                last.then_inc(value_mm, 1)

            def turn_sums(b, g, half, shifted):
                gn = b * NG + g
                pe.wait_ge(of_out, gn * 2 + (half + 2))
                pe.wait_ge(neg_done, done(b, NG, shifted))
                pe.wait_ge(nd_out, gn * 2 + (half + 1))
                for n in range(HB):
                    last = nc.tensor.transpose(c.PS[:, 7, n * P:(n + 1) * P], c.OF[:, n * P:(n + 1) * P],
                                               c.IDENT[:, :])
                last.then_inc(of_t, 1)

            def batch(b, last):
                for g in range(NG):
                    pe.wait_ge(shift_rows, (b * NG + g + 1) * (16 * NS))
                    for u, (half, s) in enumerate(UNITS):
                        w, first = width(half, s)
                        for p in range(2):
                            pe.wait_ge(exp_done, exped(serial(b, g, u - 1, p)))
                            for k in range(2):
                                h = 2 * p + k
                                mm = nc.tensor.matmul(c.PS[:, h, 0:w], c.KS[0:KA, g, h, s * P:(s + 1) * P],
                                                      c.QS[0:KA, g, h, first:first + w], start=True, stop=True)
                            mm.then_inc(score_mm, 1)
                            k = LEAD + (2 * u + p) * AT_ONCE
                            ahead = g + 1 + k // NM
                            if k == NM + AT_ONCE and (g + 1 < NG or not last):
                                turn_shift(b, g + 1)
                            if ahead < NG or not last:
                                maxima(b, ahead, range(k % NM, k % NM + AT_ONCE))
                        if u:
                            values(b, g, u - 1)
                        if u == 5:
                            turn_sums(b, g, 0, g)
                    values(b, g, NU - 1)
                    turn_sums(b, g, 1, g + 1 if g + 1 < NG or not last else g)

            maxima(0, 0, range(NM))
            maxima(0, 1, range(AT_ONCE))
            pe.wait_ge(shift_done, done(0))
            nc.tensor.transpose(c.PS[0:NC * GH, 7, 0:P], c.MG[:, :, :].rearrange("p h n -> p (h n)"),
                                c.IDENT[:, :]).then_inc(shift_t, 1)
            maxima(0, 1, range(AT_ONCE, LEAD))
            with pe.Fori(0, B - 1) as b:
                batch(b, False)
            batch(B - 1, True)


F1 = 4 * D
NB1 = F1 // P


def attention_output(nc, m, c, dram, scratch):
    ln = LnSems(m, "ao")
    loaded, vf_loaded, hin_loaded = m.sem("ao_loaded"), m.sem("ao_vf_loaded"), m.sem("ao_h_loaded")
    less, exp_done, prod_done, num_done, den_done, rec_done, o_done, both_done = (
        m.sem("ao_" + n) for n in ("less", "exp", "prod", "num", "den", "rec", "o", "both"))
    o_t, o_out, proj_mm, x1_done, turned, z_ready = (
        m.sem("ao_" + n) for n in ("o_t", "o_out", "proj", "x1", "turned", "z"))
    up_mm, gelu_done, down_mm, y_done, gated, res_done = (
        m.sem("ao_" + n) for n in ("up", "gelu", "down", "y", "gated", "res"))
    X4 = c.X[:, :, :].rearrange("p (b n) d -> p b n d", b=B)
    F4 = c.FUT[:, :, :].rearrange("p (b n) d -> p b n d", b=B)
    M4 = c.SHIFT[:, :, :].rearrange("p (b n) d -> p b n d", b=B)
    N4 = c.ND[:, :, :, :].rearrange("p (b n) h r -> p b n (h r)", b=B)
    two = lambda bank, o: c.PS[:, bank, o:o + 2 * P].rearrange("p (b n) -> p b n", b=2)
    ZT = c.HT[:, :, :].rearrange("p b t -> p (b t)")
    loads = [(c.WP[:, :], dram["L1_attn_W_proj_T"]), (c.W1[:, :], dram["L1_attn_W_ff1"]),
             (c.W2[:, :, :], dram["L1_attn_W_ff2"].rearrange("(k p) d -> p k d", p=P))]

    with nc.Block() as block:

        @block.sync
        def _(sp):
            for dst, src in loads:
                sp.dma_start(dst, src).then_inc(loaded, 16)
            with sp.Fori(0, NC) as i:
                sp.wait_ge(prod_done, before(i))
                sp.dma_start(c.VF[:, :, :], scratch.vf[:, bass.ds(i, 1), :, :].rearrange("b o p n -> p b (o n)")
                             ).then_inc(vf_loaded, 16)
                sp.wait_ge(x1_done, before(i, 2))
                sp.dma_start(c.H[:, :, :], scratch.h[:, bass.ds(i, 1), :, :].rearrange("b o p d -> p b (o d)")
                             ).then_inc(hin_loaded, 16)

        @block.vector
        def _(dve):
            credit(dve, ln.dve() + [less, prod_done, num_done, den_done, both_done, rec_done, o_done, x1_done,
                                    y_done, gated, res_done])

            def front(i):
                fi, mi, ni = at(F4, i), at(M4, i), at(N4, i)
                for b in range(B):
                    last = nc.vector.tensor_tensor(
                        c.PF[:, b, :].rearrange("p (f h) -> p f h", f=NF), fi[:, b, :].rearrange("p (f h) -> p f h", f=NF),
                        bcast(mi[:, b, :].unsqueeze(1), [P, NF, H1]), ALU.subtract)
                last.then_inc(less, 1)
                dve.wait_ge(exp_done, done(i))
                dve.wait_ge(vf_loaded, i * 16 + 16)
                for b in range(B):
                    last = nc.vector.tensor_tensor(
                        c.FP[:, b, :, :].rearrange("p f (h d) -> p (f h) d", d=HS),
                        c.VF[:, b, :].rearrange("p (n d) -> p n d", d=HS),
                        bcast(c.PF[:, b, :].unsqueeze(2), [P, NF * H1, HS]), ALU.mult)
                last.then_inc(prod_done, 1)
                dve.wait_ge(prod_done, done(i))
                for b in range(B):
                    nc.vector.tensor_reduce(c.O[:, b, :], c.FP[:, b, :, :].rearrange("p f n -> p n f"), X_AXIS, ALU.add)
                    last = nc.vector.tensor_reduce(c.DEN[:, b, :], c.PF[:, b, :].rearrange("p (f h) -> p h f", f=NF),
                                                   X_AXIS, ALU.add)
                last.then_inc(num_done, 1)
                dve.wait_ge(num_done, done(i))
                n9 = ni.rearrange("p b (h r) -> p b h r", r=HS + 1)
                for b in range(B):
                    nc.vector.tensor_tensor(c.DEN[:, b, :], c.DEN[:, b, :], n9[:, b, :, HS], ALU.add)
                    last = nc.vector.tensor_tensor(c.O[:, b, :].rearrange("p (h d) -> p h d", d=HS),
                                                   c.O[:, b, :].rearrange("p (h d) -> p h d", d=HS),
                                                   n9[:, b, :, 0:HS], ALU.add)
                last.then_inc(both_done, 1)
                dve.wait_ge(both_done, done(i))
                nc.vector.reciprocal(c.DEN[:, :, :], c.DEN[:, :, :]).then_inc(rec_done, 1)
                dve.wait_ge(rec_done, done(i))
                nc.vector.tensor_tensor(c.O[:, :, :].rearrange("p b (h d) -> p (b h) d", d=HS),
                                        c.O[:, :, :].rearrange("p b (h d) -> p (b h) d", d=HS),
                                        bcast(c.DEN[:, :, :].rearrange("p b h -> p (b h)").unsqueeze(2),
                                              [P, B * H1, HS]), ALU.mult).then_inc(o_done, 1)

            def middle(i):
                dve.wait_ge(hin_loaded, i * 16 + 16)
                for h, half, _ in HALF_BATCHES:
                    dve.wait_ge(proj_mm, done(i, 2, h))
                    nc.vector.tensor_tensor(c.X1[:, half, :], two(2 + h, 0), c.H[:, half, :], ALU.add
                                            ).then_inc(x1_done, 1)
                dve.wait_ge(x1_done, done(i, 2, 1))
                ln_stats(nc, dve, c, ln, lambda b: c.X1[:, b, :], i)
                ln_apply(nc, dve, c, ln, lambda b: c.X1[:, b, :], lambda b: c.XN[:, b, :], i)

            def back(i):
                xi = at(X4, i)
                for h, half, _ in HALF_BATCHES:
                    dve.wait_ge(down_mm, done(i, 2, h))
                    nc.vector.tensor_tensor(c.Y[:, half, :], two(2 + h, 256), c.X1[:, half, :], ALU.add
                                            ).then_inc(y_done, 1)
                    dve.wait_ge(y_done, done(i, 2, h))
                    nc.vector.tensor_tensor(c.Y[:, half, :], c.Y[:, half, :], c.MROW[:, 1, half, GATE_A, :], ALU.mult
                                            ).then_inc(gated, 1)
                    dve.wait_ge(gated, done(i, 2, h))
                    nc.vector.tensor_tensor(xi[:, half, :], xi[:, half, :], c.Y[:, half, :], ALU.add
                                            ).then_inc(res_done, 1)

            front(0)
            with dve.Fori(0, NC - 1) as i:
                middle(i)
                front(i + 1)
                back(i)
            middle(NC - 1)
            back(NC - 1)

        @block.gpsimd
        def _(pool):
            credit(pool, ln.pool())
            with pool.Fori(0, NC) as i:
                ln_rstd(nc, pool, c, ln, i)

        @block.scalar
        def _(act):
            credit(act, [exp_done, o_out, z_ready, gelu_done])

            def front(i):
                act.wait_ge(less, done(i))
                nc.scalar.activation(c.PF[:, :, :], c.PF[:, :, :], ACT.Exp).then_inc(exp_done, 1)

            def middle(i):
                for h, half, _ in HALF_BATCHES:
                    act.wait_ge(o_t, done(i, 2, h))
                    nc.scalar.copy(c.OT[:, half, :], two(h, 0)).then_inc(o_out, 1)
                for h, half, _ in HALF_BATCHES:
                    act.wait_ge(turned, done(i, 2, h))
                    nc.scalar.activation(ZT[:, h * 256:h * 256 + 256], c.PS[:, h, 256:512], ACT.Identity,
                                         scale=c.LNG[:, 2:3], bias=c.LNG[:, 3:4]).then_inc(z_ready, 1)

            def back(i):
                for h, _, _ in HALF_BATCHES:
                    act.wait_ge(up_mm, done(i, 2, h))
                    nc.scalar.activation(c.GE[:, h, :, :], c.PS[:, 4 + 2 * h:6 + 2 * h, :].rearrange(
                        "p k (a n) -> p (k a) n", a=2), ACT.Gelu).then_inc(gelu_done, 1)

            front(0)
            with act.Fori(0, NC - 1) as i:
                middle(i)
                front(i + 1)
                back(i)
            middle(NC - 1)
            back(NC - 1)

        @block.tensor
        def _(pe):
            credit(pe, [o_t, proj_mm, turned, up_mm, down_mm])
            pe.wait_ge(loaded, 16 * len(loads))
            with pe.Fori(0, NC) as i:
                pe.wait_ge(o_done, done(i))
                for h, _, batches in HALF_BATCHES:
                    turn_half(nc, c, h, 0, c.O, batches).then_inc(o_t, 1)
                pe.wait_ge(y_done, before(i, 2))
                for h, _, batches in HALF_BATCHES:
                    pe.wait_ge(o_out, done(i, 2, h))
                    for n, b in enumerate(batches):
                        last = nc.tensor.matmul(c.PS[:, 2 + h, n * P:(n + 1) * P], c.OT[:, b, :], c.WP[:, :],
                                                start=True, stop=True)
                    last.then_inc(proj_mm, 1)
                for h, _, batches in HALF_BATCHES:
                    pe.wait_ge(ln.normed, done(i, 2, h))
                    turn_half(nc, c, h, 256, c.XN, batches).then_inc(turned, 1)
                for h, half, batches in HALF_BATCHES:
                    pe.wait_ge(z_ready, done(i, 2, h))
                    for k in range(NB1):
                        last = nc.tensor.matmul(c.PS[:, 4 + 2 * h + k // 2, 256 * (k % 2):256 * (k % 2) + 256],
                                                c.W1[:, k * P:(k + 1) * P], ZT[:, h * 256:h * 256 + 256],
                                                start=True, stop=True)
                    last.then_inc(up_mm, 1)
                for h, _, batches in HALF_BATCHES:
                    pe.wait_ge(gelu_done, done(i, 2, h))
                    for n in range(2):
                        for k in range(NB1):
                            last = nc.tensor.matmul(c.PS[:, 2 + h, 256 + n * P:256 + (n + 1) * P],
                                                    c.GE[:, h, k, n * P:(n + 1) * P], c.W2[:, k, :],
                                                    start=(k == 0), stop=(k == NB1 - 1))
                    last.then_inc(down_mm, 1)


E1 = 64
PAIRS = B * T // 8 // 2
SB, BP = 128, 8
NSB, NBP = PAIRS // SB, SB // BP
GR = NSB * 2


def experts_input(nc, m, c, scratch):
    ln = LnSems(m, "ki")
    turned, h_ready, x_stored = m.sem("ki_turned"), m.sem("ki_h"), m.sem("ki_x_stored")
    X4 = c.X[:, :, :].rearrange("p (b n) d -> p b n d", b=B)
    H4 = c.HTA[:, :].rearrange("p (b n t) -> p b n t", b=B, n=NC)
    with nc.Block() as block:

        @block.sync
        def _(sp):
            sp.dma_start(scratch.x, c.X[:, :, :]).then_inc(x_stored, 16)
            sp.wait_ge(h_ready, NC + 1)
            sp.dma_start(scratch.ht, c.HTA[:, :]).then_inc(x_stored, 16)
            sp.wait_ge(x_stored, 32)

        @block.vector
        def _(dve):
            credit(dve, ln.dve())
            with dve.Fori(0, NC) as i:
                xi = at(X4, i)
                ln_stats(nc, dve, c, ln, lambda b: xi[:, b, :], i)
                dve.wait_ge(turned, before(i))
                ln_apply(nc, dve, c, ln, lambda b: xi[:, b, :], lambda b: c.XN[:, b, :], i)

        @block.gpsimd
        def _(pool):
            credit(pool, ln.pool())
            with pool.Fori(0, NC) as i:
                ln_rstd(nc, pool, c, ln, i)

        @block.scalar
        def _(act):
            credit(act, [h_ready])
            with act.Fori(0, NC) as i:
                act.wait_ge(turned, done(i))
                hi = at(H4, i)
                for b in range(B):
                    last = nc.scalar.activation(hi[:, b, :], c.PS[:, 0, b * P:(b + 1) * P], ACT.Identity,
                                                scale=c.MCOL[:, 1, SCALE_B, b:b + 1],
                                                bias=c.MCOL[:, 1, SHIFT_B, b:b + 1])
                last.then_inc(h_ready, 1)

        @block.tensor
        def _(pe):
            credit(pe, [turned])
            with pe.Fori(0, NC) as i:
                pe.wait_ge(ln.normed, done(i, 2, 1))
                pe.wait_ge(h_ready, before(i))
                for b in range(B):
                    last = nc.tensor.transpose(c.PS[:, 0, b * P:(b + 1) * P], c.XN[:, b, :], c.IDENT[:, :])
                last.then_inc(turned, 1)


def route(nc, m, c, tag, logits_mm):
    names = ("logit_mm", "logit_out", "top", "idx", "idx_f", "diff", "exp", "sum", "rec", "second", "hot",
             "weighed", "turned")
    s = {n: m.sem(tag + "_" + n) for n in names}
    with nc.Block() as block:

        @block.vector
        def _(dve):
            dve.wait_ge(s["logit_mm"], 1)
            nc.vector.tensor_copy(c.LG1[:, :, :], c.PS[:, 0, 0:GR * E1].rearrange("p (g e) -> p g e", g=GR)
                                  ).then_inc(s["logit_out"], 1)
            dve.wait_ge(s["logit_out"], 1)
            for g in range(GR):
                last = nc.vector.max(c.TOP1[:, g, :], c.LG1[:, g, :])
            last.then_inc(s["top"], 1)
            dve.wait_ge(s["top"], 1)
            nc.vector.tensor_tensor(c.PR[:, :, 1:2], c.TOP1[:, :, 1:2], c.TOP1[:, :, 0:1], ALU.subtract
                                    ).then_inc(s["diff"], 1)
            for g in range(GR):
                last = nc.vector.max_index(c.TIX1[:, g, :], c.TOP1[:, g, :], c.LG1[:, g, :])
            last.then_inc(s["idx"], 1)
            dve.wait_ge(s["idx"], 1)
            nc.vector.tensor_copy(c.TIF1[:, :, :], c.TIX1[:, :, 0:2]).then_inc(s["idx_f"], 1)
            dve.wait_ge(s["idx_f"], 1)
            for k in range(2):
                for twin in range(2):
                    last = nc.vector.tensor_tensor(c.OH[:, k, :, twin, :],
                                                   bcast(c.IOTA1[:, :].unsqueeze(1), [P, GR, E1]),
                                                   bcast(c.TIF1[:, :, k:k + 1], [P, GR, E1]), ALU.is_equal)
            last.then_inc(s["hot"], 1)
            dve.wait_ge(s["exp"], 1)
            nc.vector.tensor_scalar_add(c.PR[:, :, 2:3], c.PR[:, :, 1:2], 1.0).then_inc(s["sum"], 1)
            dve.wait_ge(s["sum"], 1)
            nc.vector.reciprocal(c.PR[:, :, 0:1], c.PR[:, :, 2:3]).then_inc(s["rec"], 1)
            dve.wait_ge(s["rec"], 1)
            nc.vector.tensor_tensor(c.PR[:, :, 1:2], c.PR[:, :, 1:2], c.PR[:, :, 0:1], ALU.mult
                                    ).then_inc(s["second"], 1)
            dve.wait_ge(s["second"], 1)
            dve.wait_ge(s["hot"], 1)
            for k in range(2):
                last = nc.vector.tensor_tensor(c.OHW[:, k, :, :], c.OH[:, k, :, 0, :],
                                               bcast(c.PR[:, :, k:k + 1], [P, GR, E1]), ALU.mult)
            last.then_inc(s["weighed"], 1)
            dve.wait_ge(s["turned"], 1)
            nc.vector.tensor_copy(c.OHT[:, :, :], c.PS[:, 4:6, :])
            nc.vector.tensor_copy(c.OHTW[:, :, :], c.PS[0:E1, 6:8, :])

        @block.scalar
        def _(act):
            act.wait_ge(s["diff"], 1)
            nc.scalar.activation(c.PR[:, :, 1:2], c.PR[:, :, 1:2], ACT.Exp).then_inc(s["exp"], 1)

        @block.tensor
        def _(pe):
            logits_mm(pe).then_inc(s["logit_mm"], 1)
            pe.wait_ge(s["weighed"], 1)
            for k in range(2):
                for g in range(GR):
                    nc.tensor.transpose(c.PS[:, 4 + k, g * P:(g + 1) * P],
                                        c.OH[:, k, g, :, :].rearrange("p t e -> p (t e)"), c.IDENT[:, :])
                    last = nc.tensor.transpose(c.PS[0:E1, 6 + k, g * P:(g + 1) * P], c.OHW[:, k, g, :],
                                               c.IDENT[:, :])
            last.then_inc(s["turned"], 1)


def up_logits(nc, c):
    H = c.HTA[:, :].rearrange("p (n r k) -> p n r k", r=2, k=8)
    for sb in range(NSB):
        for r in range(2):
            o = (sb * 2 + r) * E1
            for k in range(8):
                last = nc.tensor.matmul(c.PS[:, 0, o:o + E1], H[:, sb * SB:(sb + 1) * SB, r, k], c.WUR[:, k, :],
                                        start=(k == 0), stop=(k == 7))
    return last


def down_turned(nc, c):
    for sb in range(NSB):
        last = nc.tensor.transpose(c.PS[:, 0, sb * P:(sb + 1) * P], c.LT[:, sb * SB:(sb + 1) * SB], c.IDENT[:, :])
    return last


def table_loads(c, dram, layer):
    flat = lambda name: dram[name].rearrange("e o i -> e (o i)")
    return [(table_rows(c, n)[E1 * twin:E1 * twin + E1, :], flat(f"L1_ffn_{n}_{layer}"))
            for n in "AB" for twin in range(2)]


def table_rows(c, name):
    k = 16 * "AB".index(name)
    return c.BG[:, k:k + 16, :].rearrange("p k n -> p (k n)")


def split_tables(nc, dve, c, split):
    pairs = [(table_rows(c, "A"), c.TWO[:, 0, :], c.LOW[:, 0, :]), (table_rows(c, "B"), c.TWO[:, 1, :], c.LOW[:, 1, :])]
    for rows, two, low in pairs:
        last = nc.vector.tensor_copy(two, rows)
    last.then_inc(split, 1)
    dve.wait_ge(split, 1)
    for rows, two, low in pairs:
        last = nc.vector.tensor_tensor(rows, rows, two, ALU.subtract)
    last.then_inc(split, 1)
    dve.wait_ge(split, 2)
    for rows, two, low in pairs:
        nc.vector.tensor_copy(two[E1:P, :], rows[E1:P, :])
        last = nc.vector.tensor_copy(low[0:E1, :], rows[0:E1, :])
    last.then_inc(split, 1)
    dve.wait_ge(split, 3)
    for rows, two, low in pairs:
        nc.vector.tensor_tensor(low[0:E1, :], rows[0:E1, :], low[0:E1, :], ALU.subtract)


def kronecker_loads(nc, m, c, dram, scratch):
    loaded, tables, split = m.sem("ke_loaded"), m.sem("ke_tables"), m.sem("ke_split")
    first = table_loads(c, dram, "up")
    loads = [(c.WUR[:, :, :], dram["L1_ffn_W_up"]),
             (c.SCL[:, 0:1], dram["L1_ffn_scale_up"].partition_broadcast(P)),
             (c.SCL[:, 1:2], dram["L1_ffn_scale_down"].partition_broadcast(P)),
             (c.BUP[0:64, :], dram["L1_ffn_bias_up"]), (c.BUP[64:128, :], dram["L1_ffn_bias_up"]),
             (c.BDN[:, :], dram["L1_ffn_bias_down"]), (c.HTA[:, :], scratch.ht)]
    with nc.Block() as block:

        @block.sync
        def _(sp):
            for dst, src in first:
                sp.dma_start(dst, src).then_inc(tables, 16)
            for dst, src in loads:
                sp.dma_start(dst, src).then_inc(loaded, 16)
            sp.wait_ge(loaded, 16 * len(loads))

        @block.vector
        def _(dve):
            nc.vector.memset(c.LOW[E1:P, :, :], 0.0)
            dve.wait_ge(tables, 16 * len(first))
            split_tables(nc, dve, c, split)

        @block.gpsimd
        def _(pool):
            nc.gpsimd.iota(c.IOTA1[:, :], [[1, E1]], base=0, channel_multiplier=0,
                           allow_small_or_imprecise_dtypes=True)
            nc.gpsimd.memset(c.XD[:, :, :, :], 0.0)
            nc.gpsimd.memset(c.T2[:, :, :, :], 0.0)


def kronecker(nc, m, c, up):
    tag = "ku" if up else "kd"
    names = ("oh_laid", "w_mm", "w_out", "gath_mm", "gath_dve", "gath_act", "x_dve", "x_pool", "one_mm", "t_out",
             "two_mm", "y_out")
    s = {n: m.sem(tag + "_" + n) for n in names}
    WIDE = 64
    NBANK = WIDE // 4
    G = 2 * NBANK
    HALF_B = NBP // 2 - 1
    HD = c.HD[:, :, :]
    made = lambda q: q + 3
    freed = lambda q: q + 1

    def gather(pe, n):
        table = (n + 1) % 2
        for k in range(4):
            col = (n // 2) * 4 + k
            o = c.PS[:, n % 4, k * P:(k + 1) * P]
            for part, start in ((c.TWO, True), (c.LOW, False)):
                for r in range(2):
                    cols = slice(r * SB, (r + 1) * SB)
                    if up:
                        for e in range(2):
                            q = 32 * (2 * r + e)
                            last = nc.tensor.matmul(o[q:q + 32, :], part[:, table, col * 32:col * 32 + 32],
                                                    c.OHB[:, e, cols], start=start, stop=not start)
                    else:
                        e, w = col // 32, col % 32
                        last = nc.tensor.matmul(o[64 * r:64 * r + 64, :], part[:, table, w * 64:w * 64 + 64],
                                                c.OHB[:, e, cols], start=start, stop=not start)
        return last

    def spread_weights():
        for r in range(2):
            for e in range(2):
                w = c.OHBW[:, e, r * SB:(r + 1) * SB]
                if up:
                    q = 32 * (2 * r + e)
                    last = nc.tensor.matmul(c.PS[q:q + 32, 7, 0:SB], c.ONES[0:E1, 0:32], w, start=True, stop=True)
                else:
                    last = nc.tensor.matmul(c.PS[64 * r:64 * r + 64, 7, e * SB:(e + 1) * SB], c.ONES[0:E1, 0:64],
                                            w, start=True, stop=True)
        return last

    def lay_up(engine, q, par, blocks):
        H = c.HTA[:, :].rearrange("p (n r k) -> p n r k", r=2, k=8)[:, bass.ds(q * BP, BP), :, :]
        for r, e in blocks:
            z = 32 * (2 * r + e)
            dst = c.XD[z:z + 32, par, :, z:z + 32].rearrange("p n (k f) -> p n k f", f=4)
            for f in range(4):
                last = engine.tensor_copy(dst[:, :, :, f], H[32 * f:32 * f + 32, :, r, :])
        return last

    def lay_down(engine, q, par, r):
        z = 64 * r
        return engine.tensor_copy(c.XD[z:z + 64, par, :, z:z + 64], HD[z:z + 64, bass.ds(q * BP, BP), :])

    with nc.Block() as block:

        @block.vector
        def _(dve):
            credit(dve, [s["oh_laid"], s["w_out"], s["gath_dve"], s["gath_dve"], s["x_dve"], s["y_out"], s["y_out"]])

            def lay(q, par):
                dve.wait_ge(s["one_mm"], freed(q))
                last = lay_up(nc.vector, q, par, ((0, 0), (0, 1), (1, 0))) if up else lay_down(nc.vector, q, par, 0)
                last.then_inc(s["x_dve"], 1)

            def product_out(q, par):
                dve.wait_ge(s["two_mm"], made(q))
                if up:
                    nc.vector.scalar_tensor_tensor(
                        HD[:, bass.ds(q * BP, BP), :], c.PS[:, 6 + par, :].rearrange("p (n o) -> p n o", n=BP),
                        c.SCL[:, 0:1], bcast(c.BUP[:, :].unsqueeze(1), [P, BP, 64]), ALU.mult, ALU.add
                    ).then_inc(s["y_out"], 1)
                else:
                    src = c.PS[:, 6 + par, 0:BP * 32].rearrange("p (n k f) -> p n k f", n=BP, f=4)
                    Y = c.YT[:, :].rearrange("p (n r k) -> p n r k", r=2, k=8)[:, bass.ds(q * BP, BP), :, :]
                    for r in range(2):
                        for f in range(4):
                            last = nc.vector.tensor_scalar(
                                Y[32 * f:32 * f + 32, :, r, :], src[32 * r:32 * r + 32, :, :, f],
                                c.SCL[32 * r:32 * r + 32, 1:2], None, ALU.mult)
                    last.then_inc(s["y_out"], 1)

            with dve.Fori(0, NSB) as sb:
                part = lambda t: t[:, :, :].rearrange("e k (b n) -> e k b n", b=NSB)[
                    :, :, bass.ds(sb, 1), :].rearrange("e k o n -> e k (o n)")
                nc.vector.tensor_copy(c.OHBW[:, :, :], part(c.OHTW))
                nc.vector.tensor_copy(c.OHB[:, :, :], part(c.OHT)).then_inc(s["oh_laid"], 1)
                for k in range(2):
                    lay(sb * NBP + k, k)
                dve.wait_ge(s["w_mm"], sb + 1)
                nc.vector.tensor_copy(c.WGT[:, :, :], c.PS[:, 7, 0:2 * SB].rearrange("p (e n) -> p e n", e=2)
                                      if not up else bcast(c.PS[:, 7, 0:SB].unsqueeze(1), [P, 2, SB])
                                      ).then_inc(s["w_out"], 1)
                dve.wait_ge(s["w_out"], done(sb))
                for n in range(0, G, 2):
                    k = (n // 2) * 4
                    e = k // 32
                    dve.wait_ge(s["gath_mm"], sb * G + n + 1)
                    nc.vector.tensor_tensor(c.BG[:, k:k + 4, :], c.PS[:, n % 4, :].rearrange("p (k n) -> p k n", k=4),
                                            bcast(c.WGT[:, e:e + 1, :], [P, 4, SB]), ALU.mult
                                            ).then_inc(s["gath_dve"], 1)
                with dve.Fori(0, HALF_B) as it:
                    for par in range(2):
                        q = sb * NBP + it * 2 + par
                        lay(q + 2, par)
                        product_out(q, par)
                for par in range(2):
                    product_out(sb * NBP + (NBP - 2 + par), par)

        @block.gpsimd
        def _(pool):
            credit(pool, [s["x_pool"]])
            with pool.Fori(0, NSB * NBP // 2) as it:
                for par in range(2):
                    q = it * 2 + par
                    pool.wait_ge(s["one_mm"], freed(q))
                    pool.sem_inc(c.passed, 1)
                    last = lay_up(nc.gpsimd, q, par, ((1, 1),)) if up else lay_down(nc.gpsimd, q, par, 1)
                    last.then_inc(s["x_pool"], 1)

        @block.scalar
        def _(act):
            credit(act, [s["gath_act"], s["gath_act"], s["t_out"], s["t_out"]])
            with act.Fori(0, NSB) as sb:
                for n in range(1, G, 2):
                    k = (n // 2) * 4
                    act.wait_ge(s["gath_mm"], sb * G + n + 1)
                    nc.scalar.copy(c.AG[:, k:k + 4, :], c.PS[:, n % 4, :].rearrange("p (k n) -> p k n", k=4)
                                   ).then_inc(s["gath_act"], 1)
                with act.Fori(0, NBP // 2) as it:
                    for par in range(2):
                        q = sb * NBP + it * 2 + par
                        act.wait_ge(s["one_mm"], made(q))
                        act.wait_ge(s["two_mm"], freed(q))
                        for r in range(2):
                            z = 64 * r
                            src = c.PS[z:z + 64, 4 + par, :]
                            if up:
                                last = nc.scalar.copy(c.T2[z:z + 64, par, :, z:z + 64],
                                                      src.rearrange("p (n k) -> p n k", n=BP))
                            else:
                                dst = c.T2[z:z + 64, par, :, :].rearrange("p n (e r k) -> p n e r k", e=2, r=2)
                                last = nc.scalar.copy(dst[:, :, :, r, :],
                                                      src.rearrange("p (n e k) -> p n e k", n=BP, e=2))
                        last.then_inc(s["t_out"], 1)
                if up:
                    act.wait_ge(s["y_out"], sb * NBP + (NBP + 2))
                    h = HD[:, bass.ds(sb * SB, SB), :]
                    nc.scalar.activation(h, h, ACT.Gelu)

        @block.tensor
        def _(pe):
            credit(pe, [s["one_mm"], s["one_mm"], s["two_mm"], s["two_mm"]])

            def column(t, place, a, b):
                return t[:, a:b, bass.ds(place, 1)].rearrange("p k o -> p (k o)")

            def one(sb, it, par):
                q = sb * NBP + it
                pe.wait_ge(s["x_dve"], done(q))
                pe.wait_ge(s["x_pool"], done(q))
                pe.wait_ge(s["t_out"], freed(q))
                pe.sem_inc(c.passed, 1)
                for j in range(BP):
                    last = nc.tensor.matmul(c.PS[:, 4 + par, j * 64:j * 64 + 64], c.XD[:, par, j, :],
                                            column(c.BG, it * BP + j, 0, 64), start=True, stop=True)
                last.then_inc(s["one_mm"], 1)

            def two(sb, it, par):
                q = sb * NBP + it
                pe.wait_ge(s["t_out"], made(q))
                pe.wait_ge(s["y_out"], freed(q))
                pe.sem_inc(c.passed, 1)
                for j in range(BP):
                    if up:
                        last = nc.tensor.matmul(c.PS[:, 6 + par, j * 64:j * 64 + 64], c.T2[:, par, j, :],
                                                column(c.AG, it * BP + j, 0, 64), start=True, stop=True)
                    else:
                        for e in range(2):
                            last = nc.tensor.matmul(c.PS[0:64, 6 + par, j * 32:j * 32 + 32],
                                                    c.T2[:, par, j, e * 64:e * 64 + 64],
                                                    column(c.AG, it * BP + j, 32 * e, 32 * e + 32),
                                                    start=(e == 0), stop=(e == 1))
                last.then_inc(s["two_mm"], 1)

            with pe.Fori(0, NSB) as sb:
                pe.wait_ge(s["oh_laid"], done(sb))
                pe.sem_inc(c.passed, 1)
                spread_weights().then_inc(s["w_mm"], 1)
                for n in range(G):
                    free = s["gath_act"] if n % 2 else s["gath_dve"]
                    pe.wait_ge(free, sb * NBANK + (n // 2 + 1))
                    pe.sem_inc(c.passed, 1)
                    gather(pe, n).then_inc(s["gath_mm"], 1)
                pe.wait_ge(s["gath_dve"], sb * NBANK + (NBANK + 2))
                pe.wait_ge(s["gath_act"], sb * NBANK + (NBANK + 2))
                pe.sem_inc(c.passed, 1)
                one(sb, 0, 0)
                with pe.Fori(0, HALF_B) as it:
                    for par in range(2):
                        one(sb, it * 2 + (par + 1), 1 - par)
                        two(sb, it * 2 + par, par)
                one(sb, NBP - 1, 1)
                two(sb, NBP - 2, 0)
                two(sb, NBP - 1, 1)


def down_logits(nc, m, c, dram):
    zeroed, loaded, mm = m.sem("dl_zeroed"), m.sem("dl_loaded"), m.sem("dl_mm")
    tables, split = m.sem("dl_tables"), m.sem("dl_split")
    tables_of_down = table_loads(c, dram, "down")
    with nc.Block() as block:

        @block.gpsimd
        def _(pool):
            nc.gpsimd.memset(c.AG[:, :, :], 0.0).then_inc(zeroed, 1)
            nc.gpsimd.memset(c.T2[:, :, :, :], 0.0)

        @block.sync
        def _(sp):
            for dst, src in tables_of_down:
                sp.dma_start(dst, src).then_inc(tables, 16)
            sp.wait_ge(zeroed, 1)
            for r in range(2):
                sp.dma_start(c.AG[64 * r:64 * r + 64, :, 64 * r:64 * r + 64], dram["L1_ffn_W_down"]
                             ).then_inc(loaded, 16)
            sp.wait_ge(loaded, 32)

        @block.vector
        def _(dve):
            dve.wait_ge(tables, 16 * len(tables_of_down))
            split_tables(nc, dve, c, split)

        @block.tensor
        def _(pe):
            pe.wait_ge(loaded, 32)
            for o in range(64):
                last = nc.tensor.matmul(c.PS[:, 1, 0:PAIRS], c.AG[:, o, :], c.HD[:, :, o],
                                        start=(o == 0), stop=(o == 63))
            last.then_inc(mm, 1)

        @block.scalar
        def _(act):
            act.wait_ge(mm, 1)
            nc.scalar.copy(c.LT[:, :], c.PS[:, 1, 0:PAIRS])


def experts_output(nc, m, c, scratch, out):
    x_loaded, biased, turned, gated, x_done, stored_ = (
        m.sem("ko_" + n) for n in ("x_loaded", "biased", "turned", "gated", "x_done", "stored"))
    Y4 = c.YT[:, :].rearrange("p (b n t) -> p b n t", b=B, n=NC)
    chunk = lambda t, i: t[:, :, bass.ds(i, 1), :].rearrange("p b o d -> p b (o d)")
    S4 = scratch.x.rearrange("p (b n) d -> p b n d", b=B)
    OUT = out.rearrange("b (n p) d -> p b n d", p=P)
    with nc.Block() as block:

        @block.sync
        def _(sp):
            sp.sem_inc(stored_, 16)
            with sp.Fori(0, NC) as i:
                sp.wait_ge(stored_, stored(i))
                sp.dma_start(c.XC[:, :, :], chunk(S4, i)).then_inc(x_loaded, 16)
                sp.wait_ge(x_done, done(i))
                sp.dma_start(chunk(OUT, i), c.XC[:, :, :]).then_inc(stored_, 16)
            sp.wait_ge(stored_, 16 * NC + 16)

        @block.vector
        def _(dve):
            credit(dve, [biased, gated, x_done])
            with dve.Fori(0, NC) as i:
                dve.wait_ge(turned, before(i))
                for b in range(B):
                    last = nc.vector.tensor_tensor(
                        c.YB[:, b, :].rearrange("p (m k) -> p m k", k=8),
                        chunk(Y4, i)[:, b, :].rearrange("p (m k) -> p m k", k=8),
                        bcast(c.BDN[:, :].unsqueeze(1), [P, P // 8, 8]), ALU.add)
                last.then_inc(biased, 1)
                dve.wait_ge(turned, done(i))
                nc.vector.tensor_tensor(c.Y[:, :, :], c.PS[:, 0, :].rearrange("p (b d) -> p b d", b=B),
                                        c.GATE[:, :, :], ALU.mult).then_inc(gated, 1)
                dve.wait_ge(gated, done(i))
                dve.wait_ge(x_loaded, i * 16 + 16)
                nc.vector.tensor_tensor(c.XC[:, :, :], c.XC[:, :, :], c.Y[:, :, :], ALU.add).then_inc(x_done, 1)

        @block.tensor
        def _(pe):
            credit(pe, [turned])
            with pe.Fori(0, NC) as i:
                pe.wait_ge(biased, done(i))
                pe.wait_ge(gated, before(i))
                for b in range(B):
                    last = nc.tensor.transpose(c.PS[:, 0, b * P:(b + 1) * P], c.YB[:, b, :], c.IDENT[:, :])
                last.then_inc(turned, 1)


class Tiles:
    pass


def allocate(m):
    c = Tiles()
    c.PS = m.ps("PS", [P, 8, 512])
    c.IDENT, c.ONES, c.UPTO = m.sb("IDENT", [P, P]), m.sb("ONES", [P, P]), m.sb("UPTO", [P, P])
    c.ZERO, c.LATER = m.sb("ZERO", [P, P], BF16), m.sb("LATER", [P, P], BF16)
    c.IDENTB = m.sb("IDENTB", [P, P], BF16)
    c.HALF, c.IOTA, c.EPS = m.sb("HALF", [P, B]), m.sb("IOTA", [P, 8]), m.sb("EPS", [P, B])
    c.COND, c.MCOL = m.sb("COND", [P, 2, B]), m.sb("MCOL", [P, 2, 6, B])
    c.ST, c.MV = m.sb("ST", [P, B, 6]), m.sb("MV", [P, B, 2])
    c.VE, c.RSTD = m.sb("VE", [P, B]), m.sb("RSTD", [P, B])
    c.Y, c.GATE = m.sb("Y", [P, B, D]), m.sb("GATE", [P, B, D])
    return c


class Scope:

    def __init__(self, nc, sem):
        self.nc, self.sem, self.stack = nc, sem, ExitStack()

    def __enter__(self):
        self.stack.__enter__()
        return self

    def __exit__(self, *e):
        return self.stack.__exit__(*e)

    def sb(self, name, shape, dt=F32):
        return self.stack.enter_context(self.nc.sbuf_tensor(name, shape, dt))


def keep_gate(nc, m, c):
    with nc.Block() as block:

        @block.vector
        def _(dve):
            nc.vector.tensor_copy(c.GATE[:, :, :], c.MROW[:, 1, :, GATE_B, :])


def build(nc, dram, out):
    with ExitStack() as ctx:
        m = Mem(nc, ctx)
        c = allocate(m)
        c.passed = m.sem("passed")
        scratch = Tiles()
        scratch.h = nc.dram_tensor("h1", (B, NC, P, D), F32, kind="Internal").ap()
        scratch.qk = nc.dram_tensor("qk_parts", (P, 3 * 2 * B, T), BF16, kind="Internal").ap()
        scratch.vf = nc.dram_tensor("future_v", (B, NC, P, NF * D), F32, kind="Internal").ap()
        scratch.ht = nc.dram_tensor("ht_mid", (P, B * T), F32, kind="Internal").ap()
        scratch.x = nc.dram_tensor("x_mid", (P, CH, D), F32, kind="Internal").ap()
        with Scope(nc, m.sem) as a:
            c.X = a.sb("X", [P, CH, D])
            c.MROW = a.sb("MROW", [P, 2, B, 6, D])
            c.XN, c.HT = a.sb("XN", [P, B, D]), a.sb("HT", [P, B, P])
            c.O, c.OT = a.sb("O", [P, B, D]), a.sb("OT", [P, B, P])
            with Scope(nc, m.sem) as t:
                c.WQKV, c.WO, c.BQKV, c.BO = (t.sb("WQKV", [P, 256]), t.sb("WO", [P, D]),
                                              t.sb("BQKV", [P, 256]), t.sb("BO", [P, D]))
                c.WMOD, c.CB, c.CB2 = t.sb("WMOD", [P, 2, 768]), t.sb("CB", [P, 8, P]), t.sb("CB2", [P, 8, P])
                c.QKV, c.NEG, c.PHI = (t.sb("QKV", [P, B, 256]), t.sb("NEG", [P, B, 128]),
                                       t.sb("PHI", [P, B, 128]))
                c.KVP, c.KVSUM, c.PROD = (t.sb(n, [P, B, 512]) for n in ("KVP", "KVSUM", "PROD"))
                c.KSUM, c.KPROD = t.sb("KSUM", [P, B, 64]), t.sb("KPROD", [P, B, 64])
                c.DEN, c.REC, c.NUM = t.sb("DEN", [P, 64]), t.sb("REC", [P, 64]), t.sb("NUM", [P, B, D])
                m.stage(setup, c, dram)
                m.stage(keep_gate, c)
                m.stage(linear_attention, c)
            with Scope(nc, m.sem) as t:
                c.WR, c.WG, c.WU = t.sb("WR", [P, 9]), t.sb("WG", [P, NE0 + 1, F0]), t.sb("WU", [P, NE0 + 1, F0])
                c.WD = t.sb("WD", [P, NE0 + 1, 2, D])
                c.LG, c.EX, c.CW = t.sb("LG", [P, B, 9]), t.sb("EX", [P, B, 9]), t.sb("CW", [P, B, 9])
                c.TOP, c.TIX = t.sb("TOP", [P, B, 8]), t.sb("TIX", [P, B, 8], U32)
                c.TIF, c.HOT = t.sb("TIF", [P, B, 2]), t.sb("HOT", [P, 2, B, 8])
                c.SUM, c.RS = t.sb("SUM", [P, B, 2]), t.sb("RS", [P, B, 2])
                c.SG, c.HH = t.sb("SG", [P, 2, 2, 512]), t.sb("HH", [P, 2, 2, 512])
                m.stage(experts, c, dram)
            with Scope(nc, m.sem) as u:
                c.VT, c.FUT, c.FMAX = (u.sb("VT", [P, CH, D]), u.sb("FUT", [P, CH, NF * H1]),
                                       u.sb("FMAX", [P, CH, H1]))
                c.SHIFT, c.LNG = u.sb("SHIFT", [P, CH, H1]), u.sb("LNG", [P, 4])
                with Scope(nc, m.sem) as t:
                    c.WT, c.WF, c.CV = t.sb("WT", [P, 4 * D]), t.sb("WF", [P, D]), t.sb("CV", [P, NF, HS])
                    c.BD, c.BLOCKS = t.sb("BD", [P, NF, P]), t.sb("BLOCKS", [P, P])
                    c.GK, c.BIG = t.sb("GK", [P, NF, 2 * D]), t.sb("BIG", [P, NF, 2 * D])
                    c.H, c.QKF = t.sb("H", [P, B, D]), t.sb("QKF", [P, 2 * B, P])
                    c.PARTS = t.sb("PARTS", [P, 6 * B, P], BF16)
                    c.QV, c.VF, c.FP = (t.sb("QV", [P, B, 2 * D]), t.sb("VF", [P, B, NF * D]),
                                        t.sb("FP", [P, B, NF, D]))
                    m.stage(attention_inputs, c, dram, scratch)
                c.ND = u.sb("ND", [P, CH, H1, HS + 1])
                with Scope(nc, m.sem) as t:
                    c.QS, c.KS = t.sb("QS", [P, NG, GH, T], BF16), t.sb("KS", [P, NG, GH, T], BF16)
                    c.PT, c.VG = t.sb("PT", [P, 2, 2, 2, 512]), t.sb("VG", [P, 2, NC, GH, 32])
                    c.MP, c.MX, c.MG = (t.sb("MP", [P, NC, 2, GH]), t.sb("MX", [P, NC, GH]),
                                        t.sb("MG", [P, GH, NC]))
                    c.SH, c.NEGM = t.sb("SH", [NC * GH, 2, P]), t.sb("NEGM", [NC * GH, 2, NS, P], BF16)
                    c.OF = t.sb("OF", [P, 512])
                    m.stage(attention, c, scratch)
                with Scope(nc, m.sem) as t:
                    c.WP, c.W1, c.W2 = t.sb("WP", [P, D]), t.sb("W1", [P, F1]), t.sb("W2", [P, NB1, D])
                    c.H, c.VF, c.FP = (t.sb("H2", [P, B, D]), t.sb("VF2", [P, B, NF * D]),
                                       t.sb("FP2", [P, B, NF, D]))
                    c.PF, c.DEN, c.X1 = (t.sb("PF", [P, B, NF * H1]), t.sb("DEN2", [P, B, H1]),
                                         t.sb("X1", [P, B, D]))
                    c.GE = t.sb("GE", [P, 2, NB1, 256])
                    m.stage(attention_output, c, dram, scratch)
            c.HTA0 = a.sb("HTA0", [P, B * T])
            c.HTA = c.HTA0
            m.stage(experts_input, c, scratch)
        with Scope(nc, m.sem) as a:
            c.HTA = a.sb("HTA", [P, B * T])
            c.YT = c.HTA
            c.BG, c.AG = a.sb("BG", [P, 64, SB]), a.sb("AG", [P, 64, SB])
            c.HD, c.XD = a.sb("HD", [P, PAIRS, 64]), a.sb("XD", [P, 2, BP, P])
            c.T2, c.WGT = a.sb("T2", [P, 2, BP, P]), a.sb("WGT", [P, 2, SB])
            c.TWO, c.LOW = a.sb("TWO", [P, 2, 2048], BF16), a.sb("LOW", [P, 2, 2048], BF16)
            c.OH, c.OHW = a.sb("OH", [P, 2, GR, 2, E1]), a.sb("OHW", [P, 2, GR, E1])
            c.OHT, c.OHTW = a.sb("OHT", [P, 2, 512], BF16), a.sb("OHTW", [E1, 2, 512])
            c.OHB, c.OHBW = a.sb("OHB", [P, 2, 2 * SB], BF16), a.sb("OHBW", [E1, 2, 2 * SB])
            c.WUR, c.LG1 = a.sb("WUR", [P, 8, E1]), a.sb("LG1", [P, GR, E1])
            c.TOP1, c.TIX1 = a.sb("TOP1", [P, GR, 8]), a.sb("TIX1", [P, GR, 8], U32)
            c.TIF1, c.PR, c.IOTA1 = a.sb("TIF1", [P, GR, 2]), a.sb("PR", [P, GR, 3]), a.sb("IOTA1", [P, E1])
            c.SCL, c.BUP, c.BDN = a.sb("SCL", [P, 2]), a.sb("BUP", [P, 64]), a.sb("BDN", [P, 8])
            c.LT = a.sb("LT", [P, PAIRS])
            c.XC, c.YB = c.BG[:, 0:B, :], c.BG[:, B:2 * B, :]
            m.stage(kronecker_loads, c, dram, scratch)
            m.stage(route, c, "ru", lambda pe: up_logits(nc, c))
            m.stage(kronecker, c, True)
            m.stage(down_logits, c, dram)
            m.stage(route, c, "rd", lambda pe: down_turned(nc, c))
            m.stage(kronecker, c, False)
            m.stage(experts_output, c, scratch, out)


_INS = ['L0_attn_x', 'L0_attn_wq', 'L0_attn_bq', 'L0_attn_wk', 'L0_attn_bk', 'L0_attn_wv', 'L0_attn_bv',
        'L0_attn_wo', 'L0_attn_bo', 'L0_wmod', 'L1_wmod',
        'L0_ffn_w_gate', 'L0_ffn_w_up', 'L0_ffn_w_down', 'L0_ffn_sw_gate', 'L0_ffn_sw_up', 'L0_ffn_sw_down',
        'L1_attn_W_qkvf', 'L1_attn_W_ff1', 'L1_attn_W_ff2', 'L1_attn_ln1_g', 'L1_attn_ln1_b',
        'L1_attn_ln2_g', 'L1_attn_ln2_b', 'L1_ffn_A_up', 'L1_ffn_B_up', 'L1_ffn_A_down', 'L1_ffn_B_down',
        'L1_ffn_scale_up', 'L1_ffn_scale_down']


def layout(inputs):
    arrays = {name: np.ascontiguousarray(inputs[name]) for name in _INS}
    for name in ("L0_c", "L1_c", "L0_ffn_router_w", "L0_ffn_gate_w"):
        arrays[name] = np.ascontiguousarray(np.transpose(inputs[name]))
    for name in ("L1_attn_W_qkvf", "L1_attn_W_proj"):
        arrays[name + "_T"] = np.ascontiguousarray(np.transpose(inputs[name]))
    arrays["L1_attn_W_conv"] = np.ascontiguousarray(np.transpose(inputs["L1_attn_W_conv"], (1, 2, 0)))
    move = lambda name, shape, axes: np.ascontiguousarray(
        np.transpose(np.reshape(np.asarray(inputs[name]), shape), axes))
    arrays["L1_ffn_W_up"] = move("L1_ffn_W_up", (64, 8, D), (2, 1, 0))
    arrays["L1_ffn_W_down"] = move("L1_ffn_W_down", (64, 64, 64), (2, 1, 0))
    arrays["L1_ffn_bias_up"] = move("L1_ffn_bias_up", (64, 64), (1, 0))
    arrays["L1_ffn_bias_down"] = move("L1_ffn_bias_down", (8, D), (1, 0))
    return arrays


def kernel(**inputs):
    import concourse.bacc as bacc
    from concourse.bass_utils import run_bass_kernel_spmd

    nc = bacc.Bacc("TRN2", target_bir_lowering=False, num_devices=1)
    arrays = layout(inputs)
    dram = {name: nc.dram_tensor(f"in_{name}", a.shape, mybir.dt.from_np(a.dtype), kind="ExternalInput").ap()
            for name, a in arrays.items()}
    out = nc.dram_tensor("out_x", (B, T, D), F32, kind="ExternalOutput").ap()
    build(nc, dram, out)
    r = run_bass_kernel_spmd(nc, [{f"in_{name}": a for name, a in arrays.items()}], core_ids=[0])
    return r.results[0]["out_x"]
```

```python
from contextlib import ExitStack

import numpy as np
import concourse.bass as bass
from concourse import mybir

F32 = mybir.dt.float32
BF16 = mybir.dt.bfloat16
U32 = mybir.dt.uint32
ALU = mybir.AluOpType
ACT = mybir.ActivationFunctionType
X_AXIS = mybir.AxisListType.X

P = 128
D = 128
B, T = 4, 1024
NC = T // P
CH = B * NC
W = B * P
EPS = 1e-5
SHIFT_A, SCALE_A, GATE_A, SHIFT_B, SCALE_B, GATE_B = range(6)

def done(i, per=1, k=0):
    return i * per + k + 2


def before(i, per=1, k=0):
    return i * per + k + 1


def stored(i, per=16):
    return i * per + per


class Mem:

    def __init__(self, nc, ctx):
        self.nc, self.ctx, self.sems = nc, ctx, []

    def sb(self, name, shape, dt=F32):
        return self.ctx.enter_context(self.nc.sbuf_tensor(name, shape, dt))

    def ps(self, name, shape, dt=F32):
        return self.ctx.enter_context(self.nc.psum_tensor(name, shape, dt))

    def sem(self, name):
        handle = self.nc.alloc_semaphore(name=name)
        self.sems.append(handle)
        return handle

    def stage(self, f, *args):
        kept, self.sems = self.sems, []
        f(self.nc, self, *args)
        self.nc.clear_and_free_semaphores(self.sems)
        self.nc.all_engine_barrier()
        self.sems = kept


def at(ap, i):
    return ap[:, :, bass.ds(i, 1), :].rearrange("p a o d -> p a (o d)")


def bcast(ap, shape):
    return ap.broadcast_to(shape)


def setup(nc, m, c, dram):
    loaded, cond_loaded = m.sem("loaded"), m.sem("cond_loaded")
    silu_done, bc_done, masks = m.sem("silu_done"), m.sem("bc_done"), m.sem("masks")
    cols_mm, cols_out = m.sem("cols_mm"), m.sem("cols_out")
    rows_mm, rows_out, fix = m.sem("rows_mm"), m.sem("rows_out"), m.sem("fix")
    loads = [
        (c.WQKV[:, 0:64], dram["L0_attn_wq"]), (c.WQKV[:, 64:128], dram["L0_attn_wk"]),
        (c.WQKV[:, 128:256], dram["L0_attn_wv"]), (c.WO[:, :], dram["L0_attn_wo"]),
        (c.BQKV[:, 0:64], dram["L0_attn_bq"].partition_broadcast(P)),
        (c.BQKV[:, 64:128], dram["L0_attn_bk"].partition_broadcast(P)),
        (c.BQKV[:, 128:256], dram["L0_attn_bv"].partition_broadcast(P)),
        (c.BO[:, :], dram["L0_attn_bo"].partition_broadcast(P)),
        (c.X[:, :, :], dram["L0_attn_x"].rearrange("b (n p) d -> p (b n) d", p=P)),
    ]
    cond = [
        (c.COND[:, 0, :], dram["L0_c"]),
        (c.COND[:, 1, :], dram["L1_c"]),
        (c.WMOD[:, 0, :], dram["L0_wmod"]), (c.WMOD[:, 1, :], dram["L1_wmod"]),
    ]
    ROWS = [(l, b) for l in range(2) for b in range(B)]
    with nc.Block() as block:

        @block.sync
        def _(sp):
            for dst, src in cond:
                sp.dma_start(dst, src).then_inc(cond_loaded, 16)
            for dst, src in loads:
                sp.dma_start(dst, src).then_inc(loaded, 16)
            sp.wait_ge(loaded, 16 * len(loads))

        @block.gpsimd
        def _(pool):
            nc.gpsimd.memset(c.IDENT[:, :], 0.0).then_inc(masks, 1)
            nc.gpsimd.memset(c.ONES[:, :], 1.0).then_inc(masks, 1)
            nc.gpsimd.memset(c.HALF[:, :], -0.5)
            nc.gpsimd.memset(c.EPS[:, :], EPS)
            nc.gpsimd.iota(c.IOTA[:, :], [[1, 8]], base=0, channel_multiplier=0,
                           allow_small_or_imprecise_dtypes=True)
            nc.gpsimd.memset(c.ZERO[:, :], 0.0).then_inc(masks, 1)
            pool.wait_ge(masks, 3)
            nc.gpsimd.affine_select(out=c.IDENT[:, :], in_=c.IDENT[:, :], compare_op=ALU.not_equal,
                                    fill=1.0, base=0, pattern=[[-1, P]], channel_multiplier=1)
            nc.gpsimd.affine_select(out=c.IDENTB[:, :], in_=c.ZERO[:, :], compare_op=ALU.not_equal,
                                    fill=1.0, base=0, pattern=[[-1, P]], channel_multiplier=1)
            nc.gpsimd.affine_select(out=c.UPTO[:, :], in_=c.ONES[:, :], compare_op=ALU.is_ge,
                                    fill=0.0, base=0, pattern=[[1, P]], channel_multiplier=-1)
            nc.gpsimd.affine_select(out=c.LATER[:, :], in_=c.ZERO[:, :], compare_op=ALU.is_ge,
                                    fill=-1e30, base=0, pattern=[[-1, P]],
                                    channel_multiplier=1).then_inc(masks, 1)

        @block.scalar
        def _(act):
            act.wait_ge(cond_loaded, 16 * len(cond))
            nc.scalar.activation(c.COND[:, :, :], c.COND[:, :, :], ACT.Silu).then_inc(silu_done, 1)
            for n, (l, b) in enumerate(ROWS):
                act.wait_ge(rows_mm, n + 1)
                k = 2 * (n % 2)
                nc.scalar.copy(c.MROW[:, l, b, 0:4, :],
                               c.PS[:, k, :].rearrange("p (j d) -> p j d", d=D))
                nc.scalar.copy(c.MROW[:, l, b, 4:6, :],
                               c.PS[:, k + 1, 0:256].rearrange("p (j d) -> p j d", d=D)
                               ).then_inc(rows_out, 1)

        @block.vector
        def _(dve):
            dve.wait_ge(silu_done, 1)
            for n, (l, b) in enumerate(ROWS):
                nc.vector.tensor_copy(c.CB[:, n, :], bcast(c.COND[:, l, b:b + 1], [P, P])
                                      ).then_inc(bc_done, 1)
            dve.wait_ge(cols_mm, 1)
            nc.vector.tensor_copy(c.MCOL[:, :, :, :], c.PS[:, 4, 0:48].rearrange(
                "p (l j b) -> p l j b", l=2, j=6)).then_inc(cols_out, 1)
            dve.wait_ge(cols_out, 1)
            for j in (SCALE_A, SCALE_B):
                nc.vector.tensor_scalar_add(c.MCOL[:, :, j, :], c.MCOL[:, :, j, :], 1.0)
            dve.wait_ge(rows_out, len(ROWS))
            for j in (SCALE_A, SCALE_B):
                nc.vector.tensor_scalar_add(c.MROW[:, :, :, j, :], c.MROW[:, :, :, j, :], 1.0)
            k = 0
            for j in (GATE_A, GATE_B):
                g = c.MROW[:, :, :, j, :].rearrange("p l b d -> p (l b) d")
                nc.vector.tensor_scalar(c.CB[:, :, :], g, 0.0, 2.0, ALU.is_ge, ALU.mult).then_inc(fix, 1)
                nc.vector.tensor_scalar(c.CB2[:, :, :], g, -1.0, None, ALU.mult).then_inc(fix, 1)
                dve.wait_ge(fix, k + 2)
                nc.vector.tensor_scalar_add(c.CB[:, :, :], c.CB[:, :, :], -1.0).then_inc(fix, 1)
                nc.vector.tensor_tensor(c.CB2[:, :, :], c.CB2[:, :, :], g, ALU.max).then_inc(fix, 1)
                dve.wait_ge(fix, k + 4)
                nc.vector.scalar_tensor_tensor(g, c.CB2[:, :, :], 0.25, c.CB[:, :, :], ALU.max,
                                               ALU.mult).then_inc(fix, 1)
                dve.wait_ge(fix, k + 5)
                k += 5
            nc.vector.tensor_copy(c.GATE[:, :, :], c.MROW[:, 1, :, GATE_B, :])

        @block.tensor
        def _(pe):
            pe.wait_ge(silu_done, 1)
            for l in range(2):
                for j in range(6):
                    o = (l * 6 + j) * B
                    last = nc.tensor.matmul(c.PS[:, 4, o:o + B], c.WMOD[:, l, j * D:(j + 1) * D],
                                            c.COND[:, l, :], start=True, stop=True)
            last.then_inc(cols_mm, 1)
            for n, (l, b) in enumerate(ROWS):
                pe.wait_ge(bc_done, n + 1)
                if n >= 2:
                    pe.wait_ge(rows_out, n - 1)
                k = 2 * (n % 2)
                nc.tensor.matmul(c.PS[:, k, :], c.CB[:, n, :], c.WMOD[:, l, 0:512], start=True, stop=True)
                nc.tensor.matmul(c.PS[:, k + 1, 0:256], c.CB[:, n, :], c.WMOD[:, l, 512:768],
                                 start=True, stop=True).then_inc(rows_mm, 1)


HALF_BATCHES = ((0, slice(0, 2), (0, 1)), (1, slice(2, 4), (2, 3)))


def ln_stats(nc, dve, c, s, src, i):
    for _, _, batches in HALF_BATCHES:
        for b in batches:
            ins = nc.vector.bn_stats(c.ST[:, b, :], src(b))
        ins.then_inc(s.stats, 1)
    for h, _, batches in HALF_BATCHES:
        dve.wait_ge(s.stats, done(i, 2, h))
        dve.sem_inc(c.passed, 1)
        for b in batches:
            ins = nc.vector.bn_aggr(c.MV[:, b, :], c.ST[:, b, :])
        ins.then_inc(s.moments, 1)


def ln_rstd(nc, pool, c, s, i):
    for h, half, _ in HALF_BATCHES:
        pool.wait_ge(s.moments, done(i, 2, h))
        nc.gpsimd.tensor_tensor(c.VE[:, half], c.MV[:, half, 1], c.EPS[:, half], ALU.add).then_inc(s.var_eps, 1)
        pool.wait_ge(s.var_eps, done(i, 2, h))
        nc.gpsimd.tensor_tensor(c.RSTD[:, half], c.VE[:, half], c.HALF[:, half], ALU.pow).then_inc(s.rstd, 1)


def ln_apply(nc, dve, c, s, src, dst, i):
    for h, _, batches in HALF_BATCHES:
        dve.wait_ge(s.rstd, done(i, 2, h))
        for b in batches:
            ins = nc.vector.tensor_scalar(dst(b), src(b), c.MV[:, b, 0:1], c.RSTD[:, b:b + 1],
                                          ALU.subtract, ALU.mult)
        ins.then_inc(s.normed, 1)


def turn_half(nc, c, bank, offset, src, batches):
    for n, b in enumerate(batches):
        ins = nc.tensor.transpose(c.PS[:, bank, offset + n * P:offset + (n + 1) * P], src[:, b, :], c.IDENT[:, :])
    return ins


def one_ahead(engine, front, back):
    front(0)
    with engine.Fori(0, NC - 1) as i:
        front(i + 1)
        back(i)
    back(NC - 1)


class LnSems:
    def __init__(self, m, tag):
        self.stats, self.moments = m.sem(tag + "_stats"), m.sem(tag + "_moments")
        self.var_eps, self.rstd = m.sem(tag + "_var_eps"), m.sem(tag + "_rstd")
        self.normed = m.sem(tag + "_normed")

    def dve(self):
        return [self.stats, self.moments, self.normed]

    def pool(self):
        return [self.var_eps, self.rstd]


def credit(engine, sems):
    for s in sems:
        engine.sem_inc(s, 1)


def linear_attention(nc, m, c, dram):
    H, F, G = 16, 4, 8
    ln = LnSems(m, "la")
    turned, h_ready, qkv_mm, qkv_out = (m.sem("la_" + n) for n in ("turned", "h_ready", "qkv_mm", "qkv_out"))
    neg_done, exp_done, phi_done = (m.sem("la_" + n) for n in ("neg", "exp", "phi"))
    kv_dve, kv_pool, cum_mm, sum_done = (m.sem("la_" + n) for n in ("kv_dve", "kv_pool", "cum_mm", "sum"))
    prod_done, red_done, den_done, rec_done, o_done = (
        m.sem("la_" + n) for n in ("prod", "red", "den", "rec", "o"))
    o_turned, o_out, proj_mm, y_done, gated, res_done = (
        m.sem("la_" + n) for n in ("o_turned", "o_out", "proj", "y", "gated", "res"))
    X4 = c.X[:, :, :].rearrange("p (b n) d -> p b n d", b=B)
    two = lambda h, o, n: c.PS[:, h, o:o + 2 * n].rearrange("p (b n) -> p b n", b=2)

    def kv_product(engine, b):
        k = c.PHI[:, b, 64:128].rearrange("p (h f) -> p h f", f=F).unsqueeze(3)
        v = c.QKV[:, b, 128:256].rearrange("p (h g) -> p h g", g=G).unsqueeze(2)
        return engine.tensor_tensor(c.KVP[:, b, :].rearrange("p (h f g) -> p h f g", h=H, f=F),
                                    bcast(k, [P, H, F, G]), bcast(v, [P, H, F, G]), ALU.mult)

    with nc.Block() as block:

        @block.sync
        def _(sp):
            for dst, src in load_experts(nc, m, c, dram):
                sp.dma_start(dst, src).then_inc(c.experts_loaded, 16)

        @block.vector
        def _(dve):
            credit(dve, ln.dve() + [qkv_out, neg_done, phi_done, kv_dve, prod_done, red_done,
                                    den_done, rec_done, o_done, y_done])

            def norm(i):
                xi = at(X4, i)
                ln_stats(nc, dve, c, ln, lambda b: xi[:, b, :], i)
                dve.wait_ge(turned, before(i, 2))
                ln_apply(nc, dve, c, ln, lambda b: xi[:, b, :], lambda b: c.XN[:, b, :], i)

            def chunk(i, last_one):
                for h, half, batches in HALF_BATCHES:
                    dve.wait_ge(qkv_mm, done(i, 2, h))
                    nc.vector.tensor_tensor(c.QKV[:, half, :], two(2 * h + 1, 0, 256),
                                            bcast(c.BQKV[:, :].unsqueeze(1), [P, 2, 256]), ALU.add
                                            ).then_inc(qkv_out, 1)
                    dve.wait_ge(qkv_out, done(i, 2, h))
                    nc.vector.tensor_scalar(c.NEG[:, half, :], c.QKV[:, half, 0:128], 0.0, None, ALU.min
                                            ).then_inc(neg_done, 1)
                for h, half, batches in HALF_BATCHES:
                    dve.wait_ge(exp_done, done(i, 2, h))
                    dve.wait_ge(sum_done, i * 2 + (h + 1))
                    nc.vector.scalar_tensor_tensor(c.PHI[:, half, :], c.QKV[:, half, 0:128], 0.0, c.NEG[:, half, :],
                                                   ALU.max, ALU.add).then_inc(phi_done, 1)
                    dve.wait_ge(phi_done, done(i, 2, h))
                    kv_product(nc.vector, batches[0]).then_inc(kv_dve, 1)
                if not last_one:
                    norm(i + 1)
                for h, half, batches in HALF_BATCHES:
                    dve.wait_ge(cum_mm, done(i, 2, h))
                    for b in batches:
                        q = c.PHI[:, b, 0:64].rearrange("p (h f) -> p h f", f=F).unsqueeze(3)
                        nc.vector.tensor_tensor(
                            c.PROD[:, b, :].rearrange("p (h f g) -> p h f g", h=H, f=F),
                            c.PS[:, 4 + b, :].rearrange("p (h f g) -> p h f g", h=H, f=F),
                            bcast(q, [P, H, F, G]), ALU.mult)
                    nc.vector.tensor_tensor(c.KPROD[:, half, :], two(2 * h, 0, 64), c.PHI[:, half, 0:64], ALU.mult
                                            ).then_inc(prod_done, 1)
                    dve.wait_ge(prod_done, done(i, 2, h))
                    den = slice(h * 2 * H, (h + 1) * 2 * H)
                    nc.vector.tensor_reduce(c.DEN[:, den], c.KPROD[:, half, :].rearrange(
                        "p b (h f) -> p (b h) f", f=F), X_AXIS, ALU.add).then_inc(red_done, 1)
                    for b in batches:
                        last = nc.vector.tensor_reduce(
                            c.NUM[:, b, :], c.PROD[:, b, :].rearrange("p (h f g) -> p h g f", h=H, f=F),
                            X_AXIS, ALU.add)
                    last.then_inc(red_done, 1)
                    dve.wait_ge(red_done, done(i, 4, 2 * h))
                    nc.vector.tensor_scalar_add(c.DEN[:, den], c.DEN[:, den], 1e-6).then_inc(den_done, 1)
                    dve.wait_ge(den_done, done(i, 2, h))
                    nc.vector.reciprocal(c.REC[:, den], c.DEN[:, den]).then_inc(rec_done, 1)
                    dve.wait_ge(rec_done, done(i, 2, h))
                    dve.wait_ge(red_done, done(i, 4, 2 * h + 1))
                    nc.vector.tensor_tensor(c.O[:, half, :].rearrange("p b (h g) -> p (b h) g", g=G),
                                            c.NUM[:, half, :].rearrange("p b (h g) -> p (b h) g", g=G),
                                            bcast(c.REC[:, den].unsqueeze(2), [P, 2 * H, G]), ALU.mult
                                            ).then_inc(o_done, 1)
                for h, half, batches in HALF_BATCHES:
                    dve.wait_ge(proj_mm, done(i, 2, h))
                    nc.vector.tensor_tensor(c.Y[:, half, :], two(2 * h + 1, 0, D),
                                            bcast(c.BO[:, :].unsqueeze(1), [P, 2, D]), ALU.add
                                            ).then_inc(y_done, 1)

            norm(0)
            with dve.Fori(0, NC - 1) as i:
                chunk(i, False)
            chunk(NC - 1, True)

        @block.gpsimd
        def _(pool):
            credit(pool, ln.pool() + [kv_pool, gated, res_done])
            nc.gpsimd.memset(c.KVSUM[:, :, :], 0.0)
            nc.gpsimd.memset(c.KSUM[:, :, :], 0.0).then_inc(sum_done, 2)

            def chunk(i, last_one):
                for h, half, batches in HALF_BATCHES:
                    pool.wait_ge(phi_done, done(i, 2, h))
                    kv_product(nc.gpsimd, batches[1]).then_inc(kv_pool, 1)
                if not last_one:
                    ln_rstd(nc, pool, c, ln, i + 1)
                for h, half, batches in HALF_BATCHES:
                    pool.wait_ge(kv_pool, done(i, 2, h))
                    pool.wait_ge(kv_dve, done(i, 2, h))
                    pool.wait_ge(cum_mm, done(i, 2, h))
                    nc.gpsimd.tensor_tensor(c.KVSUM[:, half, :], c.KVSUM[:, half, :], c.KVP[:, half, :], ALU.add)
                    nc.gpsimd.tensor_tensor(c.KSUM[:, half, :], c.KSUM[:, half, :], c.PHI[:, half, 64:128], ALU.add
                                            ).then_inc(sum_done, 1)
                xi = at(X4, i)
                for h, half, batches in HALF_BATCHES:
                    pool.wait_ge(y_done, done(i, 2, h))
                    nc.gpsimd.tensor_tensor(c.Y[:, half, :], c.Y[:, half, :], c.MROW[:, 0, half, GATE_A, :], ALU.mult
                                            ).then_inc(gated, 1)
                    pool.wait_ge(gated, done(i, 2, h))
                    nc.gpsimd.tensor_tensor(xi[:, half, :], xi[:, half, :], c.Y[:, half, :], ALU.add
                                            ).then_inc(res_done, 1)

            ln_rstd(nc, pool, c, ln, 0)
            with pool.Fori(0, NC - 1) as i:
                chunk(i, False)
            chunk(NC - 1, True)

        @block.scalar
        def _(act):
            credit(act, [h_ready, exp_done, o_out])
            with act.Fori(0, NC) as i:
                for h, half, batches in HALF_BATCHES:
                    act.wait_ge(turned, done(i, 2, h))
                    for n, b in enumerate(batches):
                        last = nc.scalar.activation(c.HT[:, b, :], c.PS[:, 2 * h, n * P:(n + 1) * P], ACT.Identity,
                                                    scale=c.MCOL[:, 0, SCALE_A, b:b + 1],
                                                    bias=c.MCOL[:, 0, SHIFT_A, b:b + 1])
                    last.then_inc(h_ready, 1)
                for h, half, batches in HALF_BATCHES:
                    act.wait_ge(neg_done, done(i, 2, h))
                    nc.scalar.activation(c.NEG[:, half, :], c.NEG[:, half, :], ACT.Exp).then_inc(exp_done, 1)
                for h, half, batches in HALF_BATCHES:
                    act.wait_ge(o_turned, done(i, 2, h))
                    nc.scalar.copy(c.OT[:, half, :], two(2 * h, 256, P)).then_inc(o_out, 1)

        @block.tensor
        def _(pe):
            credit(pe, [turned, qkv_mm, cum_mm, o_turned, proj_mm])
            with pe.Fori(0, NC) as i:
                for h, half, batches in HALF_BATCHES:
                    pe.wait_ge(ln.normed, done(i, 2, h))
                    turn_half(nc, c, 2 * h, 0, c.XN, batches).then_inc(turned, 1)
                pe.wait_ge(y_done, before(i, 2))
                for h, half, batches in HALF_BATCHES:
                    pe.wait_ge(h_ready, done(i, 2, h))
                    for n, b in enumerate(batches):
                        last = nc.tensor.matmul(c.PS[:, 2 * h + 1, 256 * n:256 * n + 256], c.HT[:, b, :],
                                                c.WQKV[:, :], start=True, stop=True)
                    last.then_inc(qkv_mm, 1)
                for h, half, batches in HALF_BATCHES:
                    pe.wait_ge(sum_done, i * 2 + (h + 1))
                    pe.wait_ge(phi_done, done(i, 2, h))
                    kp = c.PS[:, 2 * h, 0:128]
                    nc.tensor.matmul(kp, c.UPTO[:, :], c.PHI[:, half, 64:128], start=True, stop=False)
                    nc.tensor.matmul(kp, c.ONES[:, :], c.KSUM[:, half, :], start=False, stop=True)
                    pe.wait_ge(kv_dve, done(i, 2, h))
                    pe.wait_ge(kv_pool, done(i, 2, h))
                    for b in batches:
                        nc.tensor.matmul(c.PS[:, 4 + b, :], c.UPTO[:, :], c.KVP[:, b, :], start=True, stop=False)
                        last = nc.tensor.matmul(c.PS[:, 4 + b, :], c.ONES[:, :], c.KVSUM[:, b, :],
                                                start=False, stop=True)
                    last.then_inc(cum_mm, 1)
                for h, half, batches in HALF_BATCHES:
                    pe.wait_ge(o_done, done(i, 2, h))
                    turn_half(nc, c, 2 * h, 256, c.O, batches).then_inc(o_turned, 1)
                for h, half, batches in HALF_BATCHES:
                    pe.wait_ge(o_out, done(i, 2, h))
                    for n, b in enumerate(batches):
                        last = nc.tensor.matmul(c.PS[:, 2 * h + 1, n * P:(n + 1) * P], c.OT[:, b, :], c.WO[:, :],
                                                start=True, stop=True)
                    last.then_inc(proj_mm, 1)


NE0, F0 = 8, 256


def load_experts(nc, m, c, dram):
    return [
        (c.WR[:, 0:8], dram["L0_ffn_router_w"]), (c.WR[:, 8:9], dram["L0_ffn_gate_w"]),
        (c.WG[:, 0:NE0, :], dram["L0_ffn_w_gate"].rearrange("e d f -> d e f")),
        (c.WU[:, 0:NE0, :], dram["L0_ffn_w_up"].rearrange("e d f -> d e f")),
        (c.WD[:, 0:NE0, :, :], dram["L0_ffn_w_down"].rearrange("e (k p) d -> p e k d", p=P)),
        (c.WG[:, NE0, :], dram["L0_ffn_sw_gate"]), (c.WU[:, NE0, :], dram["L0_ffn_sw_up"]),
        (c.WD[:, NE0, :, :], dram["L0_ffn_sw_down"].rearrange("(k p) d -> p k d", p=P)),
    ]


def experts(nc, m, c, dram):
    NE = NE0 + 1
    OUT_BANK = [6] * NE0 + [2 * ((NE0 - 1) % 2)]
    ln = LnSems(m, "ex")
    turned, h_ready, logit_mm, logit_out = (m.sem("ex_" + n) for n in ("turned", "h_ready", "logit_mm", "logit_out"))
    top_done, idx_done, idx_f, shifted, exp_done = (
        m.sem("ex_" + n) for n in ("top", "idx", "idx_f", "shifted", "exp"))
    hot, sum_done, rec_done, cw_done = (m.sem("ex_" + n) for n in ("hot", "sum", "rec", "cw"))
    gate_mm, up_mm, silu_done, mul_done, down_mm, acc_done = (
        m.sem("ex_" + n) for n in ("gate_mm", "up_mm", "silu", "mul", "down_mm", "acc"))
    y_done, res_done = m.sem("ex_y"), m.sem("ex_res")
    X4 = c.X[:, :, :].rearrange("p (b n) d -> p b n d", b=B)
    HT = c.HT[:, :, :].rearrange("p b t -> p (b t)")
    loaded, loads = c.experts_loaded, load_experts(nc, m, c, dram)

    with nc.Block() as block:

        @block.vector
        def _(dve):
            credit(dve, ln.dve() + [logit_out, top_done, idx_done, idx_f, shifted, hot, sum_done,
                                    rec_done, cw_done, mul_done, acc_done, y_done])

            def stats(i):
                xi = at(X4, i)
                ln_stats(nc, dve, c, ln, lambda b: xi[:, b, :], i)

            def apply(i):
                xi = at(X4, i)
                dve.wait_ge(turned, before(i))
                ln_apply(nc, dve, c, ln, lambda b: xi[:, b, :], lambda b: c.XN[:, b, :], i)

            def chunk(i, last_one):
                xi = at(X4, i)
                dve.wait_ge(logit_mm, done(i))
                nc.vector.tensor_copy(c.LG[:, :, :], c.PS[:, 7, 0:64].rearrange("p (b e) -> p b e", b=B)[:, :, 0:9]
                                      ).then_inc(logit_out, 1)
                dve.wait_ge(logit_out, done(i))
                dve.sem_inc(c.passed, 1)
                for b in range(B):
                    last = nc.vector.max(c.TOP[:, b, :], c.LG[:, b, 0:8])
                last.then_inc(top_done, 1)
                dve.wait_ge(top_done, done(i))
                nc.vector.tensor_tensor(c.EX[:, :, 0:8], c.LG[:, :, 0:8], bcast(c.TOP[:, :, 0:1], [P, B, 8]),
                                        ALU.subtract)
                nc.vector.tensor_scalar(c.EX[:, :, 8:9], c.LG[:, :, 8:9], -1.0, None, ALU.mult
                                        ).then_inc(shifted, 1)
                for b in range(B):
                    last = nc.vector.max_index(c.TIX[:, b, :], c.TOP[:, b, :], c.LG[:, b, 0:8])
                last.then_inc(idx_done, 1)
                dve.wait_ge(idx_done, done(i))
                nc.vector.tensor_copy(c.TIF[:, :, :], c.TIX[:, :, 0:2]).then_inc(idx_f, 1)
                dve.wait_ge(idx_f, done(i))
                for k in range(2):
                    last = nc.vector.tensor_tensor(c.HOT[:, k, :, :], bcast(c.IOTA[:, :].unsqueeze(1), [P, B, 8]),
                                                   bcast(c.TIF[:, :, k:k + 1], [P, B, 8]), ALU.is_equal)
                last.then_inc(hot, 1)
                def weights():
                    dve.wait_ge(hot, done(i))
                    dve.wait_ge(exp_done, done(i))
                    nc.vector.tensor_reduce(c.SUM[:, :, 0:1], c.EX[:, :, 0:8], X_AXIS, ALU.add)
                    nc.vector.tensor_scalar_add(c.SUM[:, :, 1:2], c.EX[:, :, 8:9], 1.0)
                    nc.vector.tensor_tensor(c.HOT[:, 0, :, :], c.HOT[:, 0, :, :], c.HOT[:, 1, :, :], ALU.add
                                            ).then_inc(sum_done, 1)
                    dve.wait_ge(sum_done, done(i))
                    nc.vector.reciprocal(c.RS[:, :, :], c.SUM[:, :, :])
                    nc.vector.tensor_tensor(c.HOT[:, 0, :, :], c.HOT[:, 0, :, :], c.EX[:, :, 0:8], ALU.mult
                                            ).then_inc(rec_done, 1)
                    dve.wait_ge(rec_done, done(i))
                    nc.vector.tensor_tensor(c.CW[:, :, 0:8], c.HOT[:, 0, :, :], bcast(c.RS[:, :, 0:1], [P, B, 8]),
                                            ALU.mult)
                    nc.vector.tensor_copy(c.CW[:, :, 8:9], c.RS[:, :, 1:2]).then_inc(cw_done, 1)

                def accumulate(e):
                    dve.wait_ge(down_mm, done(i, NE, e))
                    if e == 0:
                        dve.wait_ge(cw_done, done(i))
                    else:
                        dve.wait_ge(acc_done, done(i, NE, e - 1))
                    for b in range(B):
                        y = c.PS[:, OUT_BANK[e], b * P:(b + 1) * P]
                        if e == 0:
                            last = nc.vector.tensor_scalar(c.Y[:, b, :], y, c.CW[:, b, e:e + 1], None, ALU.mult)
                        else:
                            last = nc.vector.scalar_tensor_tensor(c.Y[:, b, :], y, c.CW[:, b, e:e + 1],
                                                                  c.Y[:, b, :], ALU.mult, ALU.add)
                    last.then_inc(acc_done, 1)

                for e in range(NE):
                    dve.wait_ge(silu_done, done(i, NE, e))
                    dve.wait_ge(up_mm, done(i, NE, e))
                    nc.vector.tensor_tensor(c.HH[:, e % 2, :, :], c.PS[:, 4:6, :], c.SG[:, e % 2, :, :],
                                            ALU.mult).then_inc(mul_done, 1)
                    if e == 0:
                        weights()
                    if e >= 1:
                        accumulate(e - 1)
                    if e == 3 and not last_one:
                        stats(i + 1)
                    if e == 4 and not last_one:
                        apply(i + 1)
                accumulate(NE - 1)
                dve.wait_ge(acc_done, done(i, NE, NE - 1))
                nc.vector.tensor_tensor(c.Y[:, :, :], c.Y[:, :, :], c.MROW[:, 0, :, GATE_B, :], ALU.mult
                                        ).then_inc(y_done, 1)
                dve.wait_ge(y_done, done(i))
                nc.vector.tensor_tensor(xi, xi, c.Y[:, :, :], ALU.add)

            stats(0)
            apply(0)
            with dve.Fori(0, NC - 1) as i:
                chunk(i, False)
            chunk(NC - 1, True)

        @block.gpsimd
        def _(pool):
            credit(pool, ln.pool())
            with pool.Fori(0, NC) as i:
                ln_rstd(nc, pool, c, ln, i)

        @block.scalar
        def _(act):
            credit(act, [h_ready, exp_done, silu_done])
            with act.Fori(0, NC) as i:
                act.wait_ge(turned, done(i))
                act.wait_ge(up_mm, before(i, NE))
                for b in range(B):
                    last = nc.scalar.activation(c.HT[:, b, :], c.PS[:, 7, b * P:(b + 1) * P], ACT.Identity,
                                                scale=c.MCOL[:, 0, SCALE_B, b:b + 1],
                                                bias=c.MCOL[:, 0, SHIFT_B, b:b + 1])
                last.then_inc(h_ready, 1)
                act.wait_ge(shifted, done(i))
                nc.scalar.activation(c.EX[:, :, :], c.EX[:, :, :], ACT.Exp).then_inc(exp_done, 1)
                for e in range(NE):
                    act.wait_ge(gate_mm, done(i, NE, e))
                    k = 2 * (e % 2)
                    if e >= 2:
                        act.wait_ge(mul_done, done(i, NE, e - 2))
                    nc.scalar.activation(c.SG[:, e % 2, :, :], c.PS[:, k:k + 2, :], ACT.Silu
                                         ).then_inc(silu_done, 1)

        @block.tensor
        def _(pe):
            credit(pe, [turned, logit_mm, gate_mm, up_mm, down_mm])
            pe.wait_ge(loaded, 16 * len(loads))

            def turn(i):
                pe.wait_ge(logit_out, before(i))
                for h, _, batches in HALF_BATCHES:
                    pe.wait_ge(ln.normed, done(i, 2, h))
                    last = turn_half(nc, c, 7, h * 2 * P, c.XN, batches)
                last.then_inc(turned, 1)

            def chunk(i, last_one):
                pe.wait_ge(h_ready, done(i))
                for b in range(B):
                    last = nc.tensor.matmul(c.PS[:, 7, 16 * b:16 * b + 9], c.HT[:, b, :], c.WR[:, :],
                                            start=True, stop=True)
                last.then_inc(logit_mm, 1)

                def down(e):
                    pe.wait_ge(mul_done, done(i, NE, e))
                    if e and OUT_BANK[e] == OUT_BANK[e - 1]:
                        pe.wait_ge(acc_done, done(i, NE, e - 1))
                    for b in range(B):
                        for k in range(2):
                            last = nc.tensor.matmul(c.PS[:, OUT_BANK[e], b * P:(b + 1) * P],
                                                    c.HH[:, e % 2, k, b * P:(b + 1) * P], c.WD[:, e, k, :],
                                                    start=(k == 0), stop=(k == 1))
                    last.then_inc(down_mm, 1)

                for e in range(NE):
                    if e == 1:
                        pe.wait_ge(acc_done, before(i, NE))
                    if e >= 2:
                        pe.wait_ge(silu_done, done(i, NE, e - 2))
                    for k in range(2):
                        last = nc.tensor.matmul(c.PS[:, 2 * (e % 2) + k, :], c.WG[:, e, k * P:(k + 1) * P], HT,
                                                start=True, stop=True)
                    last.then_inc(gate_mm, 1)
                    if e >= 1:
                        pe.wait_ge(mul_done, done(i, NE, e - 1))
                    for k in range(2):
                        last = nc.tensor.matmul(c.PS[:, 4 + k, :], c.WU[:, e, k * P:(k + 1) * P], HT,
                                                start=True, stop=True)
                    last.then_inc(up_mm, 1)
                    if e >= 1:
                        down(e - 1)
                    if e == NE - 2 and not last_one:
                        turn(i + 1)
                down(NE - 1)

            turn(0)
            with pe.Fori(0, NC - 1) as i:
                chunk(i, False)
            chunk(NC - 1, True)


H1, HS, NF = 16, 8, 4
GH = 4
NG = H1 // GH
ROW_Q = (0, 0, 1, 1, 0, 2)
ROW_K = (0, 1, 0, 1, 2, 0)
NT = len(ROW_Q)
NS = 3
KM = 96
KA = KM + NS


def attention_inputs(nc, m, c, dram, scratch):
    lx, lh = LnSems(m, "ax"), LnSems(m, "ah")
    loaded, mask_done, bd_done = m.sem("ai_loaded"), m.sem("ai_mask"), m.sem("ai_bd")
    g_mm, g_out, big_mm, big_out = (m.sem("ai_" + n) for n in ("g_mm", "g_out", "big_mm", "big_out"))
    scaled, h_done, h_stored = m.sem("ai_scaled"), m.sem("ai_h"), m.sem("ai_h_stored")
    turned, z_ready, qk_mm, qk_out = (m.sem("ai_" + n) for n in ("turned", "z", "qk_mm", "qk_out"))
    rest1, part2, part3 = (m.sem("ai_" + n) for n in ("rest1", "part2", "part3"))
    part_stored = [m.sem(f"ai_part_stored{n}") for n in range(3)]
    tok_mm, qv_out, vf_out, vf_stored = (m.sem("ai_" + n) for n in ("tok_mm", "qv_out", "vf_out", "vf_stored"))
    prod_done, logit_done, v_kept, fmax_done = (m.sem("ai_" + n) for n in ("prod", "logit", "v_kept", "fmax"))
    X4 = c.X[:, :, :].rearrange("p (b n) d -> p b n d", b=B)
    V4 = c.VT[:, :, :].rearrange("p (b n) d -> p b n d", b=B)
    F4 = c.FUT[:, :, :].rearrange("p (b n) d -> p b n d", b=B)
    M4 = c.FMAX[:, :, :].rearrange("p (b n) d -> p b n d", b=B)
    ZT = c.HT[:, :, :].rearrange("p b t -> p (b t)")
    BANKS = ((3, 4, 5), (6, 7, 0))
    conv = dram["L1_attn_W_conv"]
    loads = [(c.WT[:, :], dram["L1_attn_W_qkvf_T"]), (c.WF[:, :], dram["L1_attn_W_qkvf"][3 * D:4 * D, :]),
             (c.LNG[:, 0:1], dram["L1_attn_ln1_g"].rearrange("(d o) -> d o", o=1)),
             (c.LNG[:, 1:2], dram["L1_attn_ln1_b"].rearrange("(d o) -> d o", o=1)),
             (c.LNG[:, 2:3], dram["L1_attn_ln2_g"].rearrange("(d o) -> d o", o=1)),
             (c.LNG[:, 3:4], dram["L1_attn_ln2_b"].rearrange("(d o) -> d o", o=1))]
    loads += [(c.CV[HS * h:HS * h + HS, :, :], conv) for h in range(H1)]

    with nc.Block() as block:

        @block.sync
        def _(sp):
            for dst, src in loads:
                sp.dma_start(dst, src).then_inc(loaded, 16)
            for s in [h_stored, vf_stored] + part_stored:
                sp.sem_inc(s, 16)

            def front(i):
                sp.wait_ge(h_done, done(i, 2, 1))
                sp.dma_start(scratch.h[:, bass.ds(i, 1), :, :].rearrange("b o p d -> p b (o d)"), c.H[:, :, :]
                             ).then_inc(h_stored, 16)

            def back(i):
                for n, made in enumerate((qk_out, part2, part3)):
                    sp.wait_ge(made, done(i))
                    sp.dma_start(scratch.qk[:, 8 * n:8 * n + 8, bass.ds(i * P, P)], c.PARTS[:, 8 * n:8 * n + 8, :]
                                 ).then_inc(part_stored[n], 16)
                sp.wait_ge(vf_out, done(i, B, B - 1))
                sp.dma_start(scratch.vf[:, bass.ds(i, 1), :, :].rearrange("b o p n -> p b (o n)"), c.VF[:, :, :]
                             ).then_inc(vf_stored, 16)
            one_ahead(sp, front, back)
            sp.wait_ge(h_stored, 16 * NC + 16)
            for s in part_stored:
                sp.wait_ge(s, 16 * NC + 16)
            sp.wait_ge(vf_stored, 16 * NC + 16)

        @block.vector
        def _(dve):
            credit(dve, lx.dve() + lh.dve() + [scaled, h_done, rest1, prod_done, logit_done, fmax_done])
            def front(i):
                xi = at(X4, i)
                ln_stats(nc, dve, c, lx, lambda b: xi[:, b, :], i)
                ln_apply(nc, dve, c, lx, lambda b: xi[:, b, :], lambda b: c.XN[:, b, :], i)
                for h, half, _ in HALF_BATCHES:
                    dve.wait_ge(lx.normed, done(i, 2, h))
                    nc.vector.tensor_tensor(c.Y[:, half, :], c.XN[:, half, :], c.MROW[:, 1, half, SCALE_A, :],
                                            ALU.mult).then_inc(scaled, 1)
                dve.wait_ge(h_stored, stored(i))
                for h, half, _ in HALF_BATCHES:
                    dve.wait_ge(scaled, done(i, 2, h))
                    nc.vector.tensor_tensor(c.H[:, half, :], c.Y[:, half, :], c.MROW[:, 1, half, SHIFT_A, :],
                                            ALU.add).then_inc(h_done, 1)

            def norm(i):
                dve.wait_ge(h_done, done(i, 2, 1))
                ln_stats(nc, dve, c, lh, lambda b: c.H[:, b, :], i)
                dve.wait_ge(turned, before(i, 2))
                ln_apply(nc, dve, c, lh, lambda b: c.H[:, b, :], lambda b: c.O[:, b, :], i)

            def rest(i):
                dve.wait_ge(qk_out, done(i))
                nc.vector.tensor_tensor(c.QKF[:, :, :], c.QKF[:, :, :], c.PARTS[:, 0:8, :], ALU.subtract
                                        ).then_inc(rest1, 1)

            def products(i, batches):
                for b in batches:
                    dve.wait_ge(tok_mm, done(i, B, b))
                    dve.wait_ge(qv_out, done(i, B, b))
                    q = c.QV[:, b, 0:D].unsqueeze(1)
                    nc.vector.tensor_tensor(c.FP[:, b, :, :], c.PS[:, BANKS[b % 2][1], :].rearrange(
                        "p (f n) -> p f n", f=NF), bcast(q, [P, NF, D]), ALU.mult).then_inc(prod_done, 1)

            def logits(i):
                dve.wait_ge(prod_done, done(i, B, B - 1))
                fi = at(F4, i)
                for b in range(B):
                    last = nc.vector.tensor_reduce(fi[:, b, :], c.FP[:, b, :, :].rearrange(
                        "p f (h d) -> p (f h) d", d=HS), X_AXIS, ALU.add)
                last.then_inc(logit_done, 1)
                dve.wait_ge(logit_done, done(i))
                mi = at(M4, i)
                for b in range(B):
                    last = nc.vector.tensor_reduce(mi[:, b, :], fi[:, b, :].rearrange("p (f h) -> p h f", f=NF),
                                                   X_AXIS, ALU.max)
                last.then_inc(fmax_done, 1)

            front(0)
            norm(0)
            dve.wait_ge(loaded, 16 * len(loads))
            dve.wait_ge(mask_done, 3)
            for f in range(NF):
                last = nc.vector.tensor_tensor(
                    c.BD[:, f, :].rearrange("p (h c) -> p h c", c=HS),
                    bcast(c.CV[:, f, :].unsqueeze(1), [P, H1, HS]),
                    c.BLOCKS[:, :].rearrange("p (h c) -> p h c", c=HS), ALU.mult)
            last.then_inc(bd_done, 1)
            dve.wait_ge(g_mm, 1)
            nc.vector.tensor_copy(c.GK[:, :, :], c.PS[:, 0:2, :].rearrange("p k (f n) -> p (k f) n", n=256)
                                  ).then_inc(g_out, 1)
            dve.wait_ge(big_mm, 1)
            nc.vector.tensor_copy(c.BIG[:, :, :], c.PS[:, 2:4, :].rearrange("p k (f n) -> p (k f) n", n=256)
                                  ).then_inc(big_out, 1)
            with dve.Fori(0, NC - 1) as i:
                front(i + 1)
                rest(i)
                products(i, (0, 1))
                norm(i + 1)
                products(i, (2, 3))
                logits(i)
            rest(NC - 1)
            products(NC - 1, range(B))
            logits(NC - 1)

        @block.gpsimd
        def _(pool):
            credit(pool, lx.pool() + lh.pool() + [part3, v_kept])
            nc.gpsimd.memset(c.BLOCKS[:, :], 1.0).then_inc(mask_done, 1)
            blocks = c.BLOCKS[:, :].rearrange("p (h c) -> p h c", c=HS)
            for n, (base, step, mult) in enumerate(((0, -HS, 1), (HS - 1, HS, -1))):
                pool.wait_ge(mask_done, n + 1)
                nc.gpsimd.affine_select(out=blocks, in_=blocks, compare_op=ALU.is_ge, fill=0.0, base=base,
                                        pattern=[[step, H1], [0, HS]], channel_multiplier=mult
                                        ).then_inc(mask_done, 1)

            def third_part(i):
                pool.wait_ge(part2, done(i))
                pool.wait_ge(part_stored[2], stored(i))
                nc.gpsimd.tensor_tensor(c.PARTS[:, 16:24, :], c.QKF[:, :, :], c.PARTS[:, 8:16, :], ALU.subtract
                                        ).then_inc(part3, 1)
                pool.wait_ge(qv_out, done(i, B, B - 1))
                pool.sem_inc(c.passed, 1)
                nc.gpsimd.tensor_copy(at(V4, i), c.QV[:, :, D:2 * D]).then_inc(v_kept, 1)

            ln_rstd(nc, pool, c, lx, 0)
            ln_rstd(nc, pool, c, lh, 0)
            with pool.Fori(0, NC - 1) as i:
                ln_rstd(nc, pool, c, lx, i + 1)
                ln_rstd(nc, pool, c, lh, i + 1)
                third_part(i)
            third_part(NC - 1)

        @block.scalar
        def _(act):
            credit(act, [z_ready, qk_out, qv_out, vf_out, part2])
            act.wait_ge(loaded, 16 * len(loads))
            with act.Fori(0, NC) as i:
                for h, half, _ in HALF_BATCHES:
                    act.wait_ge(turned, done(i, 2, h))
                    nc.scalar.activation(ZT[:, h * 256:h * 256 + 256], c.PS[:, h, 0:256], ACT.Identity,
                                         scale=c.LNG[:, 0:1], bias=c.LNG[:, 1:2]).then_inc(z_ready, 1)
                act.wait_ge(qk_mm, done(i))
                act.wait_ge(part_stored[0], stored(i))
                act.wait_ge(part3, before(i))
                for n, scale in enumerate((HS ** -0.5, 1.0)):
                    flat = c.QKF[:, 4 * n:4 * n + 4, :].rearrange("p b t -> p (b t)")
                    part = c.PARTS[:, 4 * n:4 * n + 4, :].rearrange("p b t -> p (b t)")
                    nc.scalar.mul(flat, c.PS[:, 1 + n, :], scale)
                    last = nc.scalar.mul(part, c.PS[:, 1 + n, :], scale)
                last.then_inc(qk_out, 1)
                act.wait_ge(vf_stored, stored(i))
                act.wait_ge(v_kept, before(i))
                for b in range(B):
                    act.wait_ge(tok_mm, done(i, B, b))
                    bank = BANKS[b % 2]
                    nc.scalar.copy(c.QV[:, b, :], c.PS[:, bank[0], 0:2 * D]).then_inc(qv_out, 1)
                    nc.scalar.copy(c.VF[:, b, :], c.PS[:, bank[2], :]).then_inc(vf_out, 1)
                    if b == 1:
                        act.wait_ge(rest1, done(i))
                        act.wait_ge(part_stored[1], stored(i))
                        nc.scalar.copy(c.PARTS[:, 8:16, :], c.QKF[:, :, :]).then_inc(part2, 1)

        @block.tensor
        def _(pe):
            credit(pe, [turned, qk_mm, tok_mm])
            pe.wait_ge(bd_done, 1)
            for f in range(NF):
                last = nc.tensor.matmul(c.PS[:, f // 2, 256 * (f % 2):256 * (f % 2) + 256], c.BD[:, f, :],
                                        c.WT[:, D:3 * D], start=True, stop=True)
            last.then_inc(g_mm, 1)
            pe.wait_ge(g_out, 1)
            for f in range(NF):
                last = nc.tensor.matmul(c.PS[:, 2 + f // 2, 256 * (f % 2):256 * (f % 2) + 256], c.WF[:, :],
                                        c.GK[:, f, :], start=True, stop=True)
            last.then_inc(big_mm, 1)
            pe.wait_ge(big_out, 1)
            with pe.Fori(0, NC) as i:
                pe.wait_ge(vf_out, before(i, B, 0))
                pe.wait_ge(qk_out, before(i))
                for h, _, batches in HALF_BATCHES:
                    pe.wait_ge(lh.normed, done(i, 2, h))
                    turn_half(nc, c, h, 0, c.O, batches).then_inc(turned, 1)
                pe.wait_ge(z_ready, done(i, 2, 1))
                for n in range(2):
                    last = nc.tensor.matmul(c.PS[:, 1 + n, :], c.WT[:, n * D:(n + 1) * D], ZT, start=True, stop=True)
                last.then_inc(qk_mm, 1)
                for b in range(B):
                    bank = BANKS[b % 2]
                    if b >= 2:
                        pe.wait_ge(vf_out, done(i, B, b - 2))
                        pe.wait_ge(prod_done, done(i, B, b - 2))
                    else:
                        pe.wait_ge(prod_done, before(i, B, 0))
                    zb = c.HT[:, b, :]
                    nc.tensor.matmul(c.PS[:, bank[0], 0:D], zb, c.WT[:, 0:D], start=True, stop=True)
                    nc.tensor.matmul(c.PS[:, bank[0], D:2 * D], zb, c.WT[:, 2 * D:3 * D], start=True, stop=True)
                    nc.tensor.matmul(c.PS[:, bank[1], :], zb, c.BIG[:, :, 0:D], start=True, stop=True)
                    nc.tensor.matmul(c.PS[:, bank[2], :], zb, c.BIG[:, :, D:2 * D], start=True, stop=True
                                     ).then_inc(tok_mm, 1)


HALVES, HB = 2, 4
UNITS = [(half, s) for half in range(HALVES) for s in range(HB * (half + 1))]
MAX_UNITS = [(t, half, h) for t in range(NC) for half in range(t // HB + 1) for h in range(GH)]


def attention(nc, m, c, scratch):
    NU, NM = len(UNITS), len(MAX_UNITS)
    set_dve, set_act, set_pool, v_laid = (m.sem("at_" + n) for n in ("set_dve", "set_act", "set_pool", "v_laid"))
    qk_loaded = [m.sem(f"at_qk_loaded{g}") for g in range(NG)]
    max_mm, max_taken, top_done, shift_done = (m.sem("at_" + n) for n in ("max_mm", "max_taken", "top", "shift"))
    shift_t, neg_done, n1, r1, n2, r2 = (m.sem("at_" + n) for n in ("shift_t", "neg", "n1", "r1", "n2", "r2"))
    shift_rows = m.sem("at_shift_rows")
    score_mm, exp_done, masked, value_mm = (m.sem("at_" + n) for n in ("score_mm", "exp", "masked", "value_mm"))
    of_out, of_t, nd_out = m.sem("at_of_out"), m.sem("at_of_t"), m.sem("at_nd_out")
    C4 = lambda t, b: t[:, bass.ds(b * NC, NC), :]
    LOADS = 2 * NT
    PER_UNIT, LEAD = NM // NU, 14
    ORDER = ("first scores", "maximum", "second scores", "maximum", "values", "maximum", "maximum")
    serial = lambda b, g, u, p=0: ((b * NG + g) * NU + u) * 2 + p
    scored = lambda n: n + 1 + NG * NU * 2
    exped = lambda n: n + 3
    valued = lambda b, g, u: (b * NG + g) * NU + u + 1 + 2 * NU

    def width(half, s):
        first = max(s - HB * half, 0)
        return (HB - first) * P, (HB * half + first) * P

    with nc.Block() as block:

        @block.sync
        def _(sp):
            def load(b, g):
                sp.wait_ge(score_mm, (b * NG + g + 1) * (2 * NU))
                for tile, qk, rows in ((c.QS, 0, ROW_Q), (c.KS, 1, ROW_K)):
                    for r, part in enumerate(rows):
                        src = scratch.qk[GH * g * HS:GH * (g + 1) * HS,
                                         bass.ds(b + (part * 2 + qk) * B, 1), :].rearrange(
                            "(h d) o t -> d h (o t)", d=HS)
                        sp.dma_start(tile[r * HS:(r + 1) * HS, g, :, :], src).then_inc(qk_loaded[g], 16)

            def shift(b, g):
                sp.wait_ge(r2, done(b, NG, g))
                for n in range(NS):
                    dst = c.QS[KM + n:KM + n + 1, g, :, :].rearrange("o h t -> o (h t)")
                    sp.dma_start(dst, c.NEGM[:, g % 2, n, :]).then_inc(shift_rows, 16)

            def batch(b, last):
                shift(b, 0)
                load(b, NG - 1)
                for g in range(1, NG):
                    shift(b, g)
                    if not last:
                        load(b + 1, g - 1)

            for g in range(NG - 1):
                sp.wait_ge(set_dve, 1)
                sp.wait_ge(set_act, 2 * g + 1)
                sp.wait_ge(set_pool, g + 1)
                load(0, g)
            sp.wait_ge(set_act, 2 * NG - 1)
            sp.wait_ge(set_pool, NG)
            with sp.Fori(0, B - 1) as b:
                batch(b, False)
            batch(B - 1, True)
            sp.wait_ge(shift_rows, 16 * NS * B * NG)

        @block.vector
        def _(dve):
            nc.vector.memset(c.QS[:, 0, :, :], 0.0).then_inc(set_dve, 1)
            nc.vector.memset(c.MP[:, :, :, :], -1e30).then_inc(max_taken, 2)
            credit(dve, [top_done, shift_done, neg_done, n1, r1, n2, r2])

            def reduce(b, g, units):
                for u in units:
                    t, half, h = MAX_UNITS[u]
                    w = min(512, (t + 1) * P - 512 * half)
                    dve.wait_ge(max_mm, (b * NG + g) * NM + u + 1)
                    nc.vector.reduce_max(c.MP[:, t, half, h:h + 1], c.PS[:, 4 + u % 2, 0:w], X_AXIS
                                         ).then_inc(max_taken, 1)

            def group(b, g, last_one):
                reduce(b, g, range(2, NM))
                dve.wait_ge(max_taken, (b * NG + g + 1) * NM + 2)
                nc.vector.tensor_tensor(c.MX[:, :, :], c.MP[:, :, 0, :], c.MP[:, :, 1, :], ALU.max
                                        ).then_inc(top_done, 1)
                dve.wait_ge(top_done, done(b, NG, g))
                for dst in (C4(c.SHIFT, b)[:, :, GH * g:GH * g + GH], c.MG[:, :, :].rearrange("p h n -> p n h")):
                    last = nc.vector.tensor_tensor(dst, c.MX[:, :, :], C4(c.FMAX, b)[:, :, GH * g:GH * g + GH],
                                                   ALU.max)
                last.then_inc(shift_done, 1)
                dve.wait_ge(shift_t, done(b, NG, g))
                nc.vector.tensor_scalar(c.SH[:, 0, :], c.PS[0:NC * GH, 7, 0:P], -1.0, None, ALU.mult
                                        ).then_inc(neg_done, 1)
                if not last_one:
                    reduce(b, g + 1, range(2))
                dve.wait_ge(neg_done, done(b, NG, g))
                parts = c.NEGM[:, g % 2, :, :]
                nc.vector.tensor_copy(parts[:, 0, :], c.SH[:, 0, :]).then_inc(n1, 1)
                dve.wait_ge(n1, done(b, NG, g))
                nc.vector.tensor_tensor(c.SH[:, 1, :], c.SH[:, 0, :], parts[:, 0, :], ALU.subtract).then_inc(r1, 1)
                dve.wait_ge(r1, done(b, NG, g))
                nc.vector.tensor_copy(parts[:, 1, :], c.SH[:, 1, :]).then_inc(n2, 1)
                dve.wait_ge(n2, done(b, NG, g))
                nc.vector.tensor_tensor(parts[:, 2, :], c.SH[:, 1, :], parts[:, 1, :], ALU.subtract).then_inc(r2, 1)

            reduce(0, 0, range(2))
            with dve.Fori(0, B - 1) as b:
                for g in range(NG):
                    group(b, g, False)
            for g in range(NG):
                group(B - 1, g, g == NG - 1)

        @block.gpsimd
        def _(pool):
            for g in range(NG):
                nc.gpsimd.memset(c.KS[0:KM, g, :, :], 0.0).then_inc(set_pool, 1)
            nc.gpsimd.memset(c.VG[:, :, :, :, :], 0.0).then_inc(set_pool, 1)
            pool.wait_ge(set_pool, NG + 1)
            nc.gpsimd.memset(c.VG[:, :, :, :, HS:HS + 1], 1.0)
            credit(pool, [v_laid, masked])
            with pool.Fori(0, B) as b:
                for g in range(NG):
                    pool.wait_ge(value_mm, (b * NG + g + 1) * NU)
                    v = C4(c.VT, b)[:, :, GH * HS * g:GH * HS * (g + 1)].rearrange("p n (h d) -> p n h d", d=HS)
                    pool.sem_inc(c.passed, 1)
                    for h in range(GH):
                        last = nc.gpsimd.tensor_copy(c.VG[:, g % 2, :, h, 0:HS], v[:, :, h, :])
                    last.then_inc(v_laid, 1)
                    for u, (half, s) in enumerate(UNITS):
                        if s < HB * half:
                            continue
                        for p in range(2):
                            pool.wait_ge(exp_done, exped(serial(b, g, u, p)))
                            pool.sem_inc(c.passed, 1)
                            diagonal = c.PT[:, u % 2, p, :, 0:P]
                            nc.gpsimd.affine_select(out=diagonal, in_=diagonal, compare_op=ALU.is_ge, fill=0.0,
                                                    base=0, pattern=[[0, 2], [1, P]], channel_multiplier=-1
                                                    ).then_inc(masked, 1)

        @block.scalar
        def _(act):
            for g in range(NG):
                if g:
                    nc.scalar.copy(c.QS[:, g, :, :], bcast(c.ZERO[:, 0:1].unsqueeze(2), [P, GH, T])
                                   ).then_inc(set_act, 1)
                nc.scalar.copy(c.KS[KM:P, g, :, :], bcast(c.ONES[KM:P, 0:1].unsqueeze(2), [P - KM, GH, T])
                               ).then_inc(set_act, 1)
            credit(act, [exp_done, exp_done, of_out, nd_out])

            def sums_out(b, g, half):
                n = (b * NG + g) * 2 + half
                act.wait_ge(value_mm, valued(b, g, (3, 11)[half]))
                act.wait_ge(of_t, n + 1)
                nc.scalar.copy(c.OF[:, :], c.PS[:, 6, :]).then_inc(of_out, 1)

            def sums_kept(b, g, half):
                act.wait_ge(of_t, (b * NG + g) * 2 + half + 2)
                nd = c.ND[:, bass.ds(b * NC + HB * half, HB), GH * g:GH * g + GH, :]
                src = c.PS[:, 7, :].rearrange("p (n h r) -> p n h r", n=HB, h=GH)
                for h in range(GH):
                    last = nc.scalar.copy(nd[:, :, h, :], src[:, :, h, 0:HS + 1])
                last.then_inc(nd_out, 1)

            with act.Fori(0, B) as b:
                for g in range(NG):
                    for u, (half, s) in enumerate(UNITS):
                        w, _ = width(half, s)
                        for p in range(2):
                            act.wait_ge(score_mm, scored(serial(b, g, u, p)))
                            act.wait_ge(value_mm, valued(b, g, u - 2))
                            nc.scalar.activation(c.PT[:, u % 2, p, :, 0:w], c.PS[:, 2 * p:2 * p + 2, 0:w],
                                                 ACT.Exp).then_inc(exp_done, 1)
                        if u == 4:
                            sums_out(b, g, 0)
                        if u == 6:
                            sums_kept(b, g, 0)
                    sums_out(b, g, 1)
                    sums_kept(b, g, 1)

        @block.tensor
        def _(pe):
            credit(pe, [shift_t, of_t])
            pe.sem_inc(score_mm, NG * NU * 2)
            pe.sem_inc(value_mm, 2 * NU)

            def maxima(b, g, units):
                slot = g % NG
                for u in units:
                    t, half, h = MAX_UNITS[u]
                    w = min(512, (t + 1) * P - 512 * half)
                    if u == 0:
                        pe.wait_ge(qk_loaded[slot], (b + g // NG) * (16 * LOADS) + 16 * LOADS)
                    pe.wait_ge(max_taken, (b * NG + g) * NM + u + 1)
                    diagonal = half == t // HB
                    last = nc.tensor.matmul(c.PS[:, 4 + u % 2, 0:w], c.QS[0:KM, slot, h, t * P:(t + 1) * P],
                                            c.KS[0:KM, slot, h, 512 * half:512 * half + w],
                                            start=True, stop=not diagonal)
                    if diagonal:
                        last = nc.tensor.matmul(c.PS[:, 4 + u % 2, w - P:w], c.IDENTB[:, :], c.LATER[:, :],
                                                start=False, stop=True)
                    last.then_inc(max_mm, 1)

            def turn_shift(b, g):
                pe.wait_ge(shift_done, done(b, NG, g))
                pe.wait_ge(nd_out, (b * NG + g) * 2)
                nc.tensor.transpose(c.PS[0:NC * GH, 7, 0:P], c.MG[:, :, :].rearrange("p h n -> p (h n)"),
                                    c.IDENT[:, :]).then_inc(shift_t, 1)

            def values(b, g, u):
                half, s = UNITS[u]
                w, first = width(half, s)
                gn = b * NG + g
                pe.wait_ge(exp_done, exped(serial(b, g, u, 1)))
                if s >= HB * half:
                    seen = sum(1 for q in UNITS[:u + 1] if q[1] >= HB * q[0])
                    pe.wait_ge(masked, gn * (2 * NC) + (2 * seen + 1))
                if u == 0:
                    pe.wait_ge(v_laid, done(b, NG, g))
                if s == 0:
                    pe.wait_ge(of_out, gn * 2 + (half + 1))
                o = first - 512 * half
                for h in range(GH):
                    last = nc.tensor.matmul(c.PS[32 * h:32 * h + 32, 6, o:o + w], c.VG[:, g % 2, s, h, :],
                                            c.PT[:, u % 2, h // 2, h % 2, 0:w],
                                            start=(s == 0), stop=(s == HB * (half + 1) - 1))
                last.then_inc(value_mm, 1)

            def turn_sums(b, g, half, shifted):
                gn = b * NG + g
                pe.wait_ge(of_out, gn * 2 + (half + 2))
                pe.wait_ge(neg_done, done(b, NG, shifted))
                pe.wait_ge(nd_out, gn * 2 + (half + 1))
                for n in range(HB):
                    last = nc.tensor.transpose(c.PS[:, 7, n * P:(n + 1) * P], c.OF[:, n * P:(n + 1) * P],
                                               c.IDENT[:, :])
                last.then_inc(of_t, 1)

            def batch(b, last):
                for g in range(NG):

                    def scores(u, p):
                        half, s = UNITS[u]
                        w, first = width(half, s)
                        pe.wait_ge(exp_done, exped(serial(b, g, u - 1, p)))
                        for k in range(2):
                            h = 2 * p + k
                            mm = nc.tensor.matmul(c.PS[:, h, 0:w], c.KS[0:KA, g, h, s * P:(s + 1) * P],
                                                  c.QS[0:KA, g, h, first:first + w], start=True, stop=True)
                        mm.then_inc(score_mm, 1)

                    pe.wait_ge(shift_rows, (b * NG + g + 1) * (16 * NS))
                    for u in range(NU):
                        taken = LEAD + u * PER_UNIT
                        for step in ORDER:
                            if step == "first scores":
                                scores(u, 0)
                            elif step == "second scores":
                                scores(u, 1)
                            elif step == "values" and u:
                                values(b, g, u - 1)
                            elif step == "maximum":
                                n, taken = taken, taken + 1
                                if n == NM + 2 and (g + 1 < NG or not last):
                                    turn_shift(b, g + 1)
                                if g + 1 + n // NM < NG or not last:
                                    maxima(b, g + 1 + n // NM, [n % NM])
                        if u == 5:
                            turn_sums(b, g, 0, g)
                    values(b, g, NU - 1)
                    turn_sums(b, g, 1, g + 1 if g + 1 < NG or not last else g)

            maxima(0, 0, range(NM))
            maxima(0, 1, range(2))
            pe.wait_ge(shift_done, done(0))
            nc.tensor.transpose(c.PS[0:NC * GH, 7, 0:P], c.MG[:, :, :].rearrange("p h n -> p (h n)"),
                                c.IDENT[:, :]).then_inc(shift_t, 1)
            maxima(0, 1, range(2, LEAD))
            with pe.Fori(0, B - 1) as b:
                batch(b, False)
            batch(B - 1, True)


F1 = 4 * D
NB1 = F1 // P


def attention_output(nc, m, c, dram, scratch):
    ln = LnSems(m, "ao")
    loaded, vf_loaded, hin_loaded = m.sem("ao_loaded"), m.sem("ao_vf_loaded"), m.sem("ao_h_loaded")
    less, exp_done, prod_done, num_done, den_done, rec_done, o_done, both_done = (
        m.sem("ao_" + n) for n in ("less", "exp", "prod", "num", "den", "rec", "o", "both"))
    o_t, o_out, proj_mm, x1_done, turned, z_ready = (
        m.sem("ao_" + n) for n in ("o_t", "o_out", "proj", "x1", "turned", "z"))
    prod_pool = m.sem("ao_prod_pool")
    up_mm, gelu_done, down_mm, y_done, gated, res_done = (
        m.sem("ao_" + n) for n in ("up", "gelu", "down", "y", "gated", "res"))
    X4 = c.X[:, :, :].rearrange("p (b n) d -> p b n d", b=B)
    F4 = c.FUT[:, :, :].rearrange("p (b n) d -> p b n d", b=B)
    M4 = c.SHIFT[:, :, :].rearrange("p (b n) d -> p b n d", b=B)
    N4 = c.ND[:, :, :, :].rearrange("p (b n) h r -> p b n (h r)", b=B)
    two = lambda bank, o: c.PS[:, bank, o:o + 2 * P].rearrange("p (b n) -> p b n", b=2)
    ZT = c.HT[:, :, :].rearrange("p b t -> p (b t)")
    loads = [(c.WP[:, :], dram["L1_attn_W_proj_T"]), (c.W1[:, :], dram["L1_attn_W_ff1"]),
             (c.W2[:, :, :], dram["L1_attn_W_ff2"].rearrange("(k p) d -> p k d", p=P))]

    def weigh(engine, b):
        return engine.tensor_tensor(
            c.FP[:, b, :, :].rearrange("p f (h d) -> p (f h) d", d=HS),
            c.VF[:, b, :].rearrange("p (n d) -> p n d", d=HS),
            bcast(c.PF[:, b, :].unsqueeze(2), [P, NF * H1, HS]), ALU.mult)

    with nc.Block() as block:

        @block.sync
        def _(sp):
            with sp.Fori(0, NC) as i:
                sp.wait_ge(prod_done, before(i))
                sp.wait_ge(prod_pool, before(i))
                sp.dma_start(c.VF[:, :, :], scratch.vf[:, bass.ds(i, 1), :, :].rearrange("b o p n -> p b (o n)")
                             ).then_inc(vf_loaded, 16)
                sp.wait_ge(x1_done, before(i, 2))
                sp.dma_start(c.H[:, :, :], scratch.h[:, bass.ds(i, 1), :, :].rearrange("b o p d -> p b (o d)")
                             ).then_inc(hin_loaded, 16)

        @block.vector
        def _(dve):
            credit(dve, ln.dve() + [less, prod_done, num_done, den_done, both_done, rec_done, o_done, x1_done,
                                    y_done])

            def shift(i):
                fi, mi = at(F4, i), at(M4, i)
                for b in range(B):
                    last = nc.vector.tensor_tensor(
                        c.PF[:, b, :].rearrange("p (f h) -> p f h", f=NF), fi[:, b, :].rearrange("p (f h) -> p f h", f=NF),
                        bcast(mi[:, b, :].unsqueeze(1), [P, NF, H1]), ALU.subtract)
                last.then_inc(less, 1)

            def front(i):
                ni = at(N4, i)
                dve.wait_ge(exp_done, done(i))
                dve.wait_ge(vf_loaded, i * 16 + 16)
                for b in range(B - 1):
                    last = weigh(nc.vector, b)
                last.then_inc(prod_done, 1)
                dve.wait_ge(prod_done, done(i))
                dve.wait_ge(prod_pool, done(i))
                for b in range(B):
                    nc.vector.tensor_reduce(c.O[:, b, :], c.FP[:, b, :, :].rearrange("p f n -> p n f"), X_AXIS, ALU.add)
                    last = nc.vector.tensor_reduce(c.DEN[:, b, :], c.PF[:, b, :].rearrange("p (f h) -> p h f", f=NF),
                                                   X_AXIS, ALU.add)
                last.then_inc(num_done, 1)
                dve.wait_ge(num_done, done(i))
                n9 = ni.rearrange("p b (h r) -> p b h r", r=HS + 1)
                for b in range(B):
                    nc.vector.tensor_tensor(c.DEN[:, b, :], c.DEN[:, b, :], n9[:, b, :, HS], ALU.add)
                    last = nc.vector.tensor_tensor(c.O[:, b, :].rearrange("p (h d) -> p h d", d=HS),
                                                   c.O[:, b, :].rearrange("p (h d) -> p h d", d=HS),
                                                   n9[:, b, :, 0:HS], ALU.add)
                last.then_inc(both_done, 1)
                dve.wait_ge(both_done, done(i))
                nc.vector.reciprocal(c.DEN[:, :, :], c.DEN[:, :, :]).then_inc(rec_done, 1)
                dve.wait_ge(rec_done, done(i))
                nc.vector.tensor_tensor(c.O[:, :, :].rearrange("p b (h d) -> p (b h) d", d=HS),
                                        c.O[:, :, :].rearrange("p b (h d) -> p (b h) d", d=HS),
                                        bcast(c.DEN[:, :, :].rearrange("p b h -> p (b h)").unsqueeze(2),
                                              [P, B * H1, HS]), ALU.mult).then_inc(o_done, 1)

            def middle(i):
                dve.wait_ge(hin_loaded, i * 16 + 16)
                for h, half, _ in HALF_BATCHES:
                    dve.wait_ge(proj_mm, done(i, 2, h))
                    nc.vector.tensor_tensor(c.X1[:, half, :], two(2 + h, 0), c.H[:, half, :], ALU.add
                                            ).then_inc(x1_done, 1)
                dve.wait_ge(x1_done, done(i, 2, 1))
                ln_stats(nc, dve, c, ln, lambda b: c.X1[:, b, :], i)
                ln_apply(nc, dve, c, ln, lambda b: c.X1[:, b, :], lambda b: c.XN[:, b, :], i)

            def back(i):
                dve.wait_ge(res_done, before(i, 2))
                for h, half, _ in HALF_BATCHES:
                    dve.wait_ge(down_mm, done(i, 2, h))
                    nc.vector.tensor_tensor(c.Y[:, half, :], two(2 + h, 256), c.X1[:, half, :], ALU.add
                                            ).then_inc(y_done, 1)

            shift(0)
            front(0)
            with dve.Fori(0, NC - 1) as i:
                shift(i + 1)
                middle(i)
                front(i + 1)
                back(i)
            middle(NC - 1)
            back(NC - 1)

        @block.gpsimd
        def _(pool):
            credit(pool, ln.pool() + [prod_pool, gated, res_done])

            def front(i):
                pool.wait_ge(exp_done, done(i))
                pool.wait_ge(vf_loaded, i * 16 + 16)
                weigh(nc.gpsimd, B - 1).then_inc(prod_pool, 1)

            def back(i):
                xi = at(X4, i)
                for h, half, _ in HALF_BATCHES:
                    pool.wait_ge(y_done, done(i, 2, h))
                    nc.gpsimd.tensor_tensor(c.Y[:, half, :], c.Y[:, half, :], c.MROW[:, 1, half, GATE_A, :], ALU.mult
                                            ).then_inc(gated, 1)
                for h, half, _ in HALF_BATCHES:
                    pool.wait_ge(gated, done(i, 2, h))
                    nc.gpsimd.tensor_tensor(xi[:, half, :], xi[:, half, :], c.Y[:, half, :], ALU.add
                                            ).then_inc(res_done, 1)

            front(0)
            with pool.Fori(0, NC - 1) as i:
                ln_rstd(nc, pool, c, ln, i)
                front(i + 1)
                back(i)
            ln_rstd(nc, pool, c, ln, NC - 1)
            back(NC - 1)

        @block.scalar
        def _(act):
            for dst, src in loads:
                act.dma_start(dst, src).then_inc(loaded, 16)
            credit(act, [exp_done, o_out, z_ready, gelu_done])

            def front(i):
                act.wait_ge(less, done(i))
                nc.scalar.activation(c.PF[:, :, :], c.PF[:, :, :], ACT.Exp).then_inc(exp_done, 1)

            def output(i):
                for h, half, _ in HALF_BATCHES:
                    act.wait_ge(o_t, done(i, 2, h))
                    nc.scalar.copy(c.OT[:, half, :], two(h, 0)).then_inc(o_out, 1)

            def middle(i):
                for h, half, _ in HALF_BATCHES:
                    act.wait_ge(turned, done(i, 2, h))
                    nc.scalar.activation(ZT[:, h * 256:h * 256 + 256], c.PS[:, h, 256:512], ACT.Identity,
                                         scale=c.LNG[:, 2:3], bias=c.LNG[:, 3:4]).then_inc(z_ready, 1)

            def back(i):
                for h, _, _ in HALF_BATCHES:
                    act.wait_ge(up_mm, done(i, 2, h))
                    nc.scalar.activation(c.GE[:, h, :, :], c.PS[:, 4 + 2 * h:6 + 2 * h, :].rearrange(
                        "p k (a n) -> p (k a) n", a=2), ACT.Gelu).then_inc(gelu_done, 1)

            front(0)
            with act.Fori(0, NC - 1) as i:
                output(i)
                front(i + 1)
                middle(i)
                back(i)
            output(NC - 1)
            middle(NC - 1)
            back(NC - 1)

        @block.tensor
        def _(pe):
            credit(pe, [o_t, proj_mm, turned, up_mm, down_mm])
            pe.wait_ge(loaded, 16 * len(loads))
            with pe.Fori(0, NC) as i:
                pe.wait_ge(o_done, done(i))
                for h, _, batches in HALF_BATCHES:
                    turn_half(nc, c, h, 0, c.O, batches).then_inc(o_t, 1)
                pe.wait_ge(y_done, before(i, 2))
                for h, _, batches in HALF_BATCHES:
                    pe.wait_ge(o_out, done(i, 2, h))
                    for n, b in enumerate(batches):
                        last = nc.tensor.matmul(c.PS[:, 2 + h, n * P:(n + 1) * P], c.OT[:, b, :], c.WP[:, :],
                                                start=True, stop=True)
                    last.then_inc(proj_mm, 1)
                for h, _, batches in HALF_BATCHES:
                    pe.wait_ge(ln.normed, done(i, 2, h))
                    turn_half(nc, c, h, 256, c.XN, batches).then_inc(turned, 1)
                for h, half, batches in HALF_BATCHES:
                    pe.wait_ge(z_ready, done(i, 2, h))
                    for k in range(NB1):
                        last = nc.tensor.matmul(c.PS[:, 4 + 2 * h + k // 2, 256 * (k % 2):256 * (k % 2) + 256],
                                                c.W1[:, k * P:(k + 1) * P], ZT[:, h * 256:h * 256 + 256],
                                                start=True, stop=True)
                    last.then_inc(up_mm, 1)
                for h, _, batches in HALF_BATCHES:
                    pe.wait_ge(gelu_done, done(i, 2, h))
                    for n in range(2):
                        for k in range(NB1):
                            last = nc.tensor.matmul(c.PS[:, 2 + h, 256 + n * P:256 + (n + 1) * P],
                                                    c.GE[:, h, k, n * P:(n + 1) * P], c.W2[:, k, :],
                                                    start=(k == 0), stop=(k == NB1 - 1))
                    last.then_inc(down_mm, 1)


E1 = 64
PAIRS = B * T // 8 // 2
SB, BP = 128, 8
NSB, NBP = PAIRS // SB, SB // BP
GR = NSB * 2


def experts_input(nc, m, c, scratch):
    ln = LnSems(m, "ki")
    turned, h_ready, x_stored, h_stored = (m.sem("ki_" + n) for n in ("turned", "h", "x_stored", "h_stored"))
    X4 = c.X[:, :, :].rearrange("p (b n) d -> p b n d", b=B)
    H4 = c.HTA[:, :].rearrange("p (b n t) -> p b n t", b=B, n=NC)
    with nc.Block() as block:

        @block.sync
        def _(sp):
            sp.dma_start(scratch.x, c.X[:, :, :]).then_inc(x_stored, 16)
            HT4 = scratch.ht.rearrange("p (b n t) -> p b n t", b=B, n=NC)
            with sp.Fori(0, NC) as i:
                sp.wait_ge(h_ready, done(i))
                sp.dma_start(at(HT4, i), at(H4, i)).then_inc(h_stored, 16)
            sp.wait_ge(x_stored, 16)
            sp.wait_ge(h_stored, 16 * NC)

        @block.vector
        def _(dve):
            credit(dve, ln.dve())
            with dve.Fori(0, NC) as i:
                xi = at(X4, i)
                ln_stats(nc, dve, c, ln, lambda b: xi[:, b, :], i)
                dve.wait_ge(turned, before(i))
                ln_apply(nc, dve, c, ln, lambda b: xi[:, b, :], lambda b: c.XN[:, b, :], i)

        @block.gpsimd
        def _(pool):
            credit(pool, ln.pool())
            with pool.Fori(0, NC) as i:
                ln_rstd(nc, pool, c, ln, i)

        @block.scalar
        def _(act):
            credit(act, [h_ready])
            with act.Fori(0, NC) as i:
                act.wait_ge(turned, done(i))
                hi = at(H4, i)
                for b in range(B):
                    last = nc.scalar.activation(hi[:, b, :], c.PS[:, 0, b * P:(b + 1) * P], ACT.Identity,
                                                scale=c.MCOL[:, 1, SCALE_B, b:b + 1],
                                                bias=c.MCOL[:, 1, SHIFT_B, b:b + 1])
                last.then_inc(h_ready, 1)

        @block.tensor
        def _(pe):
            credit(pe, [turned])
            with pe.Fori(0, NC) as i:
                pe.wait_ge(ln.normed, done(i, 2, 1))
                pe.wait_ge(h_ready, before(i))
                for b in range(B):
                    last = nc.tensor.transpose(c.PS[:, 0, b * P:(b + 1) * P], c.XN[:, b, :], c.IDENT[:, :])
                last.then_inc(turned, 1)


def table_loads(c, dram, layer):
    flat = lambda name: dram[name].rearrange("e o i -> e (o i)")
    return [(table_rows(c, n)[E1 * twin:E1 * twin + E1, :], flat(f"L1_ffn_{n}_{layer}"))
            for n in "AB" for twin in range(2)]


def table_rows(c, name):
    k = 16 * "AB".index(name)
    return c.BG[:, k:k + 16, :].rearrange("p k n -> p (k n)")


class Split:

    def __init__(self, nc, m, c, tag, loads):
        self.nc, self.loads = nc, loads
        self.loaded, self.first, self.rest, self.low = (
            m.sem(tag + "_" + n) for n in ("tables_loaded", "first_part", "rest", "low"))
        self.tables = [(table_rows(c, "A"), c.TWO[:, 0, :], c.LOW[:, 0, :]),
                       (table_rows(c, "B"), c.TWO[:, 1, :], c.LOW[:, 1, :])]

    def load(self, sp):
        for dst, src in self.loads:
            sp.dma_start(dst, src).then_inc(self.loaded, 16)

    def round_off(self, act):
        act.wait_ge(self.loaded, 16 * len(self.loads))
        for rows, two, low in self.tables:
            self.nc.scalar.copy(two, rows).then_inc(self.first, 1)
        for n, (rows, two, low) in enumerate(self.tables):
            act.wait_ge(self.rest, n + 1)
            self.nc.scalar.copy(low[0:E1, :], rows[0:E1, :]).then_inc(self.low, 1)
            self.nc.scalar.copy(two[E1:P, :], rows[E1:P, :])

    def subtract_first(self, dve):
        for n, (rows, two, low) in enumerate(self.tables):
            dve.wait_ge(self.first, n + 1)
            self.nc.vector.tensor_tensor(rows, rows, two, ALU.subtract).then_inc(self.rest, 1)

    def subtract_second(self, pool):
        for n, (rows, two, low) in enumerate(self.tables):
            pool.wait_ge(self.low, n + 1)
            self.nc.gpsimd.tensor_tensor(low[0:E1, :], rows[0:E1, :], low[0:E1, :], ALU.subtract)


def route(nc, m, c, tag, logits_mm, first=None):
    names = ("logit_mm", "logit_out", "top", "idx", "idx_f", "diff", "exp", "sum", "rec", "second", "hot",
             "weighed", "turned")
    s = {n: m.sem(tag + "_" + n) for n in names}
    set_up, in_loaded, late_loaded, rest_loaded = (
        m.sem(tag + "_" + n) for n in ("set_up", "in_loaded", "late_loaded", "rest_loaded"))
    if first:
        dram, scratch = first
        split = Split(nc, m, c, tag, table_loads(c, dram, "up"))
        step = B * T // NSB
        now = [(c.WUR[:, :, :], dram["L1_ffn_W_up"])]
        now += [(c.HTA[:, n * step:(n + 1) * step], scratch.ht[:, n * step:(n + 1) * step]) for n in range(NSB)]
        later = [(c.SCL[:, 0:1], dram["L1_ffn_scale_up"].partition_broadcast(P)),
                 (c.SCL[:, 1:2], dram["L1_ffn_scale_down"].partition_broadcast(P)),
                 (c.BUP[0:64, :], dram["L1_ffn_bias_up"]), (c.BUP[64:128, :], dram["L1_ffn_bias_up"]),
                 (c.BDN[:, :], dram["L1_ffn_bias_down"])]
    with nc.Block() as block:

        @block.sync
        def _(sp):
            if first:
                for (dst, src), sem in zip(now, [in_loaded, in_loaded, late_loaded]):
                    sp.dma_start(dst, src).then_inc(sem, 16)
                split.load(sp)
                for dst, src in later:
                    sp.dma_start(dst, src).then_inc(rest_loaded, 16)
                sp.wait_ge(rest_loaded, 16 * len(later))

        @block.gpsimd
        def _(pool):
            if first:
                nc.gpsimd.iota(c.IOTA1[:, :], [[1, E1]], base=0, channel_multiplier=0,
                               allow_small_or_imprecise_dtypes=True).then_inc(set_up, 1)
                nc.gpsimd.memset(c.XD[:, :, :, :], 0.0).then_inc(set_up, 1)
                nc.gpsimd.memset(c.T2[:, :, :, :], 0.0).then_inc(set_up, 1)
                pool.wait_ge(set_up, 3)
                split.subtract_second(pool)

        @block.vector
        def _(dve):
            if first:
                nc.vector.memset(c.LOW[E1:P, :, :], 0.0)
                split.subtract_first(dve)
                dve.wait_ge(set_up, 1)
            dve.wait_ge(s["logit_mm"], 1)
            nc.vector.tensor_copy(c.LG1[:, :, :], c.PS[:, 0, 0:GR * E1].rearrange("p (g e) -> p g e", g=GR)
                                  ).then_inc(s["logit_out"], 1)
            dve.wait_ge(s["logit_out"], 1)
            for g in range(GR):
                last = nc.vector.max(c.TOP1[:, g, :], c.LG1[:, g, :])
            last.then_inc(s["top"], 1)
            dve.wait_ge(s["top"], 1)
            nc.vector.tensor_tensor(c.PR[:, :, 1:2], c.TOP1[:, :, 1:2], c.TOP1[:, :, 0:1], ALU.subtract
                                    ).then_inc(s["diff"], 1)
            for g in range(GR):
                last = nc.vector.max_index(c.TIX1[:, g, :], c.TOP1[:, g, :], c.LG1[:, g, :])
            last.then_inc(s["idx"], 1)
            dve.wait_ge(s["idx"], 1)
            nc.vector.tensor_copy(c.TIF1[:, :, :], c.TIX1[:, :, 0:2]).then_inc(s["idx_f"], 1)
            dve.wait_ge(s["idx_f"], 1)
            for k in range(2):
                for twin in range(2):
                    last = nc.vector.tensor_tensor(c.OH[:, k, :, twin, :],
                                                   bcast(c.IOTA1[:, :].unsqueeze(1), [P, GR, E1]),
                                                   bcast(c.TIF1[:, :, k:k + 1], [P, GR, E1]), ALU.is_equal)
            last.then_inc(s["hot"], 1)
            dve.wait_ge(s["exp"], 1)
            nc.vector.tensor_scalar_add(c.PR[:, :, 2:3], c.PR[:, :, 1:2], 1.0).then_inc(s["sum"], 1)
            dve.wait_ge(s["sum"], 1)
            nc.vector.reciprocal(c.PR[:, :, 0:1], c.PR[:, :, 2:3]).then_inc(s["rec"], 1)
            dve.wait_ge(s["rec"], 1)
            nc.vector.tensor_tensor(c.PR[:, :, 1:2], c.PR[:, :, 1:2], c.PR[:, :, 0:1], ALU.mult
                                    ).then_inc(s["second"], 1)
            dve.wait_ge(s["second"], 1)
            dve.wait_ge(s["hot"], 1)
            for k in range(2):
                last = nc.vector.tensor_tensor(c.OHW[:, k, :, :], c.OH[:, k, :, 0, :],
                                               bcast(c.PR[:, :, k:k + 1], [P, GR, E1]), ALU.mult)
            last.then_inc(s["weighed"], 1)
            dve.wait_ge(s["turned"], 1)
            nc.vector.tensor_copy(c.OHT[:, :, :], c.PS[:, 4:6, :])
            nc.vector.tensor_copy(c.OHTW[:, :, :], c.PS[0:E1, 6:8, :])

        @block.scalar
        def _(act):
            if first:
                split.round_off(act)
            act.wait_ge(s["diff"], 1)
            nc.scalar.activation(c.PR[:, :, 1:2], c.PR[:, :, 1:2], ACT.Exp).then_inc(s["exp"], 1)

        @block.tensor
        def _(pe):
            if first:
                pe.wait_ge(in_loaded, 32)
            for sb in range(NSB):
                if first and sb:
                    pe.wait_ge(late_loaded, 16)
                last = logits_mm(sb)
            last.then_inc(s["logit_mm"], 1)
            pe.wait_ge(s["weighed"], 1)
            for k in range(2):
                for g in range(GR):
                    nc.tensor.transpose(c.PS[:, 4 + k, g * P:(g + 1) * P],
                                        c.OH[:, k, g, :, :].rearrange("p t e -> p (t e)"), c.IDENT[:, :])
                    last = nc.tensor.transpose(c.PS[0:E1, 6 + k, g * P:(g + 1) * P], c.OHW[:, k, g, :],
                                               c.IDENT[:, :])
            last.then_inc(s["turned"], 1)


def up_logits(nc, c, sb):
    H = c.HTA[:, :].rearrange("p (n r k) -> p n r k", r=2, k=8)
    for r in range(2):
        o = (sb * 2 + r) * E1
        for k in range(8):
            last = nc.tensor.matmul(c.PS[:, 0, o:o + E1], H[:, sb * SB:(sb + 1) * SB, r, k], c.WUR[:, k, :],
                                    start=(k == 0), stop=(k == 7))
    return last


def down_turned(nc, c, sb):
    return nc.tensor.transpose(c.PS[:, 0, sb * P:(sb + 1) * P], c.LT[:, sb * SB:(sb + 1) * SB], c.IDENT[:, :])


def kronecker(nc, m, c, up):
    tag = "ku" if up else "kd"
    names = ("oh_laid", "w_mm", "w_out", "gath_mm", "gath_dve", "gath_act", "x_dve", "x_pool", "one_mm", "t_out",
             "two_mm", "y_out")
    s = {n: m.sem(tag + "_" + n) for n in names}
    WIDE = 64
    NBANK = WIDE // 4
    G = 2 * NBANK
    HALF_B = NBP // 2 - 1
    HD = c.HD[:, :, :]
    made = lambda q: q + 3
    freed = lambda q: q + 1

    def gather(pe, n):
        table = (n + 1) % 2
        for k in range(4):
            col = (n // 2) * 4 + k
            o = c.PS[:, n % 4, k * P:(k + 1) * P]
            for part, start in ((c.TWO, True), (c.LOW, False)):
                for r in range(2):
                    cols = slice(r * SB, (r + 1) * SB)
                    if up:
                        for e in range(2):
                            q = 32 * (2 * r + e)
                            last = nc.tensor.matmul(o[q:q + 32, :], part[:, table, col * 32:col * 32 + 32],
                                                    c.OHB[:, e, cols], start=start, stop=not start)
                    else:
                        e, w = col // 32, col % 32
                        last = nc.tensor.matmul(o[64 * r:64 * r + 64, :], part[:, table, w * 64:w * 64 + 64],
                                                c.OHB[:, e, cols], start=start, stop=not start)
        return last

    def spread_weights():
        for r in range(2):
            for e in range(2):
                w = c.OHBW[:, e, r * SB:(r + 1) * SB]
                if up:
                    q = 32 * (2 * r + e)
                    last = nc.tensor.matmul(c.PS[q:q + 32, 7, 0:SB], c.ONES[0:E1, 0:32], w, start=True, stop=True)
                else:
                    last = nc.tensor.matmul(c.PS[64 * r:64 * r + 64, 7, e * SB:(e + 1) * SB], c.ONES[0:E1, 0:64],
                                            w, start=True, stop=True)
        return last

    def lay_up(engine, q, par, blocks):
        H = c.HTA[:, :].rearrange("p (n r k) -> p n r k", r=2, k=8)[:, bass.ds(q * BP, BP), :, :]
        for r, e in blocks:
            z = 32 * (2 * r + e)
            dst = c.XD[z:z + 32, par, :, z:z + 32].rearrange("p n (k f) -> p n k f", f=4)
            for f in range(4):
                last = engine.tensor_copy(dst[:, :, :, f], H[32 * f:32 * f + 32, :, r, :])
        return last

    def lay_down(engine, q, par, r):
        z = 64 * r
        return engine.tensor_copy(c.XD[z:z + 64, par, :, z:z + 64], HD[z:z + 64, bass.ds(q * BP, BP), :])

    with nc.Block() as block:

        @block.vector
        def _(dve):
            credit(dve, [s["oh_laid"], s["w_out"], s["gath_dve"], s["gath_dve"], s["x_dve"], s["y_out"], s["y_out"]])

            def lay(q, par):
                dve.wait_ge(s["one_mm"], freed(q))
                last = lay_up(nc.vector, q, par, ((0, 0), (0, 1), (1, 0))) if up else lay_down(nc.vector, q, par, 0)
                last.then_inc(s["x_dve"], 1)

            def product_out(q, par):
                dve.wait_ge(s["two_mm"], made(q))
                if up:
                    nc.vector.scalar_tensor_tensor(
                        HD[:, bass.ds(q * BP, BP), :], c.PS[:, 6 + par, :].rearrange("p (n o) -> p n o", n=BP),
                        c.SCL[:, 0:1], bcast(c.BUP[:, :].unsqueeze(1), [P, BP, 64]), ALU.mult, ALU.add
                    ).then_inc(s["y_out"], 1)
                else:
                    src = c.PS[:, 6 + par, 0:BP * 32].rearrange("p (n k f) -> p n k f", n=BP, f=4)
                    Y = c.YT[:, :].rearrange("p (n r k) -> p n r k", r=2, k=8)[:, bass.ds(q * BP, BP), :, :]
                    for r in range(2):
                        for f in range(4):
                            last = nc.vector.tensor_scalar(
                                Y[32 * f:32 * f + 32, :, r, :], src[32 * r:32 * r + 32, :, :, f],
                                c.SCL[32 * r:32 * r + 32, 1:2], None, ALU.mult)
                    last.then_inc(s["y_out"], 1)

            with dve.Fori(0, NSB) as sb:
                part = lambda t: t[:, :, :].rearrange("e k (b n) -> e k b n", b=NSB)[
                    :, :, bass.ds(sb, 1), :].rearrange("e k o n -> e k (o n)")
                nc.vector.tensor_copy(c.OHBW[:, :, :], part(c.OHTW))
                nc.vector.tensor_copy(c.OHB[:, :, :], part(c.OHT)).then_inc(s["oh_laid"], 1)
                for k in range(2):
                    lay(sb * NBP + k, k)
                dve.wait_ge(s["w_mm"], sb + 1)
                nc.vector.tensor_copy(c.WGT[:, :, :], c.PS[:, 7, 0:2 * SB].rearrange("p (e n) -> p e n", e=2)
                                      if not up else bcast(c.PS[:, 7, 0:SB].unsqueeze(1), [P, 2, SB])
                                      ).then_inc(s["w_out"], 1)
                dve.wait_ge(s["w_out"], done(sb))
                for n in range(0, G, 2):
                    k = (n // 2) * 4
                    e = k // 32
                    dve.wait_ge(s["gath_mm"], sb * G + n + 1)
                    nc.vector.tensor_tensor(c.BG[:, k:k + 4, :], c.PS[:, n % 4, :].rearrange("p (k n) -> p k n", k=4),
                                            bcast(c.WGT[:, e:e + 1, :], [P, 4, SB]), ALU.mult
                                            ).then_inc(s["gath_dve"], 1)
                with dve.Fori(0, HALF_B) as it:
                    for par in range(2):
                        q = sb * NBP + it * 2 + par
                        lay(q + 2, par)
                        product_out(q, par)
                for par in range(2):
                    product_out(sb * NBP + (NBP - 2 + par), par)

        @block.gpsimd
        def _(pool):
            credit(pool, [s["x_pool"]])
            with pool.Fori(0, NSB * NBP // 2) as it:
                for par in range(2):
                    q = it * 2 + par
                    pool.wait_ge(s["one_mm"], freed(q))
                    pool.sem_inc(c.passed, 1)
                    last = lay_up(nc.gpsimd, q, par, ((1, 1),)) if up else lay_down(nc.gpsimd, q, par, 1)
                    last.then_inc(s["x_pool"], 1)

        @block.scalar
        def _(act):
            credit(act, [s["gath_act"], s["gath_act"], s["t_out"], s["t_out"]])
            with act.Fori(0, NSB) as sb:
                for n in range(1, G, 2):
                    k = (n // 2) * 4
                    act.wait_ge(s["gath_mm"], sb * G + n + 1)
                    nc.scalar.copy(c.AG[:, k:k + 4, :], c.PS[:, n % 4, :].rearrange("p (k n) -> p k n", k=4)
                                   ).then_inc(s["gath_act"], 1)
                with act.Fori(0, NBP // 2) as it:
                    for par in range(2):
                        q = sb * NBP + it * 2 + par
                        act.wait_ge(s["one_mm"], made(q))
                        act.wait_ge(s["two_mm"], freed(q))
                        for r in range(2):
                            z = 64 * r
                            src = c.PS[z:z + 64, 4 + par, :]
                            if up:
                                last = nc.scalar.copy(c.T2[z:z + 64, par, :, z:z + 64],
                                                      src.rearrange("p (n k) -> p n k", n=BP))
                            else:
                                dst = c.T2[z:z + 64, par, :, :].rearrange("p n (e r k) -> p n e r k", e=2, r=2)
                                last = nc.scalar.copy(dst[:, :, :, r, :],
                                                      src.rearrange("p (n e k) -> p n e k", n=BP, e=2))
                        last.then_inc(s["t_out"], 1)
                if up:
                    act.wait_ge(s["y_out"], sb * NBP + (NBP + 2))
                    h = HD[:, bass.ds(sb * SB, SB), :]
                    nc.scalar.activation(h, h, ACT.Gelu)

        @block.tensor
        def _(pe):
            credit(pe, [s["one_mm"], s["one_mm"], s["two_mm"], s["two_mm"]])

            def column(t, place, a, b):
                return t[:, a:b, bass.ds(place, 1)].rearrange("p k o -> p (k o)")

            def one(sb, it, par):
                q = sb * NBP + it
                pe.wait_ge(s["x_dve"], done(q))
                pe.wait_ge(s["x_pool"], done(q))
                pe.wait_ge(s["t_out"], freed(q))
                pe.sem_inc(c.passed, 1)
                for j in range(BP):
                    last = nc.tensor.matmul(c.PS[:, 4 + par, j * 64:j * 64 + 64], c.XD[:, par, j, :],
                                            column(c.BG, it * BP + j, 0, 64), start=True, stop=True)
                last.then_inc(s["one_mm"], 1)

            def two(sb, it, par):
                q = sb * NBP + it
                pe.wait_ge(s["t_out"], made(q))
                pe.wait_ge(s["y_out"], freed(q))
                pe.sem_inc(c.passed, 1)
                for j in range(BP):
                    if up:
                        last = nc.tensor.matmul(c.PS[:, 6 + par, j * 64:j * 64 + 64], c.T2[:, par, j, :],
                                                column(c.AG, it * BP + j, 0, 64), start=True, stop=True)
                    else:
                        for e in range(2):
                            last = nc.tensor.matmul(c.PS[0:64, 6 + par, j * 32:j * 32 + 32],
                                                    c.T2[:, par, j, e * 64:e * 64 + 64],
                                                    column(c.AG, it * BP + j, 32 * e, 32 * e + 32),
                                                    start=(e == 0), stop=(e == 1))
                last.then_inc(s["two_mm"], 1)

            with pe.Fori(0, NSB) as sb:
                pe.wait_ge(s["oh_laid"], done(sb))
                pe.sem_inc(c.passed, 1)
                spread_weights().then_inc(s["w_mm"], 1)
                for n in range(G):
                    free = s["gath_act"] if n % 2 else s["gath_dve"]
                    pe.wait_ge(free, sb * NBANK + (n // 2 + 1))
                    pe.sem_inc(c.passed, 1)
                    gather(pe, n).then_inc(s["gath_mm"], 1)
                pe.wait_ge(s["gath_dve"], sb * NBANK + (NBANK + 2))
                pe.wait_ge(s["gath_act"], sb * NBANK + (NBANK + 2))
                pe.sem_inc(c.passed, 1)
                one(sb, 0, 0)
                with pe.Fori(0, HALF_B) as it:
                    for par in range(2):
                        one(sb, it * 2 + (par + 1), 1 - par)
                        two(sb, it * 2 + par, par)
                one(sb, NBP - 1, 1)
                two(sb, NBP - 2, 0)
                two(sb, NBP - 1, 1)


def down_logits(nc, m, c, dram):
    PARTS, STEP = 4, 16
    zeroed, mm = m.sem("dl_zeroed"), m.sem("dl_mm")
    loaded = [m.sem(f"dl_loaded{n}") for n in range(PARTS)]
    split = Split(nc, m, c, "dl", table_loads(c, dram, "down"))
    with nc.Block() as block:

        @block.gpsimd
        def _(pool):
            for n in range(PARTS):
                o = slice(n * STEP, (n + 1) * STEP)
                for r in range(2):
                    nc.gpsimd.memset(c.AG[64 * r:64 * r + 64, o, 64 - 64 * r:128 - 64 * r], 0.0).then_inc(zeroed, 1)
            pool.wait_ge(zeroed, 2 * PARTS)
            split.subtract_second(pool)

        @block.sync
        def _(sp):
            for n in range(PARTS):
                o = slice(n * STEP, (n + 1) * STEP)
                for r in range(2):
                    sp.dma_start(c.AG[64 * r:64 * r + 64, o, 64 * r:64 * r + 64], dram["L1_ffn_W_down"][:, o, :]
                                 ).then_inc(loaded[n], 16)
            split.load(sp)

        @block.vector
        def _(dve):
            nc.vector.memset(c.T2[:, :, :, :], 0.0)
            split.subtract_first(dve)

        @block.tensor
        def _(pe):
            for n in range(PARTS):
                pe.wait_ge(loaded[n], 32)
                pe.wait_ge(zeroed, 2 * n + 2)
                for o in range(n * STEP, (n + 1) * STEP):
                    last = nc.tensor.matmul(c.PS[:, 1, 0:PAIRS], c.AG[:, o, :], c.HD[:, :, o],
                                            start=(o == 0), stop=(o == 63))
            last.then_inc(mm, 1)

        @block.scalar
        def _(act):
            split.round_off(act)
            act.wait_ge(mm, 1)
            nc.scalar.copy(c.LT[:, :], c.PS[:, 1, 0:PAIRS])


def experts_output(nc, m, c, scratch, out):
    x_loaded, biased, turned, gated, x_done, stored_ = (
        m.sem("ko_" + n) for n in ("x_loaded", "biased", "turned", "gated", "x_done", "stored"))
    Y4 = c.YT[:, :].rearrange("p (b n t) -> p b n t", b=B, n=NC)
    chunk = lambda t, i: t[:, :, bass.ds(i, 1), :].rearrange("p b o d -> p b (o d)")
    XC = c.XC.rearrange("p (b n) d -> p b n d", b=B)
    OUT = out.rearrange("b (n p) d -> p b n d", p=P)
    made = lambda i: i + 3
    freed = lambda i: i + 1
    with nc.Block() as block:

        @block.sync
        def _(sp):
            sp.dma_start(c.XC[:, 0:CH // 2, :], scratch.x[:, 0:CH // 2, :]).then_inc(x_loaded, 16)
            with sp.Fori(0, NC) as i:
                sp.wait_ge(x_done, done(i))
                sp.dma_start(chunk(OUT, i), chunk(XC, i)).then_inc(stored_, 16)
            sp.wait_ge(stored_, 16 * NC)

        @block.scalar
        def _(act):
            act.dma_start(c.XC[:, CH // 2:CH, :], scratch.x[:, CH // 2:CH, :]).then_inc(x_loaded, 16)

        @block.vector
        def _(dve):
            credit(dve, [biased, biased, gated, gated, x_done])

            def bias(i, par):
                dve.wait_ge(turned, freed(i))
                for b in range(B):
                    last = nc.vector.tensor_tensor(
                        c.YB[:, par * B + b, :].rearrange("p (m k) -> p m k", k=8),
                        chunk(Y4, i)[:, b, :].rearrange("p (m k) -> p m k", k=8),
                        bcast(c.BDN[:, :].unsqueeze(1), [P, P // 8, 8]), ALU.add)
                last.then_inc(biased, 1)

            def gate(i, par):
                dve.wait_ge(turned, made(i))
                dve.wait_ge(x_done, before(i))
                nc.vector.tensor_tensor(c.Y[:, :, :], c.PS[:, par, :].rearrange("p (b d) -> p b d", b=B),
                                        c.GATE[:, :, :], ALU.mult).then_inc(gated, 1)
                dve.wait_ge(gated, made(i))
                nc.vector.tensor_tensor(chunk(XC, i), chunk(XC, i), c.Y[:, :, :], ALU.add).then_inc(x_done, 1)

            bias(0, 0)
            dve.wait_ge(x_loaded, 32)
            with dve.Fori(0, NC // 2 - 1) as it:
                for par in range(2):
                    bias(it * 2 + (par + 1), 1 - par)
                    gate(it * 2 + par, par)
            bias(NC - 1, 1)
            gate(NC - 2, 0)
            gate(NC - 1, 1)

        @block.tensor
        def _(pe):
            credit(pe, [turned, turned])
            with pe.Fori(0, NC // 2) as it:
                for par in range(2):
                    i = it * 2 + par
                    pe.wait_ge(biased, made(i))
                    pe.wait_ge(gated, freed(i))
                    for b in range(B):
                        last = nc.tensor.transpose(c.PS[:, par, b * P:(b + 1) * P], c.YB[:, par * B + b, :],
                                                   c.IDENT[:, :])
                    last.then_inc(turned, 1)


class Tiles:
    pass


def allocate(m):
    c = Tiles()
    c.PS = m.ps("PS", [P, 8, 512])
    c.IDENT, c.ONES, c.UPTO = m.sb("IDENT", [P, P]), m.sb("ONES", [P, P]), m.sb("UPTO", [P, P])
    c.ZERO, c.LATER = m.sb("ZERO", [P, P], BF16), m.sb("LATER", [P, P], BF16)
    c.IDENTB = m.sb("IDENTB", [P, P], BF16)
    c.HALF, c.IOTA, c.EPS = m.sb("HALF", [P, B]), m.sb("IOTA", [P, 8]), m.sb("EPS", [P, B])
    c.COND, c.MCOL = m.sb("COND", [P, 2, B]), m.sb("MCOL", [P, 2, 6, B])
    c.ST, c.MV = m.sb("ST", [P, B, 6]), m.sb("MV", [P, B, 2])
    c.VE, c.RSTD = m.sb("VE", [P, B]), m.sb("RSTD", [P, B])
    c.Y, c.GATE = m.sb("Y", [P, B, D]), m.sb("GATE", [P, B, D])
    return c


class Scope:

    def __init__(self, nc, sem):
        self.nc, self.sem, self.stack = nc, sem, ExitStack()

    def __enter__(self):
        self.stack.__enter__()
        return self

    def __exit__(self, *e):
        return self.stack.__exit__(*e)

    def sb(self, name, shape, dt=F32):
        return self.stack.enter_context(self.nc.sbuf_tensor(name, shape, dt))


def build(nc, dram, out):
    with ExitStack() as ctx:
        m = Mem(nc, ctx)
        c = allocate(m)
        c.passed = m.sem("passed")
        c.experts_loaded = m.sem("experts_loaded")
        scratch = Tiles()
        scratch.h = nc.dram_tensor("h1", (B, NC, P, D), F32, kind="Internal").ap()
        scratch.qk = nc.dram_tensor("qk_parts", (P, 3 * 2 * B, T), BF16, kind="Internal").ap()
        scratch.vf = nc.dram_tensor("future_v", (B, NC, P, NF * D), F32, kind="Internal").ap()
        scratch.ht = nc.dram_tensor("ht_mid", (P, B * T), F32, kind="Internal").ap()
        scratch.x = nc.dram_tensor("x_mid", (P, CH, D), F32, kind="Internal").ap()
        with Scope(nc, m.sem) as a:
            c.X = a.sb("X", [P, CH, D])
            c.MROW = a.sb("MROW", [P, 2, B, 6, D])
            c.XN, c.HT = a.sb("XN", [P, B, D]), a.sb("HT", [P, B, P])
            c.O, c.OT = a.sb("O", [P, B, D]), a.sb("OT", [P, B, P])
            with Scope(nc, m.sem) as e:
                c.WR, c.WG, c.WU = e.sb("WR", [P, 9]), e.sb("WG", [P, NE0 + 1, F0]), e.sb("WU", [P, NE0 + 1, F0])
                c.WD = e.sb("WD", [P, NE0 + 1, 2, D])
                with Scope(nc, m.sem) as t:
                    c.WQKV, c.WO, c.BQKV, c.BO = (t.sb("WQKV", [P, 256]), t.sb("WO", [P, D]),
                                                  t.sb("BQKV", [P, 256]), t.sb("BO", [P, D]))
                    c.WMOD, c.CB, c.CB2 = t.sb("WMOD", [P, 2, 768]), t.sb("CB", [P, 8, P]), t.sb("CB2", [P, 8, P])
                    c.QKV, c.NEG, c.PHI = (t.sb("QKV", [P, B, 256]), t.sb("NEG", [P, B, 128]),
                                           t.sb("PHI", [P, B, 128]))
                    c.KVP, c.KVSUM, c.PROD = (t.sb(n, [P, B, 512]) for n in ("KVP", "KVSUM", "PROD"))
                    c.KSUM, c.KPROD = t.sb("KSUM", [P, B, 64]), t.sb("KPROD", [P, B, 64])
                    c.DEN, c.REC, c.NUM = t.sb("DEN", [P, 64]), t.sb("REC", [P, 64]), t.sb("NUM", [P, B, D])
                    m.stage(setup, c, dram)
                    m.stage(linear_attention, c, dram)
                with Scope(nc, m.sem) as t:
                    c.LG, c.EX, c.CW = t.sb("LG", [P, B, 9]), t.sb("EX", [P, B, 9]), t.sb("CW", [P, B, 9])
                    c.TOP, c.TIX = t.sb("TOP", [P, B, 8]), t.sb("TIX", [P, B, 8], U32)
                    c.TIF, c.HOT = t.sb("TIF", [P, B, 2]), t.sb("HOT", [P, 2, B, 8])
                    c.SUM, c.RS = t.sb("SUM", [P, B, 2]), t.sb("RS", [P, B, 2])
                    c.SG, c.HH = t.sb("SG", [P, 2, 2, 512]), t.sb("HH", [P, 2, 2, 512])
                    m.stage(experts, c, dram)
            with Scope(nc, m.sem) as u:
                c.VT, c.FUT, c.FMAX = (u.sb("VT", [P, CH, D]), u.sb("FUT", [P, CH, NF * H1]),
                                       u.sb("FMAX", [P, CH, H1]))
                c.SHIFT, c.LNG = u.sb("SHIFT", [P, CH, H1]), u.sb("LNG", [P, 4])
                with Scope(nc, m.sem) as t:
                    c.WT, c.WF, c.CV = t.sb("WT", [P, 4 * D]), t.sb("WF", [P, D]), t.sb("CV", [P, NF, HS])
                    c.BD, c.BLOCKS = t.sb("BD", [P, NF, P]), t.sb("BLOCKS", [P, P])
                    c.GK, c.BIG = t.sb("GK", [P, NF, 2 * D]), t.sb("BIG", [P, NF, 2 * D])
                    c.H, c.QKF = t.sb("H", [P, B, D]), t.sb("QKF", [P, 2 * B, P])
                    c.PARTS = t.sb("PARTS", [P, 6 * B, P], BF16)
                    c.QV, c.VF, c.FP = (t.sb("QV", [P, B, 2 * D]), t.sb("VF", [P, B, NF * D]),
                                        t.sb("FP", [P, B, NF, D]))
                    m.stage(attention_inputs, c, dram, scratch)
                c.ND = u.sb("ND", [P, CH, H1, HS + 1])
                with Scope(nc, m.sem) as t:
                    c.QS, c.KS = t.sb("QS", [P, NG, GH, T], BF16), t.sb("KS", [P, NG, GH, T], BF16)
                    c.PT, c.VG = t.sb("PT", [P, 2, 2, 2, 512]), t.sb("VG", [P, 2, NC, GH, 32])
                    c.MP, c.MX, c.MG = (t.sb("MP", [P, NC, 2, GH]), t.sb("MX", [P, NC, GH]),
                                        t.sb("MG", [P, GH, NC]))
                    c.SH, c.NEGM = t.sb("SH", [NC * GH, 2, P]), t.sb("NEGM", [NC * GH, 2, NS, P], BF16)
                    c.OF = t.sb("OF", [P, 512])
                    m.stage(attention, c, scratch)
                with Scope(nc, m.sem) as t:
                    c.WP, c.W1, c.W2 = t.sb("WP", [P, D]), t.sb("W1", [P, F1]), t.sb("W2", [P, NB1, D])
                    c.H, c.VF, c.FP = (t.sb("H2", [P, B, D]), t.sb("VF2", [P, B, NF * D]),
                                       t.sb("FP2", [P, B, NF, D]))
                    c.PF, c.DEN, c.X1 = (t.sb("PF", [P, B, NF * H1]), t.sb("DEN2", [P, B, H1]),
                                         t.sb("X1", [P, B, D]))
                    c.GE = t.sb("GE", [P, 2, NB1, 256])
                    m.stage(attention_output, c, dram, scratch)
            c.HTA = a.sb("HTA_OUT", [P, B * T])
            m.stage(experts_input, c, scratch)
        with Scope(nc, m.sem) as a:
            c.HTA = a.sb("HTA", [P, B * T])
            c.YT = c.HTA
            c.BG, c.AG = a.sb("BG", [P, 64, SB]), a.sb("AG", [P, 64, SB])
            c.HD, c.XD = a.sb("HD", [P, PAIRS, 64]), a.sb("XD", [P, 2, BP, P])
            c.T2, c.WGT = a.sb("T2", [P, 2, BP, P]), a.sb("WGT", [P, 2, SB])
            c.TWO, c.LOW = a.sb("TWO", [P, 2, 2048], BF16), a.sb("LOW", [P, 2, 2048], BF16)
            c.OH, c.OHW = a.sb("OH", [P, 2, GR, 2, E1]), a.sb("OHW", [P, 2, GR, E1])
            c.OHT, c.OHTW = a.sb("OHT", [P, 2, 512], BF16), a.sb("OHTW", [E1, 2, 512])
            c.OHB, c.OHBW = a.sb("OHB", [P, 2, 2 * SB], BF16), a.sb("OHBW", [E1, 2, 2 * SB])
            c.WUR, c.LG1 = a.sb("WUR", [P, 8, E1]), a.sb("LG1", [P, GR, E1])
            c.TOP1, c.TIX1 = a.sb("TOP1", [P, GR, 8]), a.sb("TIX1", [P, GR, 8], U32)
            c.TIF1, c.PR, c.IOTA1 = a.sb("TIF1", [P, GR, 2]), a.sb("PR", [P, GR, 3]), a.sb("IOTA1", [P, E1])
            c.SCL, c.BUP, c.BDN = a.sb("SCL", [P, 2]), a.sb("BUP", [P, 64]), a.sb("BDN", [P, 8])
            c.LT = a.sb("LT", [P, PAIRS])
            c.XC, c.YB = c.AG[:, 0:CH, :], c.BG[:, 0:2 * B, :]
            m.stage(route, c, "ru", lambda sb: up_logits(nc, c, sb), (dram, scratch))
            m.stage(kronecker, c, True)
            m.stage(down_logits, c, dram)
            m.stage(route, c, "rd", lambda sb: down_turned(nc, c, sb))
            m.stage(kronecker, c, False)
            m.stage(experts_output, c, scratch, out)


_INS = ['L0_attn_x', 'L0_attn_wq', 'L0_attn_bq', 'L0_attn_wk', 'L0_attn_bk', 'L0_attn_wv', 'L0_attn_bv',
        'L0_attn_wo', 'L0_attn_bo', 'L0_wmod', 'L1_wmod',
        'L0_ffn_w_gate', 'L0_ffn_w_up', 'L0_ffn_w_down', 'L0_ffn_sw_gate', 'L0_ffn_sw_up', 'L0_ffn_sw_down',
        'L1_attn_W_qkvf', 'L1_attn_W_ff1', 'L1_attn_W_ff2', 'L1_attn_ln1_g', 'L1_attn_ln1_b',
        'L1_attn_ln2_g', 'L1_attn_ln2_b', 'L1_ffn_A_up', 'L1_ffn_B_up', 'L1_ffn_A_down', 'L1_ffn_B_down',
        'L1_ffn_scale_up', 'L1_ffn_scale_down']


def layout(inputs):
    arrays = {name: np.ascontiguousarray(inputs[name]) for name in _INS}
    for name in ("L0_c", "L1_c", "L0_ffn_router_w", "L0_ffn_gate_w"):
        arrays[name] = np.ascontiguousarray(np.transpose(inputs[name]))
    for name in ("L1_attn_W_qkvf", "L1_attn_W_proj"):
        arrays[name + "_T"] = np.ascontiguousarray(np.transpose(inputs[name]))
    arrays["L1_attn_W_conv"] = np.ascontiguousarray(np.transpose(inputs["L1_attn_W_conv"], (1, 2, 0)))
    move = lambda name, shape, axes: np.ascontiguousarray(
        np.transpose(np.reshape(np.asarray(inputs[name]), shape), axes))
    arrays["L1_ffn_W_up"] = move("L1_ffn_W_up", (64, 8, D), (2, 1, 0))
    arrays["L1_ffn_W_down"] = move("L1_ffn_W_down", (64, 64, 64), (2, 1, 0))
    arrays["L1_ffn_bias_up"] = move("L1_ffn_bias_up", (64, 64), (1, 0))
    arrays["L1_ffn_bias_down"] = move("L1_ffn_bias_down", (8, D), (1, 0))
    return arrays


def kernel(**inputs):
    import concourse.bacc as bacc
    from concourse.bass_utils import run_bass_kernel_spmd

    nc = bacc.Bacc("TRN2", target_bir_lowering=False, num_devices=1)
    arrays = layout(inputs)
    dram = {name: nc.dram_tensor(f"in_{name}", a.shape, mybir.dt.from_np(a.dtype), kind="ExternalInput").ap()
            for name, a in arrays.items()}
    out = nc.dram_tensor("out_x", (B, T, D), F32, kind="ExternalOutput").ap()
    build(nc, dram, out)
    r = run_bass_kernel_spmd(nc, [{f"in_{name}": a for name, a in arrays.items()}], core_ids=[0])
    return r.results[0]["out_x"]
```
